# Optimizing a Trainium2 kernel written in Bass

```python
import numpy as np
import jax
import jax.numpy as jnp

def _softmax(x, axis=-1):
    return jax.nn.softmax(x, axis=axis)

def _gelu(x):
    return jax.nn.gelu(x, approximate=True)

def _silu(x):
    return jax.nn.silu(x)

def _sigmoid(x):
    return jax.nn.sigmoid(x)

def _layernorm(x, axis=-1, eps=1e-05):
    m = jnp.mean(x, axis=axis, keepdims=True)
    v = jnp.var(x, axis=axis, keepdims=True)
    return (x - m) / jnp.sqrt(v + eps)

def _scatter_add(tgt, idx, src, axis=0):
    return tgt.at[idx].add(src)

def _segment_sum(src, seg, n):
    return jax.ops.segment_sum(src, seg, n)
kernel_name = 'mk_gnn_resnorm_d4_gnn_r64_fa7efa'

def setup_inputs(seed: int=0):
    np.random.seed(seed)
    _w = jnp.asarray

    def _rec_inputs():
        import jax
        import jax.numpy as jnp
        _gk = jax.random.key(seed)
        x = -0.000202 + 1 * jax.random.normal(jax.random.fold_in(_gk, 1), (100000, 128), jnp.float32)
        src = jax.random.randint(jax.random.fold_in(_gk, 2), (50000,), 0, 100000, jnp.int32)
        dst = jnp.minimum((100000 * jax.random.uniform(jax.random.fold_in(_gk, 3), (50000,)) ** 2.0).astype(jnp.int32), 99999)
        _o = jnp.argsort(dst, stable=True)
        src = src[_o]
        dst = dst[_o]
        edge_attr_16 = 0.000312547 + 1.00004 * jax.random.normal(jax.random.fold_in(_gk, 12), (50000, 16), jnp.float32)
        return (x, src, dst, edge_attr_16)
    x, src, dst, edge_attr_16 = _rec_inputs()

    def _L0_gnn_setup():
        import jax, jax.numpy as jnp
        import numpy as np
        EPS = 1e-05

        def _sage_bn_relu(x, src, dst, Wl, Wr, b, gamma, beta):
            N = x.shape[0]
            agg = jax.ops.segment_sum(x[src], dst, num_segments=N)
            deg = jax.ops.segment_sum(jnp.ones_like(dst, dtype=x.dtype), dst, num_segments=N)
            mean_nbr = agg / jnp.maximum(deg, 1.0)[:, None]
            h = mean_nbr @ Wl + x @ Wr + b
            mu = jnp.mean(h, axis=0)
            var = jnp.var(h, axis=0)
            h = gamma * (h - mu) * jax.lax.rsqrt(var + EPS) + beta
            return jax.nn.relu(h)
        key = jax.random.key(seed)
        ks = jax.random.split(key, 6)
        N, E, C, H, L = (50000, 12500, 128, 128, 3)
        x = jax.random.normal(ks[0], (N, C), dtype=jnp.float32)
        edge_index = jax.random.randint(ks[1], (2, E), 0, N, dtype=jnp.int64)
        Wl = jax.random.normal(ks[2], (L, C, H), dtype=jnp.float32) / np.sqrt(C)
        Wr = jax.random.normal(ks[3], (L, C, H), dtype=jnp.float32) / np.sqrt(C)
        b = jnp.zeros((L, H), dtype=jnp.float32)
        gamma = jnp.ones((L, H), dtype=jnp.float32)
        beta = jnp.zeros((L, H), dtype=jnp.float32)
        return {'x': x, 'edge_index': edge_index, 'Wl': Wl, 'Wr': Wr, 'b': b, 'gamma': gamma, 'beta': beta}
    _L0_gnn_all = _L0_gnn_setup()
    _L0_gnn_in = {k: v for k, v in _L0_gnn_all.items() if k in ('Wl', 'Wr', 'b', 'gamma', 'beta')}
    del _L0_gnn_all

    def _L1_gnn_setup():
        import jax, jax.numpy as jnp
        import numpy as np
        N_NODES = 50000
        N_EDGES = 9375
        DIM = 128
        key = jax.random.key(seed)
        ks = jax.random.split(key, 8)
        node_feats = jax.random.normal(ks[0], (N_NODES, DIM), dtype=jnp.float32)
        edge_src = jax.random.randint(ks[1], (N_EDGES,), 0, N_NODES, dtype=jnp.int64)
        edge_dst = jax.random.randint(ks[2], (N_EDGES,), 0, N_NODES, dtype=jnp.int64)
        sc = 1.0 / np.sqrt(DIM)
        W_self = jax.random.normal(ks[3], (DIM, DIM), dtype=jnp.float32) * sc
        b_self = jax.random.normal(ks[4], (DIM,), dtype=jnp.float32) * sc
        W_neigh = jax.random.normal(ks[5], (DIM, DIM), dtype=jnp.float32) * sc
        b_neigh = jax.random.normal(ks[6], (DIM,), dtype=jnp.float32) * sc
        return {'node_feats': node_feats, 'edge_src': edge_src, 'edge_dst': edge_dst, 'W_self': W_self, 'b_self': b_self, 'W_neigh': W_neigh, 'b_neigh': b_neigh}
    _L1_gnn_all = _L1_gnn_setup()
    _L1_gnn_in = {k: v for k, v in _L1_gnn_all.items() if k in ('W_self', 'b_self', 'W_neigh', 'b_neigh')}
    del _L1_gnn_all

    def _L2_gnn_setup():
        import jax, jax.numpy as jnp
        import numpy as np
        N_NODES = 50000
        N_EDGES = 6250
        DIM = 128
        key = jax.random.key(seed)
        ks = jax.random.split(key, 12)
        s = 1.0 / np.sqrt(DIM)
        h = jax.random.normal(ks[0], (N_NODES, DIM), dtype=jnp.float32)
        src = jax.random.randint(ks[1], (N_EDGES,), 0, N_NODES, dtype=jnp.int32)
        dst = jax.random.randint(ks[2], (N_EDGES,), 0, N_NODES, dtype=jnp.int32)
        W_w = jax.random.normal(ks[3], (DIM, DIM), dtype=jnp.float32) * s
        W_b = jax.random.normal(ks[4], (DIM,), dtype=jnp.float32) * s
        WS_w = jax.random.normal(ks[5], (DIM, DIM), dtype=jnp.float32) * s
        WS_b = jax.random.normal(ks[6], (DIM,), dtype=jnp.float32) * s
        q_w = jax.random.normal(ks[7], (DIM, DIM), dtype=jnp.float32) * s
        q_b = jax.random.normal(ks[8], (DIM,), dtype=jnp.float32) * s
        k_w = jax.random.normal(ks[9], (DIM, DIM), dtype=jnp.float32) * s
        k_b = jax.random.normal(ks[10], (DIM,), dtype=jnp.float32) * s
        return {'h': h, 'src': src, 'dst': dst, 'W_w': W_w, 'W_b': W_b, 'WS_w': WS_w, 'WS_b': WS_b, 'q_w': q_w, 'q_b': q_b, 'k_w': k_w, 'k_b': k_b}
    _L2_gnn_all = _L2_gnn_setup()
    _L2_gnn_in = {k: v for k, v in _L2_gnn_all.items() if k in ('W_w', 'W_b', 'WS_w', 'WS_b', 'q_w', 'q_b', 'k_w', 'k_b')}
    del _L2_gnn_all

    def _L3_gnn_setup():
        import jax, jax.numpy as jnp
        import numpy as np
        import math
        N = 100000
        E = 15625
        D = 128
        ED = 16
        L = 5
        MID = 3
        ALPHA = 0.2
        THETA = 0.2
        NEG_SLOPE_ATT = 0.2

        def _gat_layer(x, src, dst, ea, W, We, a_src, a_dst, a_edge, b, n):
            h = x @ W
            e = ea @ We
            s = (h @ a_src)[src] + (h @ a_dst)[dst] + e @ a_edge
            s = jax.nn.leaky_relu(s, NEG_SLOPE_ATT)
            smax = jax.ops.segment_max(s, dst, num_segments=n)
            ex = jnp.exp(s - jax.lax.stop_gradient(smax)[dst])
            denom = jax.ops.segment_sum(ex, dst, num_segments=n)
            alpha = ex / denom[dst]
            out = jax.ops.segment_sum(h[src] * alpha[:, None], dst, num_segments=n)
            return out + b

        def _forward(x, edge_index, edge_attr, Ws, Wes, a_srcs, a_dsts, a_edges, biases, mid_ws):
            n = x.shape[0]
            src0, dst0 = (edge_index[0], edge_index[1])
            deg = jax.ops.segment_sum(jnp.ones_like(dst0, dtype=x.dtype), dst0, num_segments=n)
            loop_attr = jax.ops.segment_sum(edge_attr, dst0, num_segments=n) / jnp.clip(deg, 1.0)[:, None]
            loops = jnp.arange(n, dtype=src0.dtype)
            src = jnp.concatenate([src0, loops])
            dst = jnp.concatenate([dst0, loops])
            ea = jnp.concatenate([edge_attr, loop_attr], axis=0)
            x0 = _gat_layer(x, src, dst, ea, Ws[0], Wes[0], a_srcs[0], a_dsts[0], a_edges[0], biases[0], n)
            h = x0
            for i in range(MID):
                c = _gat_layer(h, src, dst, ea, Ws[i + 1], Wes[i + 1], a_srcs[i + 1], a_dsts[i + 1], a_edges[i + 1], biases[i + 1], n)
                beta = math.log(THETA / (i + 1) + 1.0)
                h = (1.0 - ALPHA) * c + ALPHA * x0
                h = (1.0 - beta) * h + beta * (h @ mid_ws[i])
                h = jax.nn.leaky_relu(h, 0.01)
            return _gat_layer(h, src, dst, ea, Ws[L - 1], Wes[L - 1], a_srcs[L - 1], a_dsts[L - 1], a_edges[L - 1], biases[L - 1], n)
        key = jax.random.key(seed)
        ks = jax.random.split(key, 10)
        s = 1.0 / np.sqrt(D)
        se = 1.0 / np.sqrt(ED)
        return {'x': jax.random.normal(ks[0], (N, D), jnp.float32), 'edge_index': jax.random.randint(ks[1], (2, E), 0, N, dtype=jnp.int64), 'edge_attr': jax.random.normal(ks[2], (E, ED), jnp.float32), 'Ws': jax.random.normal(ks[3], (L, D, D), jnp.float32) * s, 'Wes': jax.random.normal(ks[4], (L, ED, D), jnp.float32) * se, 'a_srcs': jax.random.normal(ks[5], (L, D), jnp.float32) * s, 'a_dsts': jax.random.normal(ks[6], (L, D), jnp.float32) * s, 'a_edges': jax.random.normal(ks[7], (L, D), jnp.float32) * s, 'biases': jnp.zeros((L, D), jnp.float32), 'mid_ws': jax.random.normal(ks[8], (MID, D, D), jnp.float32) * s}
    _L3_gnn_all = _L3_gnn_setup()
    _L3_gnn_in = {k: v for k, v in _L3_gnn_all.items() if k in ('Ws', 'Wes', 'a_srcs', 'a_dsts', 'a_edges', 'biases', 'mid_ws')}
    del _L3_gnn_all
    return {'x': x, 'src': src, 'dst': dst, 'edge_attr_16': edge_attr_16, 'L0_gnn_Wl': _L0_gnn_in['Wl'], 'L0_gnn_Wr': _L0_gnn_in['Wr'], 'L0_gnn_b': _L0_gnn_in['b'], 'L0_gnn_gamma': _L0_gnn_in['gamma'], 'L0_gnn_beta': _L0_gnn_in['beta'], 'L1_gnn_W_self': _L1_gnn_in['W_self'], 'L1_gnn_b_self': _L1_gnn_in['b_self'], 'L1_gnn_W_neigh': _L1_gnn_in['W_neigh'], 'L1_gnn_b_neigh': _L1_gnn_in['b_neigh'], 'L2_gnn_W_w': _L2_gnn_in['W_w'], 'L2_gnn_W_b': _L2_gnn_in['W_b'], 'L2_gnn_WS_w': _L2_gnn_in['WS_w'], 'L2_gnn_WS_b': _L2_gnn_in['WS_b'], 'L2_gnn_q_w': _L2_gnn_in['q_w'], 'L2_gnn_q_b': _L2_gnn_in['q_b'], 'L2_gnn_k_w': _L2_gnn_in['k_w'], 'L2_gnn_k_b': _L2_gnn_in['k_b'], 'L3_gnn_Ws': _L3_gnn_in['Ws'], 'L3_gnn_Wes': _L3_gnn_in['Wes'], 'L3_gnn_a_srcs': _L3_gnn_in['a_srcs'], 'L3_gnn_a_dsts': _L3_gnn_in['a_dsts'], 'L3_gnn_a_edges': _L3_gnn_in['a_edges'], 'L3_gnn_biases': _L3_gnn_in['biases'], 'L3_gnn_mid_ws': _L3_gnn_in['mid_ws']}

def reference(x, src, dst, edge_attr_16, L0_gnn_Wl, L0_gnn_Wr, L0_gnn_b, L0_gnn_gamma, L0_gnn_beta, L1_gnn_W_self, L1_gnn_b_self, L1_gnn_W_neigh, L1_gnn_b_neigh, L2_gnn_W_w, L2_gnn_W_b, L2_gnn_WS_w, L2_gnn_WS_b, L2_gnn_q_w, L2_gnn_q_b, L2_gnn_k_w, L2_gnn_k_b, L3_gnn_Ws, L3_gnn_Wes, L3_gnn_a_srcs, L3_gnn_a_dsts, L3_gnn_a_edges, L3_gnn_biases, L3_gnn_mid_ws):
    import jax
    import jax.numpy as jnp

    def _L0_gnn_ref(x, edge_index, Wl, Wr, b, gamma, beta):
        import jax, jax.numpy as jnp
        import numpy as np
        EPS = 1e-05

        def _sage_bn_relu(x, src, dst, Wl, Wr, b, gamma, beta):
            N = x.shape[0]
            agg = jax.ops.segment_sum(x[src], dst, num_segments=N)
            deg = jax.ops.segment_sum(jnp.ones_like(dst, dtype=x.dtype), dst, num_segments=N)
            mean_nbr = agg / jnp.maximum(deg, 1.0)[:, None]
            h = mean_nbr @ Wl + x @ Wr + b
            mu = jnp.mean(h, axis=0)
            var = jnp.var(h, axis=0)
            h = gamma * (h - mu) * jax.lax.rsqrt(var + EPS) + beta
            return jax.nn.relu(h)
        src, dst = (edge_index[0], edge_index[1])
        h = x
        for l in range(Wl.shape[0]):
            h = _sage_bn_relu(h, src, dst, Wl[l], Wr[l], b[l], gamma[l], beta[l])
        return h

    def _L1_gnn_ref(node_feats, edge_src, edge_dst, W_self, b_self, W_neigh, b_neigh):
        import jax, jax.numpy as jnp
        import numpy as np
        N_NODES = 50000
        N_EDGES = 9375
        DIM = 128
        N = node_feats.shape[0]
        gathered = node_feats[edge_src]
        neigh_sum = jax.ops.segment_sum(gathered, edge_dst, num_segments=N)
        deg = jax.ops.segment_sum(jnp.ones_like(edge_dst, dtype=node_feats.dtype), edge_dst, num_segments=N)
        neigh_mean = neigh_sum / jnp.maximum(deg, 1.0)[:, None]
        out = node_feats @ W_self.T + b_self + (neigh_mean @ W_neigh.T + b_neigh)
        return jax.nn.relu(out)

    def _L2_gnn_ref(h, src, dst, W_w, W_b, WS_w, WS_b, q_w, q_b, k_w, k_b):
        import jax, jax.numpy as jnp
        import numpy as np
        N_NODES = 50000
        N_EDGES = 6250
        DIM = 128
        n = h.shape[0]
        scale = 1.0 / jnp.sqrt(jnp.asarray(h.shape[1], h.dtype))
        msg_n = h @ W_w.T + W_b
        q_n = h @ q_w.T + q_b
        k_n = h @ k_w.T + k_b
        scores = jnp.sum(q_n[src] * k_n[dst], axis=-1) * scale
        smax = jax.ops.segment_max(scores, dst, num_segments=n)
        e = jnp.exp(scores - smax[dst])
        denom = jax.ops.segment_sum(e, dst, num_segments=n)
        alpha = e / denom[dst]
        h_agg = jax.ops.segment_sum(alpha[:, None] * msg_n[src], dst, num_segments=n)
        return h @ WS_w.T + WS_b + h_agg

    def _L3_gnn_ref(x, edge_index, edge_attr, Ws, Wes, a_srcs, a_dsts, a_edges, biases, mid_ws):
        import jax, jax.numpy as jnp
        import numpy as np
        import math
        N = 100000
        E = 15625
        D = 128
        ED = 16
        L = 5
        MID = 3
        ALPHA = 0.2
        THETA = 0.2
        NEG_SLOPE_ATT = 0.2

        def _gat_layer(x, src, dst, ea, W, We, a_src, a_dst, a_edge, b, n):
            h = x @ W
            e = ea @ We
            s = (h @ a_src)[src] + (h @ a_dst)[dst] + e @ a_edge
            s = jax.nn.leaky_relu(s, NEG_SLOPE_ATT)
            smax = jax.ops.segment_max(s, dst, num_segments=n)
            ex = jnp.exp(s - jax.lax.stop_gradient(smax)[dst])
            denom = jax.ops.segment_sum(ex, dst, num_segments=n)
            alpha = ex / denom[dst]
            out = jax.ops.segment_sum(h[src] * alpha[:, None], dst, num_segments=n)
            return out + b

        def _forward(x, edge_index, edge_attr, Ws, Wes, a_srcs, a_dsts, a_edges, biases, mid_ws):
            n = x.shape[0]
            src0, dst0 = (edge_index[0], edge_index[1])
            deg = jax.ops.segment_sum(jnp.ones_like(dst0, dtype=x.dtype), dst0, num_segments=n)
            loop_attr = jax.ops.segment_sum(edge_attr, dst0, num_segments=n) / jnp.clip(deg, 1.0)[:, None]
            loops = jnp.arange(n, dtype=src0.dtype)
            src = jnp.concatenate([src0, loops])
            dst = jnp.concatenate([dst0, loops])
            ea = jnp.concatenate([edge_attr, loop_attr], axis=0)
            x0 = _gat_layer(x, src, dst, ea, Ws[0], Wes[0], a_srcs[0], a_dsts[0], a_edges[0], biases[0], n)
            h = x0
            for i in range(MID):
                c = _gat_layer(h, src, dst, ea, Ws[i + 1], Wes[i + 1], a_srcs[i + 1], a_dsts[i + 1], a_edges[i + 1], biases[i + 1], n)
                beta = math.log(THETA / (i + 1) + 1.0)
                h = (1.0 - ALPHA) * c + ALPHA * x0
                h = (1.0 - beta) * h + beta * (h @ mid_ws[i])
                h = jax.nn.leaky_relu(h, 0.01)
            return _gat_layer(h, src, dst, ea, Ws[L - 1], Wes[L - 1], a_srcs[L - 1], a_dsts[L - 1], a_edges[L - 1], biases[L - 1], n)
        return _forward(x, edge_index, edge_attr, Ws, Wes, a_srcs, a_dsts, a_edges, biases, mid_ws)
    edge_index = jnp.stack([src, dst])
    x = _layernorm(x + _L0_gnn_ref(x, edge_index, L0_gnn_Wl, L0_gnn_Wr, L0_gnn_b, L0_gnn_gamma, L0_gnn_beta), axis=-1)
    x = _layernorm(x + _L1_gnn_ref(x, src, dst, L1_gnn_W_self, L1_gnn_b_self, L1_gnn_W_neigh, L1_gnn_b_neigh), axis=-1)
    x = _layernorm(x + _L2_gnn_ref(x, src, dst, L2_gnn_W_w, L2_gnn_W_b, L2_gnn_WS_w, L2_gnn_WS_b, L2_gnn_q_w, L2_gnn_q_b, L2_gnn_k_w, L2_gnn_k_b), axis=-1)
    x = _layernorm(x + _L3_gnn_ref(x, edge_index, edge_attr_16, L3_gnn_Ws, L3_gnn_Wes, L3_gnn_a_srcs, L3_gnn_a_dsts, L3_gnn_a_edges, L3_gnn_biases, L3_gnn_mid_ws), axis=-1)
    return x

_drawn_inputs = setup_inputs


def setup_inputs(seed=0):
    import zlib

    import numpy as np

    out = dict(_drawn_inputs(seed))
    spreads = {'L0_gnn_b': (0.0, 0.8),
     'L0_gnn_gamma': (1.0, 0.2),
     'L0_gnn_beta': (0.0, 0.1),
     'L3_gnn_biases': (0.0, 0.1)}
    factors = {'edge_attr_16': 4.206,
     'L2_gnn_q_b': 8.0,
     'L2_gnn_k_b': 6.856,
     'L3_gnn_Wes': 4.593,
     'L3_gnn_a_srcs': 4.589,
     'L3_gnn_a_dsts': 8.0,
     'L3_gnn_a_edges': 4.799}
    for name, (base, spread) in spreads.items():
        noise = np.random.default_rng([zlib.crc32(name.encode()), seed]).standard_normal(out[name].shape)
        drawn = base * np.exp(spread * noise) if base else spread * noise
        out[name] = jnp.asarray(drawn.astype(out[name].dtype))
    for name, factor in factors.items():
        out[name] = (out[name] * factor).astype(out[name].dtype)
    return out
```

```python
import math
from contextlib import ExitStack

import concourse.bass as bass
from concourse import mybir

F32 = mybir.dt.float32
I32 = mybir.dt.int32
ALU = mybir.AluOpType
ACT = mybir.ActivationFunctionType
AX = mybir.AxisListType.X

P = 128
D = 128
W = D + 2
ED = 16
CH = 8
G = 16
GT = 4
NG = G // GT
SUP = P * G
BIG = 1.0e30
EPS = 1e-5
LAYERS = 5
ALPHA, THETA = 0.2, 0.2
ATT_SLOPE, SLOPE = 0.2, 0.01


class Sem:

    def __init__(self, handle):
        self.h = handle
        self.base = 0

    def at(self, n):
        return self.base + n


class Chain:

    def __init__(self, eng, sem):
        self.eng, self.sem = eng, sem
        self.start, self.i, self.per, self.n, self.total = 0, None, 0, 0, 0

    def enter(self, i, per, turns):
        self.start, self.i, self.per, self.n = self.total, i, per, 0
        self.turns = turns

    def leave(self):
        if self.n != self.per:
            raise AssertionError(f"chain of {self.sem.h}: {self.n} steps in a turn, not {self.per}")
        self.total = self.start + self.turns * self.per
        self.i = None

    def __call__(self, ins):
        ins.then_inc(self.sem.h, 1)
        self.n += 1
        if self.i is None:
            self.total += 1
            self.eng.wait_ge(self.sem.h, self.sem.at(self.total))
        else:
            self.eng.wait_ge(self.sem.h, self.sem.at(self.start + self.i * self.per + self.n))


def gnn(nc, t, out):
    N = t["x"].shape[0]
    E = t["src"].shape[0]
    COLS = (E + P * CH - 1) // (P * CH) * CH
    NCH = COLS // CH
    assert NCH % 2 == 1 and NCH >= 3
    ROWS, REST = E // COLS, E % COLS
    LIVE = ROWS + (REST > 0)
    ST = N // SUP
    assert ST % 2 == 0 and ST >= 2
    LASTP = (N - ST * SUP) // G
    assert ST * SUP + LASTP * G == N and 0 < LASTP < P
    PAIRS = ST // 2

    ctx = ExitStack()
    with ctx, nc.allow_non_contiguous_dma(reason="single columns of weights and of edge lists"):
        def sb(name, shape, dt=F32):
            return ctx.enter_context(nc.sbuf_tensor(name, shape, dt))

        def sem(name):
            return Sem(ctx.enter_context(nc.semaphore(name)))

        def table(name, w=W):
            return nc.dram_tensor(name, (N, w), F32, kind="Internal").ap()
        tab_a, tab_b, tab_x0, tab_u = table("tab_a"), table("tab_b"), table("tab_x0"), table("tab_u")
        pair_tab, agg = table("pair_tab", 2), table("agg_tab")

        src_i = sb("src_i", [P, COLS + 2 * CH], I32)
        dst_i = sb("dst_i", [P, COLS + 2 * CH], I32)
        scat_i = sb("scat_i", [P, COLS], I32)
        fix_i = sb("fix_i", [P, 1], I32)
        dstf = sb("dstf", [P, COLS])
        same = sb("same", [P, COLS])
        pen = sb("pen", [P, COLS])
        fixm = sb("fixm", [P, COLS])
        inv_cnt = sb("inv_cnt", [P, COLS])
        inv_cnt_fix = sb("inv_cnt_fix", [P, 1])
        edge_c = sb("edge_c", [P, LAYERS, COLS])
        loop_c = sb("loop_c", [P, LAYERS, COLS])
        loop_fix = sb("loop_fix", [P, LAYERS])
        chain_m = sb("chain_m", [P, P])
        chain_pen = sb("chain_pen", [P, P])
        ident = sb("ident", [P, P])
        ones = sb("ones", [P, P])
        zrow = sb("zrow", [P, COLS])

        sage_l = sb("sage_l", [P, 3, D])
        sage_r = sb("sage_r", [P, 3, D])
        mean_w = sb("mean_w", [P, 2, D])
        mean_b = sb("mean_b", [P, GT, D])
        att_w = sb("att_w", [P, 2, D])
        att_b = sb("att_b", [P, GT, D])
        att_mb = sb("att_mb", [P, D])
        key_w = sb("key_w", [P, D + 1])
        key_b = sb("key_b", [P, D + 1])
        gat_w = sb("gat_w", [P, LAYERS, D])
        gat_b = sb("gat_b", [P, LAYERS, GT, D])
        gat_s = sb("gat_s", [P, LAYERS, 2])
        mid_w = sb("mid_w", [P, 3, D])
        bn_col = sb("bn_col", [P, 2])
        bn_row = sb("bn_row", [P, 2, D])
        bn_par = sb("bn_par", [P, 3, 3])

        gi = sb("gi", [P, 2, CH], I32)
        di = sb("di", [P, 2, CH], I32)
        wi = sb("wi", [P, 2, CH], I32)
        dpair = sb("dpair", [P, 2, CH, 2])
        wide = sb("wide", [P, CH, D])
        wide2 = sb("wide2", [P, CH, D])
        obuf = sb("obuf", [P, 2, CH, W])
        fixv = sb("fixv", [P, D])
        fixt = sb("fixt", [P, D])
        m_all = sb("m_all", [P, COLS + 1])
        den_all = sb("den_all", [P, COLS + 1])
        sl_all = sb("sl_all", [P, COLS])
        s8 = sb("s8", [P, CH])
        z8 = sb("z8", [P, CH])
        l8 = sb("l8", [P, CH])
        e4 = sb("e4", [P, 4 * CH])
        x4 = sb("x4", [P, 4 * CH])
        sc8 = sb("sc8", [P, 2, CH])
        fx = sb("fx", [P, 16])
        lrow = sb("lrow", [P, D + 1])
        wq = sb("wq", [P, P])
        wqt = sb("wqt", [P, P])
        fixo = sb("fixo", [P, W])

        node_in = sb("node_in", [P, 3, 2, G, W])
        in_h, in_r, in_e = (node_in[:, k] for k in range(3))
        node_out = sb("node_out", [P, 2, 2, G, W])
        outb, outu = node_out[:, 0], node_out[:, 1]
        outp = sb("outp", [P, 2, G, 2])
        yb = sb("yb", [P, 2, GT, D])
        ht = sb("ht", [P, 2, GT, D])
        rt = sb("rt", [P, 2, GT, D])
        ub = sb("ub", [P, 2, GT, D])
        ot = sb("ot", [P, 2, GT, D])
        st6 = sb("st6", [P, GT, 6])
        mv = sb("mv", [P, 2, GT, 2])
        std = sb("std", [P, 2, GT])
        col1 = sb("col1", [P, 2, G])
        acc = sb("acc", [P, 2, GT, D])
        sums = sb("sums", [P, 8])

        room = node_in[:, :, :, :, :].rearrange("p k a g w -> p (k a g w)")
        ea = room[:, 0:COLS * ED]
        at, lots = 0, []
        for w in (D, D, W, W):
            lots.append(room[:, at:at + 2 * CH * w].rearrange("p (a j w) -> p a j w", a=2, j=CH))
            at += 2 * CH * w
        state, rows_x, rows, drows = lots
        eat = node_out[:, :, :, :, :].rearrange("p k a g w -> p (k a g w)")
        assert COLS * ED <= 2 * 2 * G * W

        ps = [ctx.enter_context(nc.psum_tensor(f"ps{i}", [P, 512], F32)) for i in range(8)]

        dve_s, act_s, pool_s, pe_s = sem("dve_s"), sem("act_s"), sem("pool_s"), sem("pe_s")
        tick = sem("tick")
        d2p, p2d, d2a, a2d, p2a, a2p = (sem(n) for n in ("d2p", "p2d", "d2a", "a2d", "p2a", "a2p"))
        load = sem("load")
        gath = [sem("gath0"), sem("gath1")]
        gath_d = [sem("gath_d0"), sem("gath_d1")]
        scat = [sem("scat0"), sem("scat1")]
        scat_fix = sem("scat_fix")
        idx_ready, rows_used, ob_ready, exp_in, exp_out = (
            sem(n) for n in ("idx_ready", "rows_used", "ob_ready", "exp_in", "exp_out"))
        fix_ready = sem("fix_ready")
        ld = [sem("ld0"), sem("ld1")]
        stq = [sem("stq0"), sem("stq1")]
        y_ready, th_done, tr_done, ht_ready, rt_ready, mm_done, post_read, out_ready = (
            sem(n) for n in ("y_ready", "th_done", "tr_done", "ht_ready", "rt_ready", "mm_done", "post_read",
                             "out_ready"))
        t2_done, ot_ready, m2_done, m2_read, sq_ready, norm_ready = (
            sem(n) for n in ("t2_done", "ot_ready", "m2_done", "m2_read", "sq_ready", "norm_ready"))
        var_ready, std_ready = sem("var_ready"), sem("std_ready")

        def bc(ap, n):
            return ap.unsqueeze(1).to_broadcast([P, n, ap.shape[-1]])

        def bl(ap, n=D):
            return ap.unsqueeze(2).to_broadcast([P, ap.shape[-1], n])

        NLOAD = [0]
        with nc.Block() as block:
            def edge_load(sp, dst_ap, dram, s, w=1):
                n = 0
                src_v = dram[0:ROWS * COLS] if w == 1 else dram[0:ROWS * COLS, :]
                pat = "(p j) -> p j" if w == 1 else "(p j) k -> p (j k)"
                sp.dma_start(dst_ap[0:ROWS, 0:COLS * w], src_v.rearrange(pat, p=ROWS)).then_inc(s.h, 16)
                n += 16
                if REST:
                    src_v = dram[ROWS * COLS:E] if w == 1 else dram[ROWS * COLS:E, :]
                    sp.dma_start(dst_ap[ROWS:ROWS + 1, 0:REST * w], src_v.rearrange(pat, p=1)).then_inc(s.h, 16)
                    n += 16
                return n

            dpad = wide[:, :, :].rearrange("p a b -> p (a b)").bitcast(I32)
            bnd = fx[:, 0:2].bitcast(I32)

            @block.sync
            def _(sp):
                sp.wait_ge(d2a.h, d2a.at(1))
                sp.wait_ge(pool_s.h, pool_s.at(1))
                n = edge_load(sp, src_i, t["src"], load)
                n += edge_load(sp, dst_i, t["dst"], load)
                n += edge_load(sp, dpad, t["dst"], load)
                n += edge_load(sp, ea, t["edge_attr_16"], load, ED)
                dd = t["dst"].rearrange("(e o) -> e o", o=1)
                sp.dma_start(bnd[1:LIVE, 0:1], dd[COLS - 1:COLS - 1 + (LIVE - 2) * COLS + 1:COLS, :]).then_inc(load.h, 16)
                sp.dma_start(bnd[0:LIVE - 1, 1:2], dd[COLS:COLS + (LIVE - 2) * COLS + 1:COLS, :]).then_inc(load.h, 16)
                n += 32
                for l in range(LAYERS):
                    sp.dma_start(eat[0:ED, l * D:(l + 1) * D], t["L3_gnn_Wes"][l]).then_inc(load.h, 16)
                    for k in range(ED):
                        sp.dma_start(eat[k:k + 1, (LAYERS + l) * D:(LAYERS + l + 1) * D],
                                     t["L3_gnn_a_edges"][l:l + 1, :]).then_inc(load.h, 16)
                    n += 16 + 16 * ED
                NLOAD[0] = n
                sp.wait_ge(load.h, load.at(n))
                sp.sem_inc(a2d.h, 1)

            @block.gpsimd
            def _(pool):
                pool.memset(ea[:, :], 0.0)
                pool.memset(ident[:, :], 0.0).then_inc(pool_s.h, 1)
                pool.wait_ge(pool_s.h, pool_s.at(1))
                pool.affine_select(out=ident[:, :], in_=ident[:, :], compare_op=ALU.not_equal, fill=1.0, base=0,
                                   pattern=[[-1, P]], channel_multiplier=1).then_inc(pool_s.h, 1)
                pool.wait_ge(d2p.h, d2p.at(2))
                pool.affine_select(out=chain_m[:, :], in_=chain_m[:, :], compare_op=ALU.is_gt, fill=0.0, base=0,
                                   pattern=[[1, P]], channel_multiplier=-1).then_inc(pool_s.h, 1)
                pool.affine_select(out=chain_pen[:, :], in_=chain_pen[:, :], compare_op=ALU.is_gt, fill=0.0, base=0,
                                   pattern=[[-1, P]], channel_multiplier=1).then_inc(pool_s.h, 1)

            @block.vector
            def _(dve):
                go = Chain(dve, dve_s)
                dve.memset(src_i[:, :], 0)
                dve.memset(dst_i[:, :], 0)
                dve.memset(dpad, N)
                dve.memset(bnd[:, 0:1], -1)
                dve.memset(bnd[:, 1:2], N + 1)
                dve.memset(ones[:, :], 1.0)
                dve.memset(zrow[:, :], 1.0)
                dve.memset(same[:, 0:1], 0.0)
                dve.memset(eat[:, :], 0.0)
                go(dve.memset(obuf[:, :, :, :], 0.0))
                dve.sem_inc(d2a.h, 1)
                dve.wait_ge(a2d.h, a2d.at(1))
                dve.tensor_copy(fx[:, 2:4], bnd[:, 0:2])
                go(dve.tensor_copy(dstf[:, :], dpad[:, 0:COLS]))
                dve.tensor_tensor(same[:, 1:COLS], dstf[:, 1:COLS], dstf[:, 0:COLS - 1], ALU.is_equal)
                dve.tensor_tensor(pen[:, 0:COLS - 1], dstf[:, 0:COLS - 1], dstf[:, 1:COLS], ALU.not_equal)
                dve.tensor_tensor(pen[:, COLS - 1:COLS], dstf[:, COLS - 1:COLS], fx[:, 3:4], ALU.not_equal)
                dve.tensor_tensor(fx[:, 4:5], dstf[:, 0:1], fx[:, 2:3], ALU.is_equal)
                go(dve.tensor_scalar(fixm[:, :], dstf[:, :], dstf[:, 0:1], None, ALU.is_equal))
                go(dve.scalar_tensor_tensor(fixm[:, :], fixm[:, :], fx[:, 4:5], pen[:, :], ALU.mult, ALU.mult))
                go(dve.tensor_tensor(m_all[:, 0:COLS], pen[:, :], fixm[:, :], ALU.subtract))
                go(dve.scalar_tensor_tensor(den_all[:, 0:COLS], dstf[:, :], float(-N), m_all[:, 0:COLS], ALU.add, ALU.mult))
                dve.tensor_scalar(scat_i[:, :], den_all[:, 0:COLS], float(N), None, ALU.add)
                dve.tensor_reduce(fx[:, 5:6], fixm[:, :], AX, ALU.max)
                go(dve.tensor_scalar(pen[:, :], same[:, :], -1.0, BIG, ALU.add, ALU.mult))
                go(dve.scalar_tensor_tensor(fx[:, 6:7], dstf[:, 0:1], float(-N), fx[:, 5:6], ALU.add, ALU.mult))
                dve.tensor_scalar(fix_i[:, :], fx[:, 6:7], float(N), None, ALU.add)
                go(dve.tensor_tensor_scan(sl_all[:, :], same[:, :], zrow[:, :], 0.0, ALU.mult, ALU.add))
                go(dve.tensor_scalar(inv_cnt[:, :], sl_all[:, :], 1.0, None, ALU.max))
                go(dve.reciprocal(inv_cnt[:, :], inv_cnt[:, :]))
                dve.tensor_tensor_reduce(m_all[:, 0:COLS], fixm[:, :], sl_all[:, :], 1.0, 0.0, ALU.mult, ALU.add,
                                         fx[:, 7:8])
                dve.tensor_scalar(wq[:, :], ones[:, :], dstf[:, 0:1], None, ALU.mult)
                go(dve.tensor_scalar(wqt[:, :], ones[:, :], dstf[:, COLS - 1:COLS], None, ALU.mult))
                for l in range(LAYERS):
                    go(dve.tensor_tensor_reduce(wide2[0:ED, 0, :], eat[0:ED, l * D:(l + 1) * D],
                                                eat[0:ED, (LAYERS + l) * D:(LAYERS + l + 1) * D], 1.0, 0.0,
                                                ALU.mult, ALU.add, e4[0:ED, l:l + 1]))
                dve.wait_ge(pool_s.h, pool_s.at(2))
                for l in range(LAYERS):
                    go(dve.tensor_scalar(lrow[0:ED, l * ED:(l + 1) * ED], ident[0:ED, 0:ED], e4[0:ED, l:l + 1], None,
                                         ALU.mult))
                dve.sem_inc(d2p.h, 1)
                dve.wait_ge(p2d.h, p2d.at(1))
                dve.tensor_scalar(chain_m[:, :], ps[0][:, 0:P], dstf[:, COLS - 1:COLS], None, ALU.is_equal)
                dve.tensor_scalar(chain_pen[:, :], ps[1][:, 0:P], dstf[:, 0:1], None, ALU.is_equal)
                go(dve.tensor_copy(wide2[:, 0, 0:LAYERS * ED], ps[2][:, 0:LAYERS * ED]))
                dve.sem_inc(d2p.h, 1)
                ea3 = ea[:, :].rearrange("p (j k) -> p j k", k=ED)
                eat3 = eat[:, 0:COLS * ED].rearrange("p (j k) -> p j k", k=ED)
                dve.tensor_copy(lrow[:, 0:1], sl_all[:, COLS - 1:COLS])
                for l in range(LAYERS):
                    v = wide2[:, 0, l * ED:(l + 1) * ED].unsqueeze(1).to_broadcast([P, COLS, ED])
                    go(dve.tensor_tensor(eat3, ea3, v, ALU.mult))
                    go(dve.tensor_reduce(edge_c[:, l, :], eat3, AX, ALU.add))
                    go(dve.tensor_tensor_scan(loop_c[:, l, :], same[:, :], edge_c[:, l, :], 0.0, ALU.mult, ALU.add))
                    dve.tensor_copy(lrow[:, 1 + l:2 + l], loop_c[:, l, COLS - 1:COLS])
                    go(dve.tensor_tensor_reduce(m_all[:, 0:COLS], fixm[:, :], loop_c[:, l, :], 1.0, 0.0, ALU.mult,
                                                ALU.add, loop_fix[:, l:l + 1]))
                    go(dve.tensor_tensor(loop_c[:, l, :], loop_c[:, l, :], inv_cnt[:, :], ALU.mult))
                dve.wait_ge(pool_s.h, pool_s.at(4))
                go(dve.tensor_scalar(chain_pen[:, :], chain_pen[:, :], -1.0, BIG, ALU.add, ALU.mult))
                dve.sem_inc(d2p.h, 1)
                dve.wait_ge(p2d.h, p2d.at(2))
                go(dve.tensor_tensor(inv_cnt_fix[:, :], ps[3][:, 0:1], fx[:, 7:8], ALU.add))
                go(dve.tensor_scalar(inv_cnt_fix[:, :], inv_cnt_fix[:, :], 1.0, None, ALU.max))
                go(dve.reciprocal(inv_cnt_fix[:, :], inv_cnt_fix[:, :]))
                go(dve.tensor_tensor(loop_fix[:, :], ps[3][:, 1:1 + LAYERS], loop_fix[:, :], ALU.add))
                go(dve.tensor_scalar(loop_fix[:, :], loop_fix[:, :], inv_cnt_fix[:, 0:1], None, ALU.mult))
                dve_s.total = go.total

            @block.tensor
            def _(pe):
                pe.wait_ge(d2p.h, d2p.at(1))
                pe.transpose(ps[0][:, 0:P], wq[:, :], ident[:, :])
                pe.transpose(ps[1][:, 0:P], wqt[:, :], ident[:, :])
                pe.matmul(ps[2][:, 0:LAYERS * ED], ones[0:ED, :], lrow[0:ED, 0:LAYERS * ED], start=True,
                          stop=True).then_inc(p2d.h, 1)
                pe.wait_ge(d2p.h, d2p.at(3))
                pe.matmul(ps[3][:, 0:1 + LAYERS], chain_m[:, :], lrow[:, 0:1 + LAYERS], start=True,
                          stop=True).then_inc(p2d.h, 1)
        dve_s.base += dve_s.total
        d2a.base += 1
        a2d.base += 1
        pool_s.base += 4
        d2p.base += 3
        p2d.base += 2
        load.base += NLOAD[0]

        raw = [in_h[:, 0, i, 0:D] for i in range(G)] + [in_h[:, 1, i, 0:D] for i in range(G)]
        mean_ws, mean_wn, att_ww, att_ws, kw, mids = raw[0], raw[1], raw[2], raw[3], raw[4], raw[5:8]
        qw = in_h[:, 0, 8, 0:D + 1]
        gat_raw_t = raw[16:16 + LAYERS]
        mbeta = raw[21:24]
        bcols = raw[24:28]
        vec = in_r[:, 0, 0, :]
        V_MS, V_MN, V_AW, V_AS, V_QB, V_KB, V_B, V_SRC, V_DST = 0, 1, 2, 3, 4, 5, 6, 11, 16
        blend = [math.log(THETA / (i + 1) + 1.0) for i in range(3)]
        with nc.Block() as block:
            @block.sync
            def _(sp):
                n = 0

                def get(dst_ap, src_ap):
                    sp.dma_start(dst_ap, src_ap).then_inc(load.h, 16)
                    return 16
                for l in range(3):
                    n += get(sage_l[:, l, :], t["L0_gnn_Wl"][l])
                    n += get(sage_r[:, l, :], t["L0_gnn_Wr"][l])
                    n += get(mids[l], t["L3_gnn_mid_ws"][l])
                for l in range(LAYERS):
                    n += get(gat_w[:, l, :], t["L3_gnn_Ws"][l])
                for a, b in ((mean_ws, "L1_gnn_W_self"), (mean_wn, "L1_gnn_W_neigh"), (att_ww, "L2_gnn_W_w"),
                             (att_ws, "L2_gnn_WS_w"), (kw, "L2_gnn_k_w")):
                    n += get(a, t[b])
                n += get(qw[:, 0:D], t["L2_gnn_q_w"])

                def col(dst_ap, v):
                    return get(dst_ap, v.rearrange("(p o) -> p o", o=1))
                n += col(vec[:, V_MS:V_MS + 1], t["L1_gnn_b_self"])
                n += col(vec[:, V_MN:V_MN + 1], t["L1_gnn_b_neigh"])
                n += col(vec[:, V_AW:V_AW + 1], t["L2_gnn_W_b"])
                n += col(vec[:, V_AS:V_AS + 1], t["L2_gnn_WS_b"])
                n += col(vec[:, V_KB:V_KB + 1], t["L2_gnn_k_b"])
                n += col(qw[:, D:D + 1], t["L2_gnn_q_b"])
                for l in range(LAYERS):
                    n += col(vec[:, V_B + l:V_B + l + 1], t["L3_gnn_biases"][l])
                    n += col(vec[:, V_SRC + 2 * l:V_SRC + 2 * l + 1], t["L3_gnn_a_srcs"][l])
                    n += col(vec[:, V_SRC + 2 * l + 1:V_SRC + 2 * l + 2], t["L3_gnn_a_dsts"][l])
                for l in range(3):
                    n += col(bn_par[:, 0, l:l + 1], t["L0_gnn_b"][l])
                    n += col(bn_par[:, 1, l:l + 1], t["L0_gnn_gamma"][l])
                    n += col(bn_par[:, 2, l:l + 1], t["L0_gnn_beta"][l])
                NLOAD[0] = n
                sp.wait_ge(d2a.h, d2a.at(1))
                zeros = outb[:, 0, :, :].rearrange("p g w -> p (g w)")
                for s in range(ST):
                    sp.dma_start(agg[s * SUP:(s + 1) * SUP, :].rearrange("(p g) w -> p (g w)", p=P),
                                 zeros).then_inc(load.h, 16)
                sp.dma_start(agg[ST * SUP:N, :].rearrange("(p g) w -> p (g w)", p=LASTP),
                             zeros[0:LASTP, :]).then_inc(load.h, 16)
                sp.wait_ge(load.h, load.at(n + 16 * (ST + 1)))
                sp.sem_inc(a2d.h, 1)

            @block.vector
            def _(dve):
                go = Chain(dve, dve_s)
                dve.memset(outu[:, :, :, :], 0.0)
                go(dve.memset(outb[:, :, :, :], 0.0))
                dve.sem_inc(d2a.h, 1)
                dve.wait_ge(a2d.h, a2d.at(1))
                for l in range(3):
                    go(dve.tensor_scalar(mbeta[l], ident[:, :], 1.0 - blend[l], None, ALU.mult))
                    go(dve.scalar_tensor_tensor(mbeta[l], mids[l], blend[l], mbeta[l], ALU.mult, ALU.add))
                    go(dve.tensor_scalar(mid_w[:, l, :], mbeta[l], ALPHA, None, ALU.mult))
                go(dve.tensor_tensor(vec[:, V_MS:V_MS + 1], vec[:, V_MS:V_MS + 1], vec[:, V_MN:V_MN + 1], ALU.add))
                go(dve.tensor_scalar(bcols[0], ones[:, :], vec[:, V_MS:V_MS + 1], None, ALU.mult))
                go(dve.tensor_scalar(bcols[1], ones[:, :], vec[:, V_AS:V_AS + 1], None, ALU.mult))
                go(dve.tensor_scalar(bcols[2], ones[:, :], vec[:, V_AW:V_AW + 1], None, ALU.mult))
                go(dve.tensor_scalar(bcols[3], ones[:, :], vec[:, V_KB:V_KB + 1], None, ALU.mult))
                dve.sem_inc(d2p.h, 1)
                dve.wait_ge(p2d.h, p2d.at(1))
                dve.tensor_copy(mean_w[:, 0, :], ps[0][:, 0:D])
                dve.tensor_copy(mean_w[:, 1, :], ps[0][:, D:2 * D])
                dve.tensor_copy(att_w[:, 0, :], ps[0][:, 2 * D:3 * D])
                dve.tensor_copy(att_w[:, 1, :], ps[0][:, 3 * D:4 * D])
                for g in range(GT):
                    dve.tensor_copy(mean_b[:, g, :], ps[1][:, 0:D])
                    dve.tensor_copy(att_b[:, g, :], ps[1][:, D:2 * D])
                dve.tensor_copy(att_mb[:, :], ps[1][:, 2 * D:3 * D])
                dve.tensor_scalar(key_w[:, :], ps[2][:, 0:D + 1], float(D) ** -0.5, None, ALU.mult)
                dve.tensor_scalar(key_b[:, :], ps[2][:, 256:256 + D + 1], float(D) ** -0.5, None, ALU.mult)
                for l in range(LAYERS):
                    go(dve.tensor_copy(gat_raw_t[l], ps[3 + l // 4][:, (l % 4) * D:(l % 4 + 1) * D]))
                for l in range(LAYERS):
                    go(dve.tensor_scalar(yb[:, l // 4, l % 4, :], ones[:, :], vec[:, V_B + l:V_B + l + 1], None, ALU.mult))
                dve.sem_inc(d2p.h, 1)
                dve.wait_ge(p2d.h, p2d.at(2))
                for l in range(LAYERS):
                    dve.tensor_copy(gat_s[:, l, :], ps[5][:, 2 * l:2 * l + 2])
                    scale = 1.0 - ALPHA if 1 <= l <= 3 else 1.0
                    for g in range(GT):
                        dve.tensor_scalar(gat_b[:, l, g, :], ps[6 + l // 4][:, (l % 4) * D:(l % 4 + 1) * D], scale,
                                          None, ALU.mult)
                for l in range(3):
                    go(dve.tensor_scalar(gat_w[:, l + 1, :], ps[0][:, l * D:(l + 1) * D], 1.0 - ALPHA, None, ALU.mult))
                dve_s.total = go.total

            @block.tensor
            def _(pe):
                pe.wait_ge(d2p.h, d2p.at(1))
                for k, w in enumerate((mean_ws, mean_wn, att_ws, att_ww)):
                    pe.transpose(ps[0][:, k * D:(k + 1) * D], w, ident[:, :])
                for k in range(3):
                    pe.matmul(ps[1][:, k * D:(k + 1) * D], bcols[k], ident[:, :], start=True, stop=True)
                pe.matmul(ps[2][:, 0:D + 1], kw, qw, start=True, stop=True)
                pe.matmul(ps[2][:, 256:256 + D + 1], bcols[3], qw, start=True, stop=True)
                for l in range(LAYERS):
                    mm = pe.transpose(ps[3 + l // 4][:, (l % 4) * D:(l % 4 + 1) * D], gat_w[:, l, :], ident[:, :])
                mm.then_inc(p2d.h, 1)
                pe.wait_ge(d2p.h, d2p.at(2))
                for l in range(3):
                    pe.matmul(ps[0][:, l * D:(l + 1) * D], gat_raw_t[l + 1], mbeta[l], start=True, stop=True)
                for l in range(LAYERS):
                    pe.matmul(ps[5][:, 2 * l:2 * l + 2], gat_raw_t[l], vec[:, V_SRC + 2 * l:V_SRC + 2 * l + 2],
                              start=True, stop=True)
                    mm = pe.matmul(ps[6 + l // 4][:, (l % 4) * D:(l % 4 + 1) * D], yb[:, l // 4, l % 4, :],
                                   mbeta[l - 1] if 1 <= l <= 3 else ident[:, :], start=True, stop=True)
                mm.then_inc(p2d.h, 1)
        dve_s.base += dve_s.total
        d2a.base += 1
        a2d.base += 1
        d2p.base += 2
        p2d.base += 2
        load.base += NLOAD[0] + 16 * (ST + 1)

        def edge_pass(mode, tab, bn=False, layer=0):
            wide_tab = tab.shape[1] == W
            buf = rows if wide_tab else rows_x
            flash = mode != "mean"
            PER = {"mean": 18 + 6 * bn, "att": 26, "gat": 36}[mode]

            with nc.Block() as block:
                @block.gpsimd
                def _(pool):
                    def ticked(s, n):
                        pool.wait_ge(s.h, s.at(n))
                        pool.sem_inc(tick.h, 1)

                    def gathers(par):
                        for j in range(CH):
                            pool.indirect_dma_start(
                                out=buf[:, par, j, :], out_offset=None, in_=tab[:, :],
                                in_offset=bass.IndirectOffsetOnAxis(ap=gi[:, par, j:j + 1], axis=0)
                            ).then_inc(gath[par].h, 16)
                            if flash:
                                dtab = tab_u if mode == "att" else pair_tab
                                dbuf = drows if mode == "att" else dpair
                                pool.indirect_dma_start(
                                    out=dbuf[:, par, j, :], out_offset=None, in_=dtab[:, :],
                                    in_offset=bass.IndirectOffsetOnAxis(ap=di[:, par, j:j + 1], axis=0)
                                ).then_inc(gath_d[par].h, 16)

                    def scatters(k, par):
                        ticked(ob_ready, k + 1)
                        for j in range(CH):
                            pool.indirect_dma_start(
                                out=agg[:, :], out_offset=bass.IndirectOffsetOnAxis(ap=wi[:, par, j:j + 1], axis=0),
                                in_=obuf[:, par, j, :], in_offset=None, bounds_check=N - 1, oob_is_err=False
                            ).then_inc(scat[par].h, 16)

                    def step(k, par, first=False):
                        ticked(idx_ready, k + 2)
                        if not first:
                            ticked(rows_used, k)
                        gathers(1 - par)
                        scatters(k, par)

                    ticked(idx_ready, 1)
                    gathers(0)
                    step(0, 0, True)
                    step(1, 1)
                    with pool.Fori(1, (NCH - 1) // 2) as i:
                        step(2 * i, 0)
                        step(2 * i + 1, 1)
                    scatters(NCH - 1, 0)
                    ticked(fix_ready, 1)
                    pool.indirect_dma_start(
                        out=agg[:, :], out_offset=bass.IndirectOffsetOnAxis(ap=fix_i[:, 0:1], axis=0),
                        in_=fixo[:, :], in_offset=None, bounds_check=N - 1, oob_is_err=False).then_inc(scat_fix.h, 16)
                    pool.wait_ge(scat_fix.h, scat_fix.at(16))
                    pool.wait_ge(scat[0].h, scat[0].at(16 * CH * ((NCH + 1) // 2)))
                    pool.wait_ge(scat[1].h, scat[1].at(16 * CH * ((NCH - 1) // 2)))

                @block.vector
                def _(dve):
                    go = Chain(dve, dve_s)

                    def copy_at(dst_ap, src_ap):
                        dve.sem_inc(tick.h, 1)
                        return dve.tensor_copy(dst_ap, src_ap)

                    def stage(k, par):
                        if flash:
                            copy_at(di[:, par, :], dst_i[:, bass.ds(k * CH, CH)])
                        copy_at(gi[:, par, :], src_i[:, bass.ds(k * CH, CH)]).then_inc(idx_ready.h, 1)

                    def chunk(k, par, it, first=False):
                        c = bass.ds(k * CH, CH)
                        c1 = bass.ds(k * CH + 1, CH)
                        now = bass.ds(k * CH, 1)
                        g = buf[:, par, :, 0:D]
                        dve.wait_ge(gath[par].h, gath[par].at(16 * CH * (it + 1)))
                        if flash:
                            dve.wait_ge(gath_d[par].h, gath_d[par].at(16 * CH * (it + 1)))
                        stage(k + 2, par)
                        if mode == "mean":
                            if bn:
                                go(dve.tensor_tensor(wide[:, :, :], g, bc(bn_row[:, 0, :], CH), ALU.mult))
                                go(dve.tensor_tensor(wide[:, :, :], wide[:, :, :], bc(bn_row[:, 1, :], CH), ALU.add))
                                go(dve.tensor_scalar(wide[:, :, :], wide[:, :, :], 0.0, None, ALU.max))
                                terms = wide
                            else:
                                terms = buf[:, par]
                            copy_at(sc8[:, 0, :], inv_cnt[:, c])
                            go(copy_at(x4[:, 0:CH], same[:, c]))
                        else:
                            if mode == "gat":
                                go(dve.tensor_tensor(z8[:, :], buf[:, par, :, D], dpair[:, par, :, 1], ALU.add))
                                dve.tensor_tensor(sl_all[:, c], dpair[:, par, :, 0], dpair[:, par, :, 1], ALU.add)
                                go(dve.tensor_tensor(z8[:, :], z8[:, :], edge_c[:, layer, c], ALU.add))
                                go(dve.tensor_tensor(l8[:, :], sl_all[:, c], loop_c[:, layer, c], ALU.add))
                                go(dve.scalar_tensor_tensor(s8[:, :], z8[:, :], ATT_SLOPE, z8[:, :], ALU.mult, ALU.max))
                                go(dve.scalar_tensor_tensor(l8[:, :], l8[:, :], ATT_SLOPE, l8[:, :], ALU.mult, ALU.max))
                            else:
                                go(dve.tensor_tensor(wide[:, :, :], g, drows[:, par, :, 0:D], ALU.mult))
                                go(dve.tensor_reduce(z8[:, :], wide[:, :, :], AX, ALU.add))
                                go(dve.tensor_tensor(s8[:, :], z8[:, :], drows[:, par, :, D], ALU.add))
                            go(dve.tensor_tensor_scan(m_all[:, c1], pen[:, c], s8[:, :], m_all[:, now], ALU.add, ALU.max))
                            go(dve.tensor_tensor(z8[:, :], m_all[:, c], pen[:, c], ALU.add))
                            dve.tensor_tensor(e4[:, 0:CH], z8[:, :], m_all[:, c1], ALU.subtract)
                            go(dve.tensor_tensor(e4[:, CH:2 * CH], s8[:, :], m_all[:, c1], ALU.subtract))
                            ne = 2
                            if mode == "gat":
                                ne = 4
                                go(dve.tensor_tensor(z8[:, :], m_all[:, c1], l8[:, :], ALU.max))
                                dve.tensor_tensor(e4[:, 2 * CH:3 * CH], m_all[:, c1], z8[:, :], ALU.subtract)
                                go(dve.tensor_tensor(e4[:, 3 * CH:4 * CH], l8[:, :], z8[:, :], ALU.subtract))
                            dve.sem_inc(exp_in.h, 1)
                            dve.wait_ge(exp_out.h, exp_out.at(k + 1))
                            go(dve.tensor_tensor_scan(den_all[:, c1], x4[:, 0:CH], x4[:, CH:2 * CH], den_all[:, now],
                                                      ALU.mult, ALU.add))
                            if mode == "gat":
                                go(dve.tensor_tensor(z8[:, :], den_all[:, c1], x4[:, 2 * CH:3 * CH], ALU.mult))
                                go(dve.tensor_tensor(z8[:, :], z8[:, :], x4[:, 3 * CH:4 * CH], ALU.add))
                                go(dve.reciprocal(z8[:, :], z8[:, :]))
                                dve.tensor_tensor(sc8[:, 0, :], z8[:, :], x4[:, 2 * CH:3 * CH], ALU.mult)
                                go(dve.tensor_tensor(l8[:, :], z8[:, :], x4[:, 3 * CH:4 * CH], ALU.mult))
                                go(dve.tensor_scalar(sc8[:, 1, :], l8[:, :], -1.0, None, ALU.add))
                            else:
                                go(copy_at(z8[:, :], den_all[:, c1]))
                                go(dve.reciprocal(sc8[:, 0, :], z8[:, :]))
                            go(dve.tensor_tensor(wide[:, :, :], g, bl(x4[:, CH:2 * CH]), ALU.mult))
                            terms = wide
                        for j in range(CH):
                            before = state[:, par, j - 1, :] if j else state[:, 1 - par, CH - 1, :]
                            go(dve.scalar_tensor_tensor(state[:, par, j, :], before, x4[:, j:j + 1],
                                                        terms[:, j, 0:D], ALU.mult, ALU.add))
                        dve.sem_inc(rows_used.h, 1)
                        if not first:
                            dve.wait_ge(scat[par].h, scat[par].at(16 * CH * it))
                        copy_at(wi[:, par, :], scat_i[:, c])
                        if flash:
                            dve.tensor_copy(obuf[:, par, :, D], sc8[:, 1, :] if mode == "gat" else ones[:, 0:CH])
                        go(dve.tensor_tensor(obuf[:, par, :, 0:D], state[:, par, :, :], bl(sc8[:, 0, :]), ALU.mult))
                        dve.sem_inc(ob_ready.h, 1)
                        go(copy_at(z8[:, :], fixm[:, c]))
                        go(dve.tensor_tensor(wide2[:, :, :], state[:, par, :, :], bl(z8[:, :]), ALU.mult))
                        go(dve.tensor_reduce(fixt[:, :], wide2[:, :, :].rearrange("p j d -> p d j"), AX, ALU.add))
                        go(dve.tensor_tensor(fixv[:, :], fixv[:, :], fixt[:, :], ALU.add))

                    go(dve.memset(state[:, :, :, :], 0.0))
                    go(dve.memset(fixv[:, :], 0.0))
                    dve.memset(m_all[:, 0:1], -BIG)
                    go(dve.memset(den_all[:, 0:1], 0.0))
                    stage(0, 0)
                    stage(1, 1)
                    chunk(0, 0, 0, True)
                    chunk(1, 1, 0, True)
                    turns = (NCH - 1) // 2 - 1
                    with dve.Fori(1, (NCH - 1) // 2) as i:
                        go.enter(i - 1, PER_TURN[mode, bn], turns)
                        chunk(2 * i, 0, i)
                        chunk(2 * i + 1, 1, i)
                        go.leave()
                    chunk(NCH - 1, 0, (NCH - 1) // 2)

                    last = state[:, 0, CH - 1, :]
                    go(dve.tensor_copy(lrow[:, 0:D], last))
                    go(dve.memset(fixo[:, :], 0.0))
                    if not flash:
                        dve.sem_inc(d2p.h, 1)
                        dve.wait_ge(p2d.h, p2d.at(1))
                        go(dve.tensor_tensor(fixt[:, :], ps[0][:, 0:D], fixv[:, :], ALU.add))
                        go(dve.tensor_scalar(fixo[:, 0:D], fixt[:, :], inv_cnt_fix[:, 0:1], None, ALU.mult))
                    else:
                        go(dve.tensor_copy(lrow[:, D:D + 1], den_all[:, COLS:COLS + 1]))
                        go(dve.tensor_scalar(wq[:, :], ones[:, :], m_all[:, COLS:COLS + 1], None, ALU.mult))
                        dve.sem_inc(d2p.h, 1)
                        for k, a in ((0, m_all[:, 1:COLS + 1]), (1, den_all[:, 1:COLS + 1]), (2, sl_all[:, :])):
                            if k < 2 or mode == "gat":
                                go(dve.tensor_tensor_reduce(zrow[:, :], fixm[:, :], a, 1.0, 0.0, ALU.mult, ALU.add,
                                                            fx[:, k:k + 1]))
                        dve.wait_ge(p2d.h, p2d.at(1))
                        go(dve.tensor_tensor(wq[:, :], ps[0][:, 0:P], chain_pen[:, :], ALU.add))
                        go(dve.tensor_reduce(fx[:, 3:4], wq[:, :], AX, ALU.max))
                        go(dve.tensor_tensor(fx[:, 3:4], fx[:, 3:4], fx[:, 0:1], ALU.max))
                        if mode == "gat":
                            go(dve.tensor_tensor(fx[:, 2:3], fx[:, 2:3], loop_fix[:, layer:layer + 1], ALU.add))
                            go(dve.scalar_tensor_tensor(fx[:, 2:3], fx[:, 2:3], ATT_SLOPE, fx[:, 2:3], ALU.mult,
                                                        ALU.max))
                            go(dve.tensor_tensor(fx[:, 3:4], fx[:, 3:4], fx[:, 2:3], ALU.max))
                            go(dve.tensor_tensor(fx[:, 5:6], fx[:, 2:3], fx[:, 3:4], ALU.subtract))
                        else:
                            go(dve.memset(fx[:, 5:6], -BIG))
                        go(dve.tensor_scalar(wq[:, :], wq[:, :], fx[:, 3:4], None, ALU.subtract))
                        go(dve.tensor_tensor(fx[:, 4:5], fx[:, 0:1], fx[:, 3:4], ALU.subtract))
                        dve.sem_inc(exp_in.h, 1)
                        dve.wait_ge(p2d.h, p2d.at(2))
                        go(dve.tensor_copy(wqt[:, :], ps[1][:, 0:P]))
                        dve.sem_inc(d2p.h, 1)
                        dve.wait_ge(p2d.h, p2d.at(3))
                        go(dve.tensor_scalar(fx[:, 8:9], fx[:, 1:2], fx[:, 6:7], None, ALU.mult))
                        go(dve.tensor_tensor(fx[:, 8:9], ps[0][:, D:D + 1], fx[:, 8:9], ALU.add))
                        go(dve.tensor_tensor(fx[:, 8:9], fx[:, 8:9], fx[:, 7:8], ALU.add))
                        go(dve.tensor_scalar(fx[:, 8:9], fx[:, 8:9], 1.0e-30, None, ALU.max))
                        go(dve.reciprocal(fx[:, 9:10], fx[:, 8:9]))
                        go(dve.scalar_tensor_tensor(fixt[:, :], fixv[:, :], fx[:, 6:7], ps[0][:, 0:D], ALU.mult, ALU.add))
                        go(dve.tensor_scalar(fixo[:, 0:D], fixt[:, :], fx[:, 9:10], None, ALU.mult))
                        if mode == "gat":
                            go(dve.tensor_tensor(fx[:, 10:11], fx[:, 7:8], fx[:, 9:10], ALU.mult))
                            go(dve.tensor_scalar(fixo[:, D:D + 1], fx[:, 10:11], -1.0, None, ALU.add))
                        else:
                            go(dve.memset(fixo[:, D:D + 1], 1.0))
                    dve.sem_inc(fix_ready.h, 1)
                    dve_s.total = go.total

                if flash:
                    @block.scalar
                    def _(act):
                        n = (4 if mode == "gat" else 2) * CH

                        def exps(k):
                            act.wait_ge(exp_in.h, exp_in.at(k + 1))
                            act.activation(x4[:, 0:n], e4[:, 0:n], ACT.Exp).then_inc(exp_out.h, 1)
                        with act.Fori(0, NCH) as k:
                            exps(k)
                        act.wait_ge(exp_in.h, exp_in.at(NCH + 1))
                        act.activation(wqt[:, :], wq[:, :], ACT.Exp)
                        act.activation(fx[:, 6:8], fx[:, 4:6], ACT.Exp).then_inc(exp_out.h, 1)
                        act.wait_ge(exp_out.h, exp_out.at(NCH + 1))
                        act.sem_inc(a2p.h, 1)

                @block.tensor
                def _(pe):
                    if not flash:
                        pe.wait_ge(d2p.h, d2p.at(1))
                        pe.matmul(ps[0][:, 0:D], chain_m[:, :], lrow[:, 0:D], start=True, stop=True).then_inc(p2d.h, 1)
                    else:
                        pe.wait_ge(d2p.h, d2p.at(1))
                        pe.transpose(ps[0][:, 0:P], wq[:, :], ident[:, :]).then_inc(p2d.h, 1)
                        pe.wait_ge(a2p.h, a2p.at(1))
                        pe.transpose(ps[1][:, 0:P], wqt[:, :], ident[:, :]).then_inc(p2d.h, 1)
                        pe.wait_ge(d2p.h, d2p.at(2))
                        pe.matmul(ps[0][:, 0:D + 1], wqt[:, :], lrow[:, :], start=True, stop=True).then_inc(p2d.h, 1)

            dve_s.base += dve_s.total
            idx_ready.base += NCH + 2
            rows_used.base += NCH
            ob_ready.base += NCH
            fix_ready.base += 1
            scat_fix.base += 16
            for par, n in ((0, (NCH + 1) // 2), (1, (NCH - 1) // 2)):
                gath[par].base += 16 * CH * n
                scat[par].base += 16 * CH * n
                if flash:
                    gath_d[par].base += 16 * CH * n
            if flash:
                exp_in.base += NCH + 1
                exp_out.base += NCH + 1
                a2p.base += 1
                d2p.base += 2
                p2d.base += 3
            else:
                d2p.base += 1
                p2d.base += 1

        PER_TURN = {("mean", False): 2 * (1 + CH + 1 + 4), ("mean", True): 2 * (4 + CH + 1 + 4),
                    ("att", False): 2 * (3 + 3 + 4 + CH + 1 + 4), ("gat", False): 2 * (5 + 3 + 2 + 7 + CH + 1 + 4)}

        def node_pass(mode, h_tab, out_tab, extra=None, bn=False, layer=0):
            has_agg = mode != "skip"
            products = mode != "skip"
            mid = mode == "gat" and 1 <= layer <= 3
            loops = mode in ("gat", "last")
            two = mode in ("sage", "mean", "att") or mid
            normed = mode in ("skip", "mean", "att", "last")
            second = {"mean": "keys", "att": "scal", "gat": "scal"}.get(mode)
            loads = 1 + has_agg + (extra is not None)
            stores = 1 + (second is not None)
            e_w = extra.shape[1] if extra is not None else W
            h_w = h_tab.shape[1]
            o_w = out_tab.shape[1]
            same_x0 = mid and layer == 1
            hb = in_h if h_w == W else in_h
            score_l = 0 if mode == "att" else layer + 1
            if mode == "sage":
                w1, w2 = sage_r[:, layer, :], sage_l[:, layer, :]
            elif mode == "mean":
                w1, w2 = mean_w[:, 0, :], mean_w[:, 1, :]
            elif mode == "att":
                w1, w2 = att_w[:, 0, :], att_w[:, 1, :]
            elif loops:
                w1 = gat_w[:, layer, :]
                w2 = mid_w[:, layer - 1, :] if mid else None
            bias = {"mean": mean_b, "att": att_b}.get(mode)
            if loops:
                bias = gat_b[:, layer]
            h_v = (lambda par, g: in_h[:, par, g * GT:(g + 1) * GT, 0:D])
            r_v = (lambda par, g: in_r[:, par, g * GT:(g + 1) * GT, 0:D])
            e_v = (lambda par, g: in_e[:, par, g * GT:(g + 1) * GT, 0:D])
            o_v = (lambda par, g: outb[:, par, g * GT:(g + 1) * GT, 0:D])

            def rows_of(tab, s, parts):
                return tab[bass.ds(s * SUP, parts * G), :].rearrange("(p g) w -> p g w", p=parts)

            def walk(eng, body, chain=None, per=0):
                body(0, (0, 1), True, P)
                with eng.Fori(1, PAIRS) as i:
                    if chain is not None:
                        chain.enter(i - 1, per, PAIRS - 1)
                    body(i, (0, 1), False, P)
                    if chain is not None:
                        chain.leave()
                body(PAIRS, (0,), False, LASTP)

            def past(q, lag, first):
                return not first or q >= lag

            NGR = NG * (ST + 1)
            with nc.Block() as block:
                @block.sync
                def _(sp):
                    def body(it, pars, first, parts):
                        for par in pars:
                            s = 2 * it + par
                            if not first:
                                sp.wait_ge(out_ready.h, out_ready.at(NG * (s - 1)))
                                if mode == "sage":
                                    sp.wait_ge(tr_done.h, tr_done.at(NG * (s - 1)))
                            for tab, b in ((h_tab, in_h), (agg if has_agg else None, in_r), (extra, in_e)):
                                if tab is not None:
                                    sp.dma_start(b[0:parts, par, :, 0:tab.shape[1]], rows_of(tab, s, parts))\
                                      .then_inc(ld[par].h, 16)
                    walk(sp, body)

                @block.gpsimd
                def _(pool):
                    def body(it, pars, first, parts):
                        for par in pars:
                            s = 2 * it + par
                            done = m2_read if second else out_ready
                            pool.wait_ge(done.h, done.at(NG * (s + 1)))
                            pool.sem_inc(tick.h, 1)
                            pool.dma_start(rows_of(out_tab, s, parts), outb[0:parts, par, :, 0:o_w])\
                                .then_inc(stq[par].h, 16)
                            if second == "keys":
                                pool.dma_start(rows_of(tab_u, s, parts), outu[0:parts, par, :, :])\
                                    .then_inc(stq[par].h, 16)
                            if second == "scal":
                                pool.dma_start(rows_of(pair_tab, s, parts), outp[0:parts, par, :, :])\
                                    .then_inc(stq[par].h, 16)
                    walk(pool, body)
                    pool.wait_ge(stq[0].h, stq[0].at(16 * stores * (PAIRS + 1)))
                    pool.wait_ge(stq[1].h, stq[1].at(16 * stores * PAIRS))

                @block.tensor
                def _(pe):
                    def body(it, pars, first, parts):
                        groups = [(par, g) for par in pars for g in range(NG)]
                        q0 = 2 * NG * it

                        def turn(n):
                            par, g = groups[n]
                            q = q0 + n
                            if g == 0:
                                pe.wait_ge(ld[par].h, ld[par].at(16 * loads * (it + 1)))
                            if loops:
                                pe.wait_ge(y_ready.h, y_ready.at(q + 1))
                            if past(q, 2, first):
                                pe.wait_ge(ht_ready.h, ht_ready.at(q + 1 - 2))
                            for k in range(GT):
                                a = yb[:, n % 2, k, :] if loops else in_h[:, par, g * GT + k, 0:D]
                                mm = pe.transpose(ps[n % 2][:, k * D:(k + 1) * D], a, ident[:, :])
                            mm.then_inc(th_done.h, 1)
                            if two:
                                if past(q, 1, first):
                                    pe.wait_ge(rt_ready.h, rt_ready.at(q + 1 - 1))
                                b = in_r if not mid else (in_h if same_x0 else in_e)
                                for k in range(GT):
                                    mm = pe.transpose(ps[2][:, k * D:(k + 1) * D], b[:, par, g * GT + k, 0:D], ident[:, :])
                                mm.then_inc(tr_done.h, 1)

                        def product(n):
                            q = q0 + n
                            pe.wait_ge(ht_ready.h, ht_ready.at(q + 1))
                            if two:
                                pe.wait_ge(rt_ready.h, rt_ready.at(q + 1))
                            if past(q, 2, first):
                                used = sq_ready if mode == "sage" else post_read
                                pe.wait_ge(used.h, used.at(q - 1))
                            for k in range(GT):
                                o = ps[3 + n % 2][:, k * D:(k + 1) * D]
                                mm = pe.matmul(o, ht[:, n % 2, k, :], w1, start=True, stop=not two)
                                if two:
                                    mm = pe.matmul(o, rt[:, n % 2, k, :], w2, start=False, stop=True)
                            mm.then_inc(mm_done.h, 1)

                        def turn_out(n):
                            par, g = groups[n]
                            q = q0 + n
                            pe.wait_ge(out_ready.h, out_ready.at(q + 1))
                            if past(q, 1, first):
                                pe.wait_ge(ot_ready.h, ot_ready.at(q + 1 - 1))
                            for k in range(GT):
                                mm = pe.transpose(ps[5][:, k * D:(k + 1) * D], outb[:, par, g * GT + k, 0:D], ident[:, :])
                            mm.then_inc(t2_done.h, 1)

                        def product_out(n):
                            q = q0 + n
                            pe.wait_ge(ot_ready.h, ot_ready.at(q + 1))
                            if past(q, 1, first):
                                pe.wait_ge(m2_read.h, m2_read.at(q + 1 - 1))
                            for k in range(GT):
                                a = ot[:, n % 2, k, :]
                                if second == "keys":
                                    mm = pe.matmul(ps[6 + k // 2][:, (k % 2) * 256:(k % 2) * 256 + D + 1], a, key_w[:, :],
                                                   start=True, stop=True)
                                else:
                                    mm = pe.matmul(ps[6][:, 2 * k:2 * k + 2], a, gat_s[:, score_l, :], start=True, stop=True)
                            mm.then_inc(m2_done.h, 1)

                        for n in range(len(groups) + 5):
                            if n < len(groups):
                                turn(n)
                            if 1 <= n <= len(groups):
                                product(n - 1)
                            if second:
                                if 4 <= n < len(groups) + 4:
                                    turn_out(n - 4)
                                if 5 <= n:
                                    product_out(n - 5)
                    if products:
                        walk(pe, body)

                @block.scalar
                def _(act):
                    go = Chain(act, act_s)

                    def body(it, pars, first, parts):
                        groups = [(par, g) for par in pars for g in range(NG)]
                        q0 = 2 * NG * it

                        def front(n):
                            q = q0 + n
                            act.wait_ge(th_done.h, th_done.at(q + 1))
                            if past(q, 2, first):
                                act.wait_ge(mm_done.h, mm_done.at(q + 1 - 2))
                            f = ht[:, n % 2, :, :].rearrange("p k d -> p (k d)")
                            if bn:
                                act.activation(f, ps[n % 2][:, :], ACT.Relu, bias=bn_col[:, 1:2],
                                               scale=bn_col[:, 0:1]).then_inc(ht_ready.h, 1)
                            else:
                                act.copy(f, ps[n % 2][:, :]).then_inc(ht_ready.h, 1)

                        def back(n):
                            par, g = groups[n]
                            q = q0 + n
                            o3 = ps[3 + n % 2][:, :].rearrange("p (k d) -> p k d", k=GT)
                            if mode == "sage":
                                act.wait_ge(mm_done.h, mm_done.at(q + 1))
                                if g == 0 and not first:
                                    act.wait_ge(stq[par].h, stq[par].at(16 * stores * it))
                                act.copy(o_v(par, g), o3).then_inc(out_ready.h, 1)
                                if past(q, 1, first):
                                    act.wait_ge(norm_ready.h, norm_ready.at(q + 1 - 1))
                                act.activation(ps[5][:, :], ps[3 + n % 2][:, :], ACT.Square).then_inc(sq_ready.h, 1)
                            if normed:
                                act.wait_ge(norm_ready.h, norm_ready.at(q + 1))
                                if g == 0 and not first:
                                    act.wait_ge(stq[par].h, stq[par].at(16 * stores * it))
                                for k in range(GT):
                                    ins = act.activation(outb[:, par, g * GT + k, 0:D], ub[:, n % 2, k, :], ACT.Identity,
                                                         bias=mv[:, n % 2, k, 0:1], scale=mv[:, n % 2, k, 1:2])
                                ins.then_inc(out_ready.h, 1)

                        def second_turn(n):
                            q = q0 + n
                            act.wait_ge(t2_done.h, t2_done.at(q + 1))
                            if past(q, 2, first):
                                act.wait_ge(m2_done.h, m2_done.at(q + 1 - 2))
                            act.copy(ot[:, n % 2, :, :].rearrange("p k d -> p (k d)"), ps[5][:, :])\
                               .then_inc(ot_ready.h, 1)

                        def root(n):
                            act.wait_ge(var_ready.h, var_ready.at(q0 + n + 1))
                            act.activation(std[:, n % 2, :], mv[:, n % 2, :, 1], ACT.Sqrt).then_inc(std_ready.h, 1)

                        for n in range(len(groups) + 4):
                            if products and n < len(groups):
                                front(n)
                            if normed and 2 <= n < len(groups) + 2:
                                root(n - 2)
                            if 3 <= n < len(groups) + 3:
                                back(n - 3)
                            if second and 4 <= n < len(groups) + 4:
                                second_turn(n - 4)
                    walk(act, body)

                @block.vector
                def _(dve):
                    go = Chain(dve, dve_s)

                    def body(it, pars, first, parts):
                        groups = [(par, g) for par in pars for g in range(NG)]
                        q0 = 2 * NG * it

                        def front(n):
                            par, g = groups[n]
                            q = q0 + n
                            if g == 0:
                                dve.wait_ge(ld[par].h, ld[par].at(16 * loads * (it + 1)))
                            if loops:
                                if g == 0:
                                    go(dve.tensor_scalar(col1[:, par, :], in_r[:, par, :, D], 1.0, None, ALU.add))
                                if past(q, 2, first):
                                    dve.wait_ge(th_done.h, th_done.at(q + 1 - 2))
                                for k in range(GT):
                                    c = g * GT + k
                                    ins = dve.scalar_tensor_tensor(yb[:, n % 2, k, :], in_h[:, par, c, 0:D],
                                                                   col1[:, par, c:c + 1], in_r[:, par, c, 0:D],
                                                                   ALU.mult, ALU.add)
                                ins.then_inc(y_ready.h, 1)

                        def operand(n):
                            q = q0 + n
                            if two:
                                dve.wait_ge(tr_done.h, tr_done.at(q + 1))
                                if past(q, 2, first):
                                    dve.wait_ge(mm_done.h, mm_done.at(q + 1 - 2))
                                dve.tensor_copy(rt[:, n % 2, :, :].rearrange("p k d -> p (k d)"), ps[2][:, :])\
                                   .then_inc(rt_ready.h, 1)

                        def post(n):
                            par, g = groups[n]
                            q = q0 + n
                            o3 = ps[3 + n % 2][:, :].rearrange("p (k d) -> p k d", k=GT)
                            u = ub[:, n % 2, :, :]
                            if mode == "sage":
                                dve.wait_ge(out_ready.h, out_ready.at(q + 1))
                            elif products:
                                dve.wait_ge(mm_done.h, mm_done.at(q + 1))
                            if mode == "sage":
                                go(dve.tensor_tensor(acc[0:parts, 0], o_v(par, g)[0:parts], acc[0:parts, 0], ALU.add))
                                dve.wait_ge(sq_ready.h, sq_ready.at(q + 1))
                                go(dve.tensor_tensor(acc[0:parts, 1],
                                                     ps[5][0:parts, :].rearrange("p (k d) -> p k d", k=GT),
                                                     acc[0:parts, 1], ALU.add))
                                dve.sem_inc(norm_ready.h, 1)
                                return
                            if mode == "gat":
                                if g == 0 and not first:
                                    dve.wait_ge(stq[par].h, stq[par].at(16 * stores * it))
                                if mid:
                                    go(dve.tensor_tensor(u, o3, bias[:, :, :], ALU.add))
                                    dve.sem_inc(post_read.h, 1)
                                    dve.scalar_tensor_tensor(o_v(par, g), u, SLOPE, u, ALU.mult, ALU.max)\
                                       .then_inc(out_ready.h, 1)
                                else:
                                    go(dve.tensor_tensor(o_v(par, g), o3, bias[:, :, :], ALU.add))
                                    dve.sem_inc(post_read.h, 1)
                                    dve.sem_inc(out_ready.h, 1)
                                return
                            if past(q, 2, first):
                                dve.wait_ge(out_ready.h, out_ready.at(q + 1 - 2))
                            if mode == "skip":
                                go(dve.tensor_tensor(u, h_v(par, g), bc(bn_row[:, 0, :], GT), ALU.mult))
                                go(dve.tensor_tensor(u, u, bc(bn_row[:, 1, :], GT), ALU.add))
                                go(dve.scalar_tensor_tensor(u, u, 0.0, e_v(par, g), ALU.max, ALU.add))
                            else:
                                go(dve.tensor_tensor(u, o3, bias[:, :, :], ALU.add))
                                dve.sem_inc(post_read.h, 1)
                            if mode == "mean":
                                go(dve.scalar_tensor_tensor(u, u, 0.0, h_v(par, g), ALU.max, ALU.add))
                            if mode == "last":
                                go(dve.tensor_tensor(u, u, e_v(par, g), ALU.add))
                            if mode == "att":
                                for k in range(GT):
                                    c = g * GT + k
                                    ins = dve.scalar_tensor_tensor(ub[:, n % 2, k, :], att_mb[:, :], in_r[:, par, c, D:D + 1],
                                                                   ub[:, n % 2, k, :], ALU.mult, ALU.add)
                                go(ins)
                                go(dve.tensor_tensor(u, u, h_v(par, g), ALU.add))
                            for k in range(GT):
                                ins = dve.bn_stats(st6[:, k, :], ub[:, n % 2, k, :])
                            go(ins)
                            dve.sem_inc(tick.h, 1)
                            for k in range(GT):
                                ins = dve.bn_aggr(mv[:, n % 2, k, :], st6[:, k, :])
                            go(ins)
                            dve.tensor_scalar(mv[:, n % 2, :, 1], mv[:, n % 2, :, 1], EPS, None, ALU.add)\
                               .then_inc(var_ready.h, 1)

                        def norm(n):
                            dve.wait_ge(std_ready.h, std_ready.at(q0 + n + 1))
                            go(dve.reciprocal(mv[:, n % 2, :, 1], std[:, n % 2, :]))
                            dve.scalar_tensor_tensor(mv[:, n % 2, :, 0], mv[:, n % 2, :, 0], -1.0, mv[:, n % 2, :, 1],
                                                     ALU.mult, ALU.mult).then_inc(norm_ready.h, 1)

                        def scalars(n):
                            par, g = groups[n]
                            q = q0 + n
                            dve.wait_ge(m2_done.h, m2_done.at(q + 1))
                            if second == "keys":
                                if g == 0 and not first:
                                    dve.wait_ge(stq[par].h, stq[par].at(16 * stores * it))
                                for k in range(GT):
                                    ins = dve.tensor_tensor(outu[:, par, g * GT + k, 0:D + 1],
                                                            ps[6 + k // 2][:, (k % 2) * 256:(k % 2) * 256 + D + 1],
                                                            key_b[:, :], ALU.add)
                                ins.then_inc(m2_read.h, 1)
                            else:
                                if g == 0 and not first:
                                    dve.wait_ge(stq[par].h, stq[par].at(16 * stores * it))
                                sv = ps[6][:, 0:2 * GT].rearrange("p (k s) -> p k s", s=2)
                                dve.tensor_copy(outb[:, par, g * GT:(g + 1) * GT, D:D + 2], sv)
                                dve.tensor_copy(outp[:, par, g * GT:(g + 1) * GT, :], sv).then_inc(m2_read.h, 1)

                        for n in range(len(groups) + 5):
                            if n < len(groups):
                                front(n)
                            if 1 <= n <= len(groups):
                                if n < len(groups) + 1:
                                    operand(n - 1)
                            if 2 <= n < len(groups) + 2:
                                post(n - 2)
                            if normed and 3 <= n < len(groups) + 3:
                                norm(n - 3)
                            if second and 5 <= n:
                                scalars(n - 5)
                    n_go = {"sage": 2, "skip": 6, "mean": 5, "att": 6, "last": 5, "gat": 1}[mode] * 2 * NG
                    n_go += 2 if loops else 0
                    if mode == "sage":
                        go(dve.memset(acc[:, :, :, :], 0.0))
                    walk(dve, body, go, n_go)
                    dve_s.total = go.total

            dve_s.base += dve_s.total
            for par, n in ((0, PAIRS + 1), (1, PAIRS)):
                ld[par].base += 16 * loads * n
                stq[par].base += 16 * stores * n
            if products:
                th_done.base += NGR
                ht_ready.base += NGR
                mm_done.base += NGR
                if mode != "sage":
                    post_read.base += NGR
            if loops:
                y_ready.base += NGR
            if two:
                tr_done.base += NGR
                rt_ready.base += NGR
            out_ready.base += NGR
            if second:
                for s in (t2_done, ot_ready, m2_done, m2_read):
                    s.base += NGR
            if mode == "sage":
                sq_ready.base += NGR
            if mode == "sage" or normed:
                norm_ready.base += NGR
            if normed:
                var_ready.base += NGR
                std_ready.base += NGR

        def batch_norm(layer):
            b, gamma, beta = (bn_par[:, k, layer:layer + 1] for k in range(3))
            with nc.Block() as block:
                @block.scalar
                def _(act):
                    act.wait_ge(d2a.h, d2a.at(1))
                    act.activation(sums[:, 4:5], sums[:, 2:3], ACT.Sqrt).then_inc(a2d.h, 1)

                @block.tensor
                def _(pe):
                    for s in range(2):
                        for k in range(GT):
                            mm = pe.matmul(ps[s][:, 0:1], acc[:, s, k, :], ones[:, 0:1], start=(k == 0),
                                           stop=(k == GT - 1))
                    mm.then_inc(p2d.h, 1)
                    pe.wait_ge(d2p.h, d2p.at(1))
                    pe.transpose(ps[2][:, 0:D], wq[:, :], ident[:, :])
                    pe.transpose(ps[2][:, D:2 * D], wqt[:, :], ident[:, :]).then_inc(p2d.h, 1)

                @block.vector
                def _(dve):
                    go = Chain(dve, dve_s)
                    mean, sq, var, full = (sums[:, k:k + 1] for k in range(4))
                    dve.wait_ge(p2d.h, p2d.at(1))
                    go(dve.tensor_scalar(mean, ps[0][:, 0:1], 1.0 / N, None, ALU.mult))
                    go(dve.tensor_scalar(sq, ps[1][:, 0:1], 1.0 / N, None, ALU.mult))
                    go(dve.tensor_tensor(var, mean, mean, ALU.mult))
                    go(dve.tensor_tensor(var, sq, var, ALU.subtract))
                    go(dve.tensor_scalar(var, var, 0.0, None, ALU.max))
                    go(dve.tensor_scalar(var, var, EPS, None, ALU.add))
                    dve.sem_inc(d2a.h, 1)
                    dve.wait_ge(a2d.h, a2d.at(1))
                    go(dve.reciprocal(var, sums[:, 4:5]))
                    go(dve.tensor_tensor(bn_col[:, 0:1], gamma, var, ALU.mult))
                    go(dve.tensor_tensor(full, mean, b, ALU.add))
                    go(dve.tensor_tensor(full, b, full, ALU.subtract))
                    go(dve.tensor_tensor(full, full, bn_col[:, 0:1], ALU.mult))
                    go(dve.tensor_tensor(bn_col[:, 1:2], full, beta, ALU.add))
                    go(dve.tensor_scalar(wq[:, :], ones[:, :], bn_col[:, 0:1], None, ALU.mult))
                    go(dve.tensor_scalar(wqt[:, :], ones[:, :], bn_col[:, 1:2], None, ALU.mult))
                    dve.sem_inc(d2p.h, 1)
                    dve.wait_ge(p2d.h, p2d.at(2))
                    go(dve.tensor_copy(bn_row[:, 0, :], ps[2][:, 0:D]))
                    go(dve.tensor_copy(bn_row[:, 1, :], ps[2][:, D:2 * D]))
                    dve_s.total = go.total
            dve_s.base += dve_s.total
            p2d.base += 2
            d2p.base += 1
            d2a.base += 1
            a2d.base += 1

        x = t["x"]
        edge_pass("mean", x)
        node_pass("sage", x, tab_a, layer=0)
        batch_norm(0)
        edge_pass("mean", tab_a, bn=True)
        node_pass("sage", tab_a, tab_b, bn=True, layer=1)
        batch_norm(1)
        edge_pass("mean", tab_b, bn=True)
        node_pass("sage", tab_b, tab_a, bn=True, layer=2)
        batch_norm(2)
        node_pass("skip", tab_a, tab_b, extra=x)
        edge_pass("mean", tab_b)
        node_pass("mean", tab_b, tab_a)
        edge_pass("att", tab_a)
        node_pass("att", tab_a, tab_b)
        edge_pass("gat", tab_b, layer=0)
        node_pass("gat", tab_b, tab_x0, layer=0)
        edge_pass("gat", tab_x0, layer=1)
        node_pass("gat", tab_x0, tab_a, layer=1)
        edge_pass("gat", tab_a, layer=2)
        node_pass("gat", tab_a, tab_u, extra=tab_x0, layer=2)
        edge_pass("gat", tab_u, layer=3)
        node_pass("gat", tab_u, tab_a, extra=tab_x0, layer=3)
        edge_pass("gat", tab_a, layer=4)
        node_pass("last", tab_a, out, extra=tab_b, layer=4)


_INS = ['x', 'src', 'dst', 'edge_attr_16', 'L0_gnn_Wl', 'L0_gnn_Wr', 'L0_gnn_b', 'L0_gnn_gamma', 'L0_gnn_beta',
        'L1_gnn_W_self', 'L1_gnn_b_self', 'L1_gnn_W_neigh', 'L1_gnn_b_neigh', 'L2_gnn_W_w', 'L2_gnn_W_b',
        'L2_gnn_WS_w', 'L2_gnn_WS_b', 'L2_gnn_q_w', 'L2_gnn_q_b', 'L2_gnn_k_w', 'L2_gnn_k_b', 'L3_gnn_Ws',
        'L3_gnn_Wes', 'L3_gnn_a_srcs', 'L3_gnn_a_dsts', 'L3_gnn_a_edges', 'L3_gnn_biases', 'L3_gnn_mid_ws']


def kernel(**inputs):
    import numpy as _np
    import concourse.bacc as _bacc
    from concourse import mybir as _mybir
    from concourse.bass_utils import run_bass_kernel_spmd as _run

    nc = _bacc.Bacc("TRN2", target_bir_lowering=False, num_devices=1)
    arrays, aps = {}, {}
    for name in _INS:
        a = _np.ascontiguousarray(inputs[name])
        arrays[f"in_{name}_dram"] = a
        aps[name] = nc.dram_tensor(f"in_{name}_dram", a.shape, _mybir.dt.from_np(a.dtype), kind="ExternalInput").ap()
    shape = tuple(inputs["x"].shape)
    out = nc.dram_tensor("out_0_dram", shape, _mybir.dt.float32, kind="ExternalOutput").ap()
    gnn(nc, aps, out)
    r = _run(nc, [arrays], core_ids=[0])
    return r.results[0]["out_0_dram"]
```

```python
import math
from contextlib import ExitStack
from typing import NamedTuple

import concourse.bass as bass
from concourse import mybir

F32 = mybir.dt.float32
I32 = mybir.dt.int32
ALU = mybir.AluOpType
ACT = mybir.ActivationFunctionType
AX = mybir.AxisListType.X

P = 128
D = 128
W = D + 2
ED = 16
CH = 8
G = 16
GT = 4
NG = G // GT
SUP = P * G
BIG = 1.0e30
EPS = 1e-5
LAYERS = 5
ALPHA, THETA = 0.2, 0.2
ATT_SLOPE, SLOPE = 0.2, 0.01


class Sem:

    def __init__(self, handle):
        self.h = handle
        self.base = 0

    def at(self, n):
        return self.base + n


class Group(NamedTuple):
    q: object
    it: object
    par: int
    g: int
    m: int
    parts: int
    past: int


class Chain:

    def __init__(self, eng, sem):
        self.eng, self.sem = eng, sem
        self.start, self.i, self.per, self.n, self.total = 0, None, 0, 0, 0

    def enter(self, i, per, turns):
        self.start, self.i, self.per, self.n = self.total, i, per, 0
        self.turns = turns

    def leave(self):
        if self.n != self.per:
            raise AssertionError(f"chain of {self.sem.h}: {self.n} steps in a turn, not {self.per}")
        self.total = self.start + self.turns * self.per
        self.i = None

    def __call__(self, ins):
        ins.then_inc(self.sem.h, 1)
        self.n += 1
        if self.i is None:
            self.total += 1
            self.eng.wait_ge(self.sem.h, self.sem.at(self.total))
        else:
            self.eng.wait_ge(self.sem.h, self.sem.at(self.start + self.i * self.per + self.n))


def gnn(nc, t, out):
    N = t["x"].shape[0]
    E = t["src"].shape[0]
    COLS = (E + P * CH - 1) // (P * CH) * CH
    NCH = COLS // CH
    assert NCH % 2 == 1 and NCH >= 3
    ROWS, REST = E // COLS, E % COLS
    LIVE = ROWS + (REST > 0)
    ST = N // SUP
    assert ST % 2 == 0 and ST >= 6
    LASTP = (N - ST * SUP) // G
    assert ST * SUP + LASTP * G == N and 0 < LASTP < P
    NGR = NG * (ST + 1)

    ctx = ExitStack()
    with ctx, nc.allow_non_contiguous_dma(reason="single columns of weights and of edge lists"):
        def sb(name, shape, dt=F32):
            return ctx.enter_context(nc.sbuf_tensor(name, shape, dt))

        def sem(name):
            return Sem(ctx.enter_context(nc.semaphore(name)))

        def table(name, w=W):
            return nc.dram_tensor(name, (N, w), F32, kind="Internal").ap()
        tab_a, tab_b, tab_x0, tab_u = table("tab_a"), table("tab_b"), table("tab_x0"), table("tab_u")
        pair_tab, agg = table("pair_tab", 2), table("agg_tab")

        src_i = sb("src_i", [P, COLS + 2 * CH], I32)
        dst_i = sb("dst_i", [P, COLS + 2 * CH], I32)
        scat_i = sb("scat_i", [P, COLS], I32)
        fix_i = sb("fix_i", [P, 1], I32)
        dstf = sb("dstf", [P, COLS])
        same = sb("same", [P, COLS])
        pen = sb("pen", [P, COLS])
        fixm = sb("fixm", [P, COLS])
        inv_cnt = sb("inv_cnt", [P, COLS])
        inv_cnt_fix = sb("inv_cnt_fix", [P, 1])
        edge_c = sb("edge_c", [P, LAYERS, COLS])
        loop_c = sb("loop_c", [P, LAYERS, COLS])
        loop_fix = sb("loop_fix", [P, LAYERS])
        chain_m = sb("chain_m", [P, P])
        chain_pen = sb("chain_pen", [P, P])
        ident = sb("ident", [P, P])
        ones = sb("ones", [P, P])
        zrow = sb("zrow", [P, COLS])

        sage_l = sb("sage_l", [P, 3, D])
        sage_r = sb("sage_r", [P, 3, D])
        mean_w = sb("mean_w", [P, 2, D])
        mean_b = sb("mean_b", [P, GT, D])
        mean_nb = sb("mean_nb", [P, GT, D])
        att_w = sb("att_w", [P, 2, D])
        att_b = sb("att_b", [P, GT, D])
        att_mb = sb("att_mb", [P, D])
        key_w = sb("key_w", [P, D + 1])
        key_b = sb("key_b", [P, D + 1])
        gat_w = sb("gat_w", [P, LAYERS, D])
        gat_b = sb("gat_b", [P, LAYERS, GT, D])
        gat_s = sb("gat_s", [P, LAYERS, 2])
        mid_w = sb("mid_w", [P, 3, D])
        bn_col = sb("bn_col", [P, 2])
        bn_row = sb("bn_row", [P, 2, D])
        bn_par = sb("bn_par", [P, 3, 3])

        gi = sb("gi", [P, 2, CH], I32)
        di = sb("di", [P, 2, CH], I32)
        wi = sb("wi", [P, 2, CH], I32)
        dpair = sb("dpair", [P, 2, CH, 2])
        wide = sb("wide", [P, CH, D])
        wide2 = sb("wide2", [P, CH, D])
        obuf = sb("obuf", [P, 2, CH, W])
        fixv = sb("fixv", [P, D])
        fixt = sb("fixt", [P, D])
        m_all = sb("m_all", [P, COLS + 1])
        den_all = sb("den_all", [P, COLS + 1])
        sl_all = sb("sl_all", [P, COLS])
        s8 = sb("s8", [P, CH])
        z8 = sb("z8", [P, CH])
        l8 = sb("l8", [P, CH])
        e4 = sb("e4", [P, 4 * CH])
        x4 = sb("x4", [P, 4 * CH])
        sc8 = sb("sc8", [P, 2, CH])
        fx = sb("fx", [P, 16])
        lrow = sb("lrow", [P, D + 1])
        wq = sb("wq", [P, P])
        wqt = sb("wqt", [P, P])
        fixo = sb("fixo", [P, W])

        node_in = sb("node_in", [P, 3, 2, G, W])
        in_h, in_r, in_e = (node_in[:, k] for k in range(3))
        node_out = sb("node_out", [P, 2, 2, G, W])
        outb, outu = node_out[:, 0], node_out[:, 1]
        outp = sb("outp", [P, 2, G, 2])
        yb = sb("yb", [P, 2, GT, D])
        ht = sb("ht", [P, 2, GT, D])
        rt = sb("rt", [P, 2, GT, D])
        ub = sb("ub", [P, 4, GT, D])
        xbuf = sb("xbuf", [P, 4, GT, D])
        ot = sb("ot", [P, 2, GT, D])
        st6 = sb("st6", [P, GT, 6])
        mv = sb("mv", [P, 4, GT, 2])
        std = sb("std", [P, 4, GT])
        col1 = sb("col1", [P, 2, G])
        acc = sb("acc", [P, 2, GT, D])
        sums = sb("sums", [P, 8])

        room = node_in[:, :, :, :, :].rearrange("p k a g w -> p (k a g w)")
        ea = room[:, 0:COLS * ED]
        at, lots = 0, []
        for w in (D, D, W, W):
            lots.append(room[:, at:at + 2 * CH * w].rearrange("p (a j w) -> p a j w", a=2, j=CH))
            at += 2 * CH * w
        state, rows_x, rows, drows = lots
        eat = node_out[:, :, :, :, :].rearrange("p k a g w -> p (k a g w)")
        assert COLS * ED <= 2 * 2 * G * W

        ps = [ctx.enter_context(nc.psum_tensor(f"ps{i}", [P, 512], F32)) for i in range(8)]

        dve_s, act_s, pool_s, pe_s = sem("dve_s"), sem("act_s"), sem("pool_s"), sem("pe_s")
        tick = sem("tick")
        d2p, p2d, d2a, a2d, p2a, a2p = (sem(n) for n in ("d2p", "p2d", "d2a", "a2d", "p2a", "a2p"))
        load = sem("load")
        gath = [sem("gath0"), sem("gath1")]
        gath_d = [sem("gath_d0"), sem("gath_d1")]
        scat = [sem("scat0"), sem("scat1")]
        scat_fix, zeroed = sem("scat_fix"), sem("zeroed")
        idx_ready, rows_used, ob_ready, exp_in, exp_out = (
            sem(n) for n in ("idx_ready", "rows_used", "ob_ready", "exp_in", "exp_out"))
        fix_ready = sem("fix_ready")
        ld = [sem("ld0"), sem("ld1")]
        stq = [sem("stq0"), sem("stq1")]
        y_ready, th_done, tr_done, ht_ready, rt_ready, mm_done, post_read, out_ready = (
            sem(n) for n in ("y_ready", "th_done", "tr_done", "ht_ready", "rt_ready", "mm_done", "post_read",
                             "out_ready"))
        t2_done, ot_ready, m2_done, m2_read, sq_ready, norm_ready = (
            sem(n) for n in ("t2_done", "ot_ready", "m2_done", "m2_read", "sq_ready", "norm_ready"))
        var_ready, std_ready = sem("var_ready"), sem("std_ready")
        pre_ready, sum_ready = sem("pre_ready"), sem("sum_ready")

        def bc(ap, n):
            return ap.unsqueeze(1).to_broadcast([P, n, ap.shape[-1]])

        def bl(ap, n=D):
            return ap.unsqueeze(2).to_broadcast([P, ap.shape[-1], n])

        NLOAD = [0]
        with nc.Block() as block:
            def edge_load(sp, dst_ap, dram, s, w=1):
                n = 0
                src_v = dram[0:ROWS * COLS] if w == 1 else dram[0:ROWS * COLS, :]
                pat = "(p j) -> p j" if w == 1 else "(p j) k -> p (j k)"
                sp.dma_start(dst_ap[0:ROWS, 0:COLS * w], src_v.rearrange(pat, p=ROWS)).then_inc(s.h, 16)
                n += 16
                if REST:
                    src_v = dram[ROWS * COLS:E] if w == 1 else dram[ROWS * COLS:E, :]
                    sp.dma_start(dst_ap[ROWS:ROWS + 1, 0:REST * w], src_v.rearrange(pat, p=1)).then_inc(s.h, 16)
                    n += 16
                return n

            dpad = wide[:, :, :].rearrange("p a b -> p (a b)").bitcast(I32)
            bnd = fx[:, 0:2].bitcast(I32)

            @block.sync
            def _(sp):
                sp.wait_ge(d2a.h, d2a.at(1))
                sp.wait_ge(pool_s.h, pool_s.at(1))
                n = edge_load(sp, src_i, t["src"], load)
                n += edge_load(sp, dst_i, t["dst"], load)
                n += edge_load(sp, dpad, t["dst"], load)
                n += edge_load(sp, ea, t["edge_attr_16"], load, ED)
                dd = t["dst"].rearrange("(e o) -> e o", o=1)
                sp.dma_start(bnd[1:LIVE, 0:1], dd[COLS - 1:COLS - 1 + (LIVE - 2) * COLS + 1:COLS, :]).then_inc(load.h, 16)
                sp.dma_start(bnd[0:LIVE - 1, 1:2], dd[COLS:COLS + (LIVE - 2) * COLS + 1:COLS, :]).then_inc(load.h, 16)
                n += 32
                for l in range(LAYERS):
                    sp.dma_start(eat[0:ED, l * D:(l + 1) * D], t["L3_gnn_Wes"][l]).then_inc(load.h, 16)
                    for k in range(ED):
                        sp.dma_start(eat[k:k + 1, (LAYERS + l) * D:(LAYERS + l + 1) * D],
                                     t["L3_gnn_a_edges"][l:l + 1, :]).then_inc(load.h, 16)
                    n += 16 + 16 * ED
                NLOAD[0] = n
                sp.wait_ge(load.h, load.at(n))
                sp.sem_inc(a2d.h, 1)

            @block.gpsimd
            def _(pool):
                pool.memset(ea[:, :], 0.0)
                pool.memset(ident[:, :], 0.0).then_inc(pool_s.h, 1)
                pool.wait_ge(pool_s.h, pool_s.at(1))
                pool.affine_select(out=ident[:, :], in_=ident[:, :], compare_op=ALU.not_equal, fill=1.0, base=0,
                                   pattern=[[-1, P]], channel_multiplier=1).then_inc(pool_s.h, 1)
                pool.wait_ge(d2p.h, d2p.at(2))
                pool.affine_select(out=chain_m[:, :], in_=chain_m[:, :], compare_op=ALU.is_gt, fill=0.0, base=0,
                                   pattern=[[1, P]], channel_multiplier=-1).then_inc(pool_s.h, 1)
                pool.affine_select(out=chain_pen[:, :], in_=chain_pen[:, :], compare_op=ALU.is_gt, fill=0.0, base=0,
                                   pattern=[[-1, P]], channel_multiplier=1).then_inc(pool_s.h, 1)

            @block.vector
            def _(dve):
                go = Chain(dve, dve_s)
                dve.memset(src_i[:, :], 0)
                dve.memset(dst_i[:, :], 0)
                dve.memset(dpad, N)
                dve.memset(bnd[:, 0:1], -1)
                dve.memset(bnd[:, 1:2], N + 1)
                dve.memset(ones[:, :], 1.0)
                dve.memset(zrow[:, :], 1.0)
                dve.memset(same[:, 0:1], 0.0)
                dve.memset(eat[:, :], 0.0)
                go(dve.memset(obuf[:, :, :, :], 0.0))
                dve.sem_inc(d2a.h, 1)
                dve.wait_ge(a2d.h, a2d.at(1))
                dve.tensor_copy(fx[:, 2:4], bnd[:, 0:2])
                go(dve.tensor_copy(dstf[:, :], dpad[:, 0:COLS]))
                dve.tensor_tensor(same[:, 1:COLS], dstf[:, 1:COLS], dstf[:, 0:COLS - 1], ALU.is_equal)
                dve.tensor_tensor(pen[:, 0:COLS - 1], dstf[:, 0:COLS - 1], dstf[:, 1:COLS], ALU.not_equal)
                dve.tensor_tensor(pen[:, COLS - 1:COLS], dstf[:, COLS - 1:COLS], fx[:, 3:4], ALU.not_equal)
                dve.tensor_tensor(fx[:, 4:5], dstf[:, 0:1], fx[:, 2:3], ALU.is_equal)
                go(dve.tensor_scalar(fixm[:, :], dstf[:, :], dstf[:, 0:1], None, ALU.is_equal))
                go(dve.scalar_tensor_tensor(fixm[:, :], fixm[:, :], fx[:, 4:5], pen[:, :], ALU.mult, ALU.mult))
                go(dve.tensor_tensor(m_all[:, 0:COLS], pen[:, :], fixm[:, :], ALU.subtract))
                go(dve.scalar_tensor_tensor(den_all[:, 0:COLS], dstf[:, :], float(-N), m_all[:, 0:COLS], ALU.add, ALU.mult))
                dve.tensor_scalar(scat_i[:, :], den_all[:, 0:COLS], float(N), None, ALU.add)
                dve.tensor_reduce(fx[:, 5:6], fixm[:, :], AX, ALU.max)
                go(dve.tensor_scalar(pen[:, :], same[:, :], -1.0, BIG, ALU.add, ALU.mult))
                go(dve.scalar_tensor_tensor(fx[:, 6:7], dstf[:, 0:1], float(-N), fx[:, 5:6], ALU.add, ALU.mult))
                dve.tensor_scalar(fix_i[:, :], fx[:, 6:7], float(N), None, ALU.add)
                go(dve.tensor_tensor_scan(sl_all[:, :], same[:, :], zrow[:, :], 0.0, ALU.mult, ALU.add))
                go(dve.tensor_scalar(inv_cnt[:, :], sl_all[:, :], 1.0, None, ALU.max))
                go(dve.reciprocal(inv_cnt[:, :], inv_cnt[:, :]))
                dve.tensor_tensor_reduce(m_all[:, 0:COLS], fixm[:, :], sl_all[:, :], 1.0, 0.0, ALU.mult, ALU.add,
                                         fx[:, 7:8])
                dve.tensor_scalar(wq[:, :], ones[:, :], dstf[:, 0:1], None, ALU.mult)
                go(dve.tensor_scalar(wqt[:, :], ones[:, :], dstf[:, COLS - 1:COLS], None, ALU.mult))
                for l in range(LAYERS):
                    go(dve.tensor_tensor_reduce(wide2[0:ED, 0, :], eat[0:ED, l * D:(l + 1) * D],
                                                eat[0:ED, (LAYERS + l) * D:(LAYERS + l + 1) * D], 1.0, 0.0,
                                                ALU.mult, ALU.add, e4[0:ED, l:l + 1]))
                dve.wait_ge(pool_s.h, pool_s.at(2))
                for l in range(LAYERS):
                    go(dve.tensor_scalar(lrow[0:ED, l * ED:(l + 1) * ED], ident[0:ED, 0:ED], e4[0:ED, l:l + 1], None,
                                         ALU.mult))
                dve.sem_inc(d2p.h, 1)
                dve.wait_ge(p2d.h, p2d.at(1))
                dve.tensor_scalar(chain_m[:, :], ps[0][:, 0:P], dstf[:, COLS - 1:COLS], None, ALU.is_equal)
                dve.tensor_scalar(chain_pen[:, :], ps[1][:, 0:P], dstf[:, 0:1], None, ALU.is_equal)
                go(dve.tensor_copy(wide2[:, 0, 0:LAYERS * ED], ps[2][:, 0:LAYERS * ED]))
                dve.sem_inc(d2p.h, 1)
                ea3 = ea[:, :].rearrange("p (j k) -> p j k", k=ED)
                eat3 = eat[:, 0:COLS * ED].rearrange("p (j k) -> p j k", k=ED)
                dve.tensor_copy(lrow[:, 0:1], sl_all[:, COLS - 1:COLS])
                for l in range(LAYERS):
                    v = wide2[:, 0, l * ED:(l + 1) * ED].unsqueeze(1).to_broadcast([P, COLS, ED])
                    go(dve.tensor_tensor(eat3, ea3, v, ALU.mult))
                    go(dve.tensor_reduce(edge_c[:, l, :], eat3, AX, ALU.add))
                    go(dve.tensor_tensor_scan(loop_c[:, l, :], same[:, :], edge_c[:, l, :], 0.0, ALU.mult, ALU.add))
                    dve.tensor_copy(lrow[:, 1 + l:2 + l], loop_c[:, l, COLS - 1:COLS])
                    go(dve.tensor_tensor_reduce(m_all[:, 0:COLS], fixm[:, :], loop_c[:, l, :], 1.0, 0.0, ALU.mult,
                                                ALU.add, loop_fix[:, l:l + 1]))
                    go(dve.tensor_tensor(loop_c[:, l, :], loop_c[:, l, :], inv_cnt[:, :], ALU.mult))
                dve.wait_ge(pool_s.h, pool_s.at(4))
                go(dve.tensor_scalar(chain_pen[:, :], chain_pen[:, :], -1.0, BIG, ALU.add, ALU.mult))
                dve.sem_inc(d2p.h, 1)
                dve.wait_ge(p2d.h, p2d.at(2))
                go(dve.tensor_tensor(inv_cnt_fix[:, :], ps[3][:, 0:1], fx[:, 7:8], ALU.add))
                go(dve.tensor_scalar(inv_cnt_fix[:, :], inv_cnt_fix[:, :], 1.0, None, ALU.max))
                go(dve.reciprocal(inv_cnt_fix[:, :], inv_cnt_fix[:, :]))
                go(dve.tensor_tensor(loop_fix[:, :], ps[3][:, 1:1 + LAYERS], loop_fix[:, :], ALU.add))
                go(dve.tensor_scalar(loop_fix[:, :], loop_fix[:, :], inv_cnt_fix[:, 0:1], None, ALU.mult))
                dve_s.total = go.total

            @block.tensor
            def _(pe):
                pe.wait_ge(d2p.h, d2p.at(1))
                pe.transpose(ps[0][:, 0:P], wq[:, :], ident[:, :])
                pe.transpose(ps[1][:, 0:P], wqt[:, :], ident[:, :])
                pe.matmul(ps[2][:, 0:LAYERS * ED], ones[0:ED, :], lrow[0:ED, 0:LAYERS * ED], start=True,
                          stop=True).then_inc(p2d.h, 1)
                pe.wait_ge(d2p.h, d2p.at(3))
                pe.matmul(ps[3][:, 0:1 + LAYERS], chain_m[:, :], lrow[:, 0:1 + LAYERS], start=True,
                          stop=True).then_inc(p2d.h, 1)
        dve_s.base += dve_s.total
        d2a.base += 1
        a2d.base += 1
        pool_s.base += 4
        d2p.base += 3
        p2d.base += 2
        load.base += NLOAD[0]

        raw = [in_h[:, 0, i, 0:D] for i in range(G)] + [in_h[:, 1, i, 0:D] for i in range(G)]
        mean_ws, mean_wn, att_ww, att_ws, kw, mids = raw[0], raw[1], raw[2], raw[3], raw[4], raw[5:8]
        qw = in_h[:, 0, 8, 0:D + 1]
        gat_raw_t = raw[16:16 + LAYERS]
        mbeta = raw[21:24]
        bcols = raw[24:28]
        vec = in_r[:, 0, 0, :]
        V_MS, V_MN, V_AW, V_AS, V_QB, V_KB, V_B, V_SRC, V_DST = 0, 1, 2, 3, 4, 5, 6, 11, 16
        blend = [math.log(THETA / (i + 1) + 1.0) for i in range(3)]
        with nc.Block() as block:
            @block.sync
            def _(sp):
                n = 0

                def get(dst_ap, src_ap):
                    sp.dma_start(dst_ap, src_ap).then_inc(load.h, 16)
                    return 16
                for l in range(3):
                    n += get(sage_l[:, l, :], t["L0_gnn_Wl"][l])
                    n += get(sage_r[:, l, :], t["L0_gnn_Wr"][l])
                    n += get(mids[l], t["L3_gnn_mid_ws"][l])
                for l in range(LAYERS):
                    n += get(gat_w[:, l, :], t["L3_gnn_Ws"][l])
                for a, b in ((mean_ws, "L1_gnn_W_self"), (mean_wn, "L1_gnn_W_neigh"), (att_ww, "L2_gnn_W_w"),
                             (att_ws, "L2_gnn_WS_w"), (kw, "L2_gnn_k_w")):
                    n += get(a, t[b])
                n += get(qw[:, 0:D], t["L2_gnn_q_w"])

                def col(dst_ap, v):
                    return get(dst_ap, v.rearrange("(p o) -> p o", o=1))
                n += col(vec[:, V_MS:V_MS + 1], t["L1_gnn_b_self"])
                n += col(vec[:, V_MN:V_MN + 1], t["L1_gnn_b_neigh"])
                n += col(vec[:, V_AW:V_AW + 1], t["L2_gnn_W_b"])
                n += col(vec[:, V_AS:V_AS + 1], t["L2_gnn_WS_b"])
                n += col(vec[:, V_KB:V_KB + 1], t["L2_gnn_k_b"])
                n += col(qw[:, D:D + 1], t["L2_gnn_q_b"])
                for l in range(LAYERS):
                    n += col(vec[:, V_B + l:V_B + l + 1], t["L3_gnn_biases"][l])
                    n += col(vec[:, V_SRC + 2 * l:V_SRC + 2 * l + 1], t["L3_gnn_a_srcs"][l])
                    n += col(vec[:, V_SRC + 2 * l + 1:V_SRC + 2 * l + 2], t["L3_gnn_a_dsts"][l])
                for l in range(3):
                    n += col(bn_par[:, 0, l:l + 1], t["L0_gnn_b"][l])
                    n += col(bn_par[:, 1, l:l + 1], t["L0_gnn_gamma"][l])
                    n += col(bn_par[:, 2, l:l + 1], t["L0_gnn_beta"][l])
                NLOAD[0] = n
                sp.wait_ge(load.h, load.at(n))
                sp.sem_inc(a2d.h, 1)
                sp.wait_ge(d2a.h, d2a.at(1))
                zeros = outb[:, 0, :, :].rearrange("p g w -> p (g w)")
                for s in range(ST):
                    sp.dma_start(agg[s * SUP:(s + 1) * SUP, :].rearrange("(p g) w -> p (g w)", p=P),
                                 zeros).then_inc(zeroed.h, 16)
                sp.dma_start(agg[ST * SUP:N, :].rearrange("(p g) w -> p (g w)", p=LASTP),
                             zeros[0:LASTP, :]).then_inc(zeroed.h, 16)

            @block.vector
            def _(dve):
                go = Chain(dve, dve_s)
                dve.memset(outu[:, :, :, :], 0.0)
                go(dve.memset(outb[:, :, :, :], 0.0))
                dve.sem_inc(d2a.h, 1)
                dve.wait_ge(a2d.h, a2d.at(1))
                for l in range(3):
                    go(dve.tensor_scalar(mbeta[l], ident[:, :], 1.0 - blend[l], None, ALU.mult))
                    go(dve.scalar_tensor_tensor(mbeta[l], mids[l], blend[l], mbeta[l], ALU.mult, ALU.add))
                    go(dve.tensor_scalar(mid_w[:, l, :], mbeta[l], ALPHA, None, ALU.mult))
                go(dve.tensor_tensor(vec[:, V_MS:V_MS + 1], vec[:, V_MS:V_MS + 1], vec[:, V_MN:V_MN + 1], ALU.add))
                go(dve.tensor_scalar(bcols[0], ones[:, :], vec[:, V_MS:V_MS + 1], None, ALU.mult))
                go(dve.tensor_scalar(bcols[1], ones[:, :], vec[:, V_AS:V_AS + 1], None, ALU.mult))
                go(dve.tensor_scalar(bcols[2], ones[:, :], vec[:, V_AW:V_AW + 1], None, ALU.mult))
                go(dve.tensor_scalar(bcols[3], ones[:, :], vec[:, V_KB:V_KB + 1], None, ALU.mult))
                dve.sem_inc(d2p.h, 1)
                dve.wait_ge(p2d.h, p2d.at(1))
                dve.tensor_copy(mean_w[:, 0, :], ps[0][:, 0:D])
                dve.tensor_copy(mean_w[:, 1, :], ps[0][:, D:2 * D])
                dve.tensor_copy(att_w[:, 0, :], ps[0][:, 2 * D:3 * D])
                dve.tensor_copy(att_w[:, 1, :], ps[0][:, 3 * D:4 * D])
                for g in range(GT):
                    dve.tensor_copy(mean_b[:, g, :], ps[1][:, 0:D])
                    dve.tensor_scalar(mean_nb[:, g, :], ps[1][:, 0:D], -1.0, None, ALU.mult)
                    dve.tensor_copy(att_b[:, g, :], ps[1][:, D:2 * D])
                dve.tensor_copy(att_mb[:, :], ps[1][:, 2 * D:3 * D])
                dve.tensor_scalar(key_w[:, :], ps[2][:, 0:D + 1], float(D) ** -0.5, None, ALU.mult)
                dve.tensor_scalar(key_b[:, :], ps[2][:, 256:256 + D + 1], float(D) ** -0.5, None, ALU.mult)
                for l in range(LAYERS):
                    go(dve.tensor_copy(gat_raw_t[l], ps[3 + l // 4][:, (l % 4) * D:(l % 4 + 1) * D]))
                for l in range(LAYERS):
                    go(dve.tensor_scalar(yb[:, l // 4, l % 4, :], ones[:, :], vec[:, V_B + l:V_B + l + 1], None, ALU.mult))
                dve.sem_inc(d2p.h, 1)
                dve.wait_ge(p2d.h, p2d.at(2))
                for l in range(LAYERS):
                    dve.tensor_copy(gat_s[:, l, :], ps[5][:, 2 * l:2 * l + 2])
                    scale = 1.0 - ALPHA if 1 <= l <= 3 else 1.0
                    for g in range(GT):
                        dve.tensor_scalar(gat_b[:, l, g, :], ps[6 + l // 4][:, (l % 4) * D:(l % 4 + 1) * D], scale,
                                          None, ALU.mult)
                for l in range(3):
                    go(dve.tensor_scalar(gat_w[:, l + 1, :], ps[0][:, l * D:(l + 1) * D], 1.0 - ALPHA, None, ALU.mult))
                dve_s.total = go.total

            @block.tensor
            def _(pe):
                pe.wait_ge(d2p.h, d2p.at(1))
                for k, w in enumerate((mean_ws, mean_wn, att_ws, att_ww)):
                    pe.transpose(ps[0][:, k * D:(k + 1) * D], w, ident[:, :])
                for k in range(3):
                    pe.matmul(ps[1][:, k * D:(k + 1) * D], bcols[k], ident[:, :], start=True, stop=True)
                pe.matmul(ps[2][:, 0:D + 1], kw, qw, start=True, stop=True)
                pe.matmul(ps[2][:, 256:256 + D + 1], bcols[3], qw, start=True, stop=True)
                for l in range(LAYERS):
                    mm = pe.transpose(ps[3 + l // 4][:, (l % 4) * D:(l % 4 + 1) * D], gat_w[:, l, :], ident[:, :])
                mm.then_inc(p2d.h, 1)
                pe.wait_ge(d2p.h, d2p.at(2))
                for l in range(3):
                    pe.matmul(ps[0][:, l * D:(l + 1) * D], gat_raw_t[l + 1], mbeta[l], start=True, stop=True)
                for l in range(LAYERS):
                    pe.matmul(ps[5][:, 2 * l:2 * l + 2], gat_raw_t[l], vec[:, V_SRC + 2 * l:V_SRC + 2 * l + 2],
                              start=True, stop=True)
                    mm = pe.matmul(ps[6 + l // 4][:, (l % 4) * D:(l % 4 + 1) * D], yb[:, l // 4, l % 4, :],
                                   mbeta[l - 1] if 1 <= l <= 3 else ident[:, :], start=True, stop=True)
                mm.then_inc(p2d.h, 1)
        dve_s.base += dve_s.total
        d2a.base += 1
        a2d.base += 1
        d2p.base += 2
        p2d.base += 2
        load.base += NLOAD[0]

        def edge_pass(mode, tab, bn=False, layer=0):
            wide_tab = tab.shape[1] == W
            buf = rows if wide_tab else rows_x
            flash = mode != "mean"
            PER = {"mean": 18 + 6 * bn, "att": 26, "gat": 36}[mode]

            with nc.Block() as block:
                @block.gpsimd
                def _(pool):
                    def ticked(s, n):
                        pool.wait_ge(s.h, s.at(n))
                        pool.sem_inc(tick.h, 1)

                    def gathers(par):
                        for j in range(CH):
                            pool.indirect_dma_start(
                                out=buf[:, par, j, :], out_offset=None, in_=tab[:, :],
                                in_offset=bass.IndirectOffsetOnAxis(ap=gi[:, par, j:j + 1], axis=0)
                            ).then_inc(gath[par].h, 16)
                            if flash:
                                dtab = tab_u if mode == "att" else pair_tab
                                dbuf = drows if mode == "att" else dpair
                                pool.indirect_dma_start(
                                    out=dbuf[:, par, j, :], out_offset=None, in_=dtab[:, :],
                                    in_offset=bass.IndirectOffsetOnAxis(ap=di[:, par, j:j + 1], axis=0)
                                ).then_inc(gath_d[par].h, 16)

                    def scatters(k, par):
                        ticked(ob_ready, k + 1)
                        for j in range(CH):
                            pool.indirect_dma_start(
                                out=agg[:, :], out_offset=bass.IndirectOffsetOnAxis(ap=wi[:, par, j:j + 1], axis=0),
                                in_=obuf[:, par, j, :], in_offset=None, bounds_check=N - 1, oob_is_err=False
                            ).then_inc(scat[par].h, 16)

                    def step(k, par, first=False):
                        ticked(idx_ready, k + 2)
                        if not first:
                            ticked(rows_used, k)
                        gathers(1 - par)
                        scatters(k, par)

                    ticked(idx_ready, 1)
                    gathers(0)
                    pool.wait_ge(zeroed.h, 16 * (ST + 1))
                    step(0, 0, True)
                    step(1, 1)
                    with pool.Fori(1, (NCH - 1) // 2) as i:
                        step(2 * i, 0)
                        step(2 * i + 1, 1)
                    scatters(NCH - 1, 0)
                    ticked(fix_ready, 1)
                    pool.indirect_dma_start(
                        out=agg[:, :], out_offset=bass.IndirectOffsetOnAxis(ap=fix_i[:, 0:1], axis=0),
                        in_=fixo[:, :], in_offset=None, bounds_check=N - 1, oob_is_err=False).then_inc(scat_fix.h, 16)
                    pool.wait_ge(scat_fix.h, scat_fix.at(16))
                    pool.wait_ge(scat[0].h, scat[0].at(16 * CH * ((NCH + 1) // 2)))
                    pool.wait_ge(scat[1].h, scat[1].at(16 * CH * ((NCH - 1) // 2)))

                @block.vector
                def _(dve):
                    go = Chain(dve, dve_s)

                    def copy_at(dst_ap, src_ap):
                        dve.sem_inc(tick.h, 1)
                        return dve.tensor_copy(dst_ap, src_ap)

                    def stage(k, par):
                        if flash:
                            copy_at(di[:, par, :], dst_i[:, bass.ds(k * CH, CH)])
                        copy_at(gi[:, par, :], src_i[:, bass.ds(k * CH, CH)]).then_inc(idx_ready.h, 1)

                    def chunk(k, par, it, first=False):
                        c = bass.ds(k * CH, CH)
                        c1 = bass.ds(k * CH + 1, CH)
                        now = bass.ds(k * CH, 1)
                        g = buf[:, par, :, 0:D]
                        dve.wait_ge(gath[par].h, gath[par].at(16 * CH * (it + 1)))
                        if flash:
                            dve.wait_ge(gath_d[par].h, gath_d[par].at(16 * CH * (it + 1)))
                        stage(k + 2, par)
                        if mode == "mean":
                            if bn:
                                go(dve.tensor_tensor(wide[:, :, :], g, bc(bn_row[:, 0, :], CH), ALU.mult))
                                go(dve.tensor_tensor(wide[:, :, :], wide[:, :, :], bc(bn_row[:, 1, :], CH), ALU.add))
                                go(dve.tensor_scalar(wide[:, :, :], wide[:, :, :], 0.0, None, ALU.max))
                                terms = wide
                            else:
                                terms = buf[:, par]
                            copy_at(sc8[:, 0, :], inv_cnt[:, c])
                            go(copy_at(x4[:, 0:CH], same[:, c]))
                        else:
                            if mode == "gat":
                                go(dve.tensor_tensor(z8[:, :], buf[:, par, :, D], dpair[:, par, :, 1], ALU.add))
                                dve.tensor_tensor(sl_all[:, c], dpair[:, par, :, 0], dpair[:, par, :, 1], ALU.add)
                                go(dve.tensor_tensor(z8[:, :], z8[:, :], edge_c[:, layer, c], ALU.add))
                                go(dve.tensor_tensor(l8[:, :], sl_all[:, c], loop_c[:, layer, c], ALU.add))
                                go(dve.scalar_tensor_tensor(s8[:, :], z8[:, :], ATT_SLOPE, z8[:, :], ALU.mult, ALU.max))
                                go(dve.scalar_tensor_tensor(l8[:, :], l8[:, :], ATT_SLOPE, l8[:, :], ALU.mult, ALU.max))
                            else:
                                go(dve.tensor_tensor(wide[:, :, :], g, drows[:, par, :, 0:D], ALU.mult))
                                go(dve.tensor_reduce(z8[:, :], wide[:, :, :], AX, ALU.add))
                                go(dve.tensor_tensor(s8[:, :], z8[:, :], drows[:, par, :, D], ALU.add))
                            go(dve.tensor_tensor_scan(m_all[:, c1], pen[:, c], s8[:, :], m_all[:, now], ALU.add, ALU.max))
                            go(dve.tensor_tensor(z8[:, :], m_all[:, c], pen[:, c], ALU.add))
                            dve.tensor_tensor(e4[:, 0:CH], z8[:, :], m_all[:, c1], ALU.subtract)
                            go(dve.tensor_tensor(e4[:, CH:2 * CH], s8[:, :], m_all[:, c1], ALU.subtract))
                            ne = 2
                            if mode == "gat":
                                ne = 4
                                go(dve.tensor_tensor(z8[:, :], m_all[:, c1], l8[:, :], ALU.max))
                                dve.tensor_tensor(e4[:, 2 * CH:3 * CH], m_all[:, c1], z8[:, :], ALU.subtract)
                                go(dve.tensor_tensor(e4[:, 3 * CH:4 * CH], l8[:, :], z8[:, :], ALU.subtract))
                            dve.sem_inc(exp_in.h, 1)
                            dve.wait_ge(exp_out.h, exp_out.at(k + 1))
                            go(dve.tensor_tensor_scan(den_all[:, c1], x4[:, 0:CH], x4[:, CH:2 * CH], den_all[:, now],
                                                      ALU.mult, ALU.add))
                            if mode == "gat":
                                go(dve.tensor_tensor(z8[:, :], den_all[:, c1], x4[:, 2 * CH:3 * CH], ALU.mult))
                                go(dve.tensor_tensor(z8[:, :], z8[:, :], x4[:, 3 * CH:4 * CH], ALU.add))
                                go(dve.reciprocal(z8[:, :], z8[:, :]))
                                dve.tensor_tensor(sc8[:, 0, :], z8[:, :], x4[:, 2 * CH:3 * CH], ALU.mult)
                                go(dve.tensor_tensor(l8[:, :], z8[:, :], x4[:, 3 * CH:4 * CH], ALU.mult))
                                go(dve.tensor_scalar(sc8[:, 1, :], l8[:, :], -1.0, None, ALU.add))
                            else:
                                go(copy_at(z8[:, :], den_all[:, c1]))
                                go(dve.reciprocal(sc8[:, 0, :], z8[:, :]))
                            go(dve.tensor_tensor(wide[:, :, :], g, bl(x4[:, CH:2 * CH]), ALU.mult))
                            terms = wide
                        for j in range(CH):
                            before = state[:, par, j - 1, :] if j else state[:, 1 - par, CH - 1, :]
                            go(dve.scalar_tensor_tensor(state[:, par, j, :], before, x4[:, j:j + 1],
                                                        terms[:, j, 0:D], ALU.mult, ALU.add))
                        dve.sem_inc(rows_used.h, 1)
                        if not first:
                            dve.wait_ge(scat[par].h, scat[par].at(16 * CH * it))
                        copy_at(wi[:, par, :], scat_i[:, c])
                        if flash:
                            dve.tensor_copy(obuf[:, par, :, D], sc8[:, 1, :] if mode == "gat" else ones[:, 0:CH])
                        go(dve.tensor_tensor(obuf[:, par, :, 0:D], state[:, par, :, :], bl(sc8[:, 0, :]), ALU.mult))
                        dve.sem_inc(ob_ready.h, 1)
                        go(copy_at(z8[:, :], fixm[:, c]))
                        go(dve.tensor_tensor(wide2[:, :, :], state[:, par, :, :], bl(z8[:, :]), ALU.mult))
                        go(dve.tensor_reduce(fixt[:, :], wide2[:, :, :].rearrange("p j d -> p d j"), AX, ALU.add))
                        go(dve.tensor_tensor(fixv[:, :], fixv[:, :], fixt[:, :], ALU.add))

                    go(dve.memset(state[:, :, :, :], 0.0))
                    go(dve.memset(fixv[:, :], 0.0))
                    dve.memset(m_all[:, 0:1], -BIG)
                    go(dve.memset(den_all[:, 0:1], 0.0))
                    stage(0, 0)
                    stage(1, 1)
                    chunk(0, 0, 0, True)
                    chunk(1, 1, 0, True)
                    turns = (NCH - 1) // 2 - 1
                    with dve.Fori(1, (NCH - 1) // 2) as i:
                        go.enter(i - 1, PER_TURN[mode, bn], turns)
                        chunk(2 * i, 0, i)
                        chunk(2 * i + 1, 1, i)
                        go.leave()
                    chunk(NCH - 1, 0, (NCH - 1) // 2)

                    last = state[:, 0, CH - 1, :]
                    go(dve.tensor_copy(lrow[:, 0:D], last))
                    go(dve.memset(fixo[:, :], 0.0))
                    if not flash:
                        dve.sem_inc(d2p.h, 1)
                        dve.wait_ge(p2d.h, p2d.at(1))
                        go(dve.tensor_tensor(fixt[:, :], ps[0][:, 0:D], fixv[:, :], ALU.add))
                        go(dve.tensor_scalar(fixo[:, 0:D], fixt[:, :], inv_cnt_fix[:, 0:1], None, ALU.mult))
                    else:
                        go(dve.tensor_copy(lrow[:, D:D + 1], den_all[:, COLS:COLS + 1]))
                        go(dve.tensor_scalar(wq[:, :], ones[:, :], m_all[:, COLS:COLS + 1], None, ALU.mult))
                        dve.sem_inc(d2p.h, 1)
                        for k, a in ((0, m_all[:, 1:COLS + 1]), (1, den_all[:, 1:COLS + 1]), (2, sl_all[:, :])):
                            if k < 2 or mode == "gat":
                                go(dve.tensor_tensor_reduce(zrow[:, :], fixm[:, :], a, 1.0, 0.0, ALU.mult, ALU.add,
                                                            fx[:, k:k + 1]))
                        dve.wait_ge(p2d.h, p2d.at(1))
                        go(dve.tensor_tensor(wq[:, :], ps[0][:, 0:P], chain_pen[:, :], ALU.add))
                        go(dve.tensor_reduce(fx[:, 3:4], wq[:, :], AX, ALU.max))
                        go(dve.tensor_tensor(fx[:, 3:4], fx[:, 3:4], fx[:, 0:1], ALU.max))
                        if mode == "gat":
                            go(dve.tensor_tensor(fx[:, 2:3], fx[:, 2:3], loop_fix[:, layer:layer + 1], ALU.add))
                            go(dve.scalar_tensor_tensor(fx[:, 2:3], fx[:, 2:3], ATT_SLOPE, fx[:, 2:3], ALU.mult,
                                                        ALU.max))
                            go(dve.tensor_tensor(fx[:, 3:4], fx[:, 3:4], fx[:, 2:3], ALU.max))
                            go(dve.tensor_tensor(fx[:, 5:6], fx[:, 2:3], fx[:, 3:4], ALU.subtract))
                        else:
                            go(dve.memset(fx[:, 5:6], -BIG))
                        go(dve.tensor_scalar(wq[:, :], wq[:, :], fx[:, 3:4], None, ALU.subtract))
                        go(dve.tensor_tensor(fx[:, 4:5], fx[:, 0:1], fx[:, 3:4], ALU.subtract))
                        dve.sem_inc(exp_in.h, 1)
                        dve.wait_ge(p2d.h, p2d.at(2))
                        go(dve.tensor_copy(wqt[:, :], ps[1][:, 0:P]))
                        dve.sem_inc(d2p.h, 1)
                        dve.wait_ge(p2d.h, p2d.at(3))
                        go(dve.tensor_scalar(fx[:, 8:9], fx[:, 1:2], fx[:, 6:7], None, ALU.mult))
                        go(dve.tensor_tensor(fx[:, 8:9], ps[0][:, D:D + 1], fx[:, 8:9], ALU.add))
                        go(dve.tensor_tensor(fx[:, 8:9], fx[:, 8:9], fx[:, 7:8], ALU.add))
                        go(dve.tensor_scalar(fx[:, 8:9], fx[:, 8:9], 1.0e-30, None, ALU.max))
                        go(dve.reciprocal(fx[:, 9:10], fx[:, 8:9]))
                        go(dve.scalar_tensor_tensor(fixt[:, :], fixv[:, :], fx[:, 6:7], ps[0][:, 0:D], ALU.mult, ALU.add))
                        go(dve.tensor_scalar(fixo[:, 0:D], fixt[:, :], fx[:, 9:10], None, ALU.mult))
                        if mode == "gat":
                            go(dve.tensor_tensor(fx[:, 10:11], fx[:, 7:8], fx[:, 9:10], ALU.mult))
                            go(dve.tensor_scalar(fixo[:, D:D + 1], fx[:, 10:11], -1.0, None, ALU.add))
                        else:
                            go(dve.memset(fixo[:, D:D + 1], 1.0))
                    dve.sem_inc(fix_ready.h, 1)
                    dve_s.total = go.total

                if flash:
                    @block.scalar
                    def _(act):
                        n = (4 if mode == "gat" else 2) * CH

                        def exps(k):
                            act.wait_ge(exp_in.h, exp_in.at(k + 1))
                            act.activation(x4[:, 0:n], e4[:, 0:n], ACT.Exp).then_inc(exp_out.h, 1)
                        with act.Fori(0, NCH) as k:
                            exps(k)
                        act.wait_ge(exp_in.h, exp_in.at(NCH + 1))
                        act.activation(wqt[:, :], wq[:, :], ACT.Exp)
                        act.activation(fx[:, 6:8], fx[:, 4:6], ACT.Exp).then_inc(exp_out.h, 1)
                        act.wait_ge(exp_out.h, exp_out.at(NCH + 1))
                        act.sem_inc(a2p.h, 1)

                @block.tensor
                def _(pe):
                    if not flash:
                        pe.wait_ge(d2p.h, d2p.at(1))
                        pe.matmul(ps[0][:, 0:D], chain_m[:, :], lrow[:, 0:D], start=True, stop=True).then_inc(p2d.h, 1)
                    else:
                        pe.wait_ge(d2p.h, d2p.at(1))
                        pe.transpose(ps[0][:, 0:P], wq[:, :], ident[:, :]).then_inc(p2d.h, 1)
                        pe.wait_ge(a2p.h, a2p.at(1))
                        pe.transpose(ps[1][:, 0:P], wqt[:, :], ident[:, :]).then_inc(p2d.h, 1)
                        pe.wait_ge(d2p.h, d2p.at(2))
                        pe.matmul(ps[0][:, 0:D + 1], wqt[:, :], lrow[:, :], start=True, stop=True).then_inc(p2d.h, 1)

            dve_s.base += dve_s.total
            idx_ready.base += NCH + 2
            rows_used.base += NCH
            ob_ready.base += NCH
            fix_ready.base += 1
            scat_fix.base += 16
            for par, n in ((0, (NCH + 1) // 2), (1, (NCH - 1) // 2)):
                gath[par].base += 16 * CH * n
                scat[par].base += 16 * CH * n
                if flash:
                    gath_d[par].base += 16 * CH * n
            if flash:
                exp_in.base += NCH + 1
                exp_out.base += NCH + 1
                a2p.base += 1
                d2p.base += 2
                p2d.base += 3
            else:
                d2p.base += 1
                p2d.base += 1

        PER_TURN = {("mean", False): 2 * (1 + CH + 1 + 4), ("mean", True): 2 * (4 + CH + 1 + 4),
                    ("att", False): 2 * (3 + 3 + 4 + CH + 1 + 4), ("gat", False): 2 * (5 + 3 + 2 + 7 + CH + 1 + 4)}

        def node_pass(mode, h_tab, out_tab, extra=None, bn=False, layer=0):
            has_agg = products = mode != "skip"
            mid = mode == "gat" and 1 <= layer <= 3
            loops = mode in ("gat", "last")
            two = mode in ("sage", "mean", "att") or mid
            normed = mode in ("skip", "mean", "att", "last")
            second = {"mean": "keys", "att": "scal", "gat": "scal"}.get(mode)
            loads = 1 + has_agg + (extra is not None)
            stores = 1 + (second is not None)
            o_w = out_tab.shape[1]
            same_x0 = mid and layer == 1
            score_l = 0 if mode == "att" else layer + 1
            if mode == "sage":
                w1, w2 = sage_r[:, layer, :], sage_l[:, layer, :]
            elif mode == "mean":
                w1, w2 = mean_w[:, 0, :], mean_w[:, 1, :]
            elif mode == "att":
                w1, w2 = att_w[:, 0, :], att_w[:, 1, :]
            elif loops:
                w1 = gat_w[:, layer, :]
                w2 = mid_w[:, layer - 1, :] if mid else None
            bias = gat_b[:, layer] if loops else None
            B = 1 if loops else 0
            R = 6 if normed else 3 + B
            DEPTH = {"sage": 3, "skip": 5, "mean": R + 2, "att": R + 2, "gat": R + 2, "last": 5 + B}[mode]
            assert DEPTH <= 2 * NG
            turn_banks = [2] if second == "keys" else [2, 7]
            NTB = len(turn_banks)
            readers = {"sage": (th_done, tr_done), "skip": (pre_ready, var_ready), "mean": (th_done, tr_done, pre_ready),
                       "att": (th_done, tr_done, pre_ready), "last": (y_ready, pre_ready),
                       "gat": (y_ready, tr_done) if mid else (y_ready,)}[mode]
            finished = m2_read if second else out_ready
            SLAG = 2 if mode == "sage" else 3
            FULL = ST // 2

            def tiles(buf, u):
                return buf[:, u.par, u.g * GT:(u.g + 1) * GT, 0:D]

            def rows_of(tab, s, parts):
                return tab[bass.ds(s * SUP, parts * G), :].rearrange("(p g) w -> p g w", p=parts)

            def group(it, n, lag):
                m = n - lag
                if isinstance(it, int):
                    q = 2 * NG * it + m
                    if not 0 <= q < NGR:
                        return None
                    it, m = q // (2 * NG), q % (2 * NG)
                    return Group(q, it, m // NG, m % NG, m, LASTP if q >= NG * ST else P, q)
                back = m < 0
                return Group(it * (2 * NG) + m, it - 1 if back else it, m % (2 * NG) // NG, m % NG, m % (2 * NG), P,
                             4 * NG)

            def walk(eng, slot, depth, chain=None, per=0):
                for n in range(4 * NG):
                    slot(0, n)
                with eng.Fori(2, FULL) as i:
                    if chain is not None:
                        chain.enter(i - 2, per, FULL - 2)
                    for n in range(2 * NG):
                        slot(i, n)
                    if chain is not None:
                        chain.leave()
                for n in range(NG + depth):
                    slot(FULL, n)

            with nc.Block() as block:
                @block.sync
                def _(sp):
                    def fetch(s, par, it, parts, waits):
                        if waits:
                            for r in readers:
                                sp.wait_ge(r.h, r.at(NG * (s - 1)))
                                sp.sem_inc(tick.h, 1)
                        for tab, b in ((h_tab, in_h), (agg if has_agg else None, in_r), (extra, in_e)):
                            if tab is not None:
                                sp.dma_start(b[0:parts, par, :, 0:tab.shape[1]], rows_of(tab, s, parts))\
                                  .then_inc(ld[par].h, 16)

                    def put(s, par, parts):
                        sp.wait_ge(finished.h, finished.at(NG * (s + 1)))
                        sp.sem_inc(tick.h, 1)
                        sp.dma_start(rows_of(out_tab, s, parts), outb[0:parts, par, :, 0:o_w]).then_inc(stq[par].h, 16)
                        if second == "keys":
                            sp.dma_start(rows_of(tab_u, s, parts), outu[0:parts, par, :, :]).then_inc(stq[par].h, 16)
                        if second == "scal":
                            sp.dma_start(rows_of(pair_tab, s, parts), outp[0:parts, par, :, :]).then_inc(stq[par].h, 16)

                    for s in range(4):
                        fetch(s, s % 2, s // 2, P, s >= 2)
                        if s >= SLAG:
                            put(s - SLAG, (s - SLAG) % 2, P)
                    with sp.Fori(2, FULL) as i:
                        for par in range(2):
                            fetch(2 * i + par, par, i, P, True)
                            put(2 * i + (par - SLAG), (par - SLAG) % 2, P)
                    fetch(ST, 0, FULL, LASTP, True)
                    for s in range(ST - SLAG, ST + 1):
                        put(s, s % 2, LASTP if s == ST else P)
                    sp.wait_ge(stq[0].h, stq[0].at(16 * stores * (FULL + 1)))
                    sp.wait_ge(stq[1].h, stq[1].at(16 * stores * FULL))

                @block.gpsimd
                def _(pool):
                    go = Chain(pool, pool_s)

                    def pre(u):
                        xb = xbuf[:, u.m % 4]
                        pool.wait_ge(ld[u.par].h, ld[u.par].at(16 * loads * (u.it + 1)))
                        if u.past >= 4:
                            pool.wait_ge(var_ready.h, var_ready.at(u.q - 3))
                        if mode == "skip":
                            go(pool.tensor_tensor(xb, tiles(in_h, u), bc(bn_row[:, 0, :], GT), ALU.mult))
                            pool.tensor_tensor(xb, xb, bc(bn_row[:, 1, :], GT), ALU.add).then_inc(pre_ready.h, 1)
                        if mode == "mean":
                            pool.tensor_tensor(xb, tiles(in_h, u), mean_b[:, :, :], ALU.add).then_inc(pre_ready.h, 1)
                        if mode == "att":
                            col = in_r[:, u.par, u.g * GT:(u.g + 1) * GT, D]
                            go(pool.tensor_tensor(xb, bc(att_mb[:, :], GT), bl(col), ALU.mult))
                            go(pool.tensor_tensor(xb, xb, tiles(in_h, u), ALU.add))
                            pool.tensor_tensor(xb, xb, att_b[:, :, :], ALU.add).then_inc(pre_ready.h, 1)
                        if mode == "last":
                            pool.tensor_tensor(xb, tiles(in_e, u), bias, ALU.add).then_inc(pre_ready.h, 1)

                    def total(u):
                        pool.wait_ge(out_ready.h, out_ready.at(u.q + 1))
                        go(pool.tensor_tensor(acc[0:u.parts, 0], tiles(outb, u)[0:u.parts], acc[0:u.parts, 0], ALU.add))
                        pool.sem_inc(sum_ready.h, 1)

                    def slot(it, n):
                        if normed and (u := group(it, n, 0)):
                            pre(u)
                        if mode == "sage" and (u := group(it, n, 3)):
                            total(u)
                    per = 2 * NG * {"skip": 1, "att": 2, "sage": 1}.get(mode, 0)
                    if mode == "sage":
                        go(pool.memset(acc[:, 0], 0.0))
                    if mode != "gat":
                        walk(pool, slot, DEPTH, go, per)
                    pool_s.total = go.total

                @block.tensor
                def _(pe):
                    def turn(u):
                        if u.g == 0:
                            pe.wait_ge(ld[u.par].h, ld[u.par].at(16 * loads * (u.it + 1)))
                        if loops:
                            pe.wait_ge(y_ready.h, y_ready.at(u.q + 1))
                        if u.past >= 2:
                            pe.wait_ge(ht_ready.h, ht_ready.at(u.q - 1))
                        for k in range(GT):
                            a = yb[:, u.m % 2, k, :] if loops else in_h[:, u.par, u.g * GT + k, 0:D]
                            mm = pe.transpose(ps[u.m % 2][:, k * D:(k + 1) * D], a, ident[:, :])
                        mm.then_inc(th_done.h, 1)
                        if two:
                            if u.past >= NTB:
                                pe.wait_ge(rt_ready.h, rt_ready.at(u.q + 1 - NTB))
                            b = in_r if not mid else (in_h if same_x0 else in_e)
                            o = ps[turn_banks[u.m % NTB]]
                            for k in range(GT):
                                mm = pe.transpose(o[:, k * D:(k + 1) * D], b[:, u.par, u.g * GT + k, 0:D], ident[:, :])
                            mm.then_inc(tr_done.h, 1)

                    def product(u):
                        pe.wait_ge(ht_ready.h, ht_ready.at(u.q + 1))
                        if two:
                            pe.wait_ge(rt_ready.h, rt_ready.at(u.q + 1))
                        if u.past >= 2:
                            used = sq_ready if mode == "sage" else post_read
                            pe.wait_ge(used.h, used.at(u.q - 1))
                        for k in range(GT):
                            o = ps[3 + u.m % 2][:, k * D:(k + 1) * D]
                            mm = pe.matmul(o, ht[:, u.m % 2, k, :], w1, start=True, stop=not two)
                            if two:
                                mm = pe.matmul(o, rt[:, u.m % 2, k, :], w2, start=False, stop=True)
                        mm.then_inc(mm_done.h, 1)

                    def turn_out(u):
                        pe.wait_ge(out_ready.h, out_ready.at(u.q + 1))
                        if u.past >= 1:
                            pe.wait_ge(ot_ready.h, ot_ready.at(u.q))
                        for k in range(GT):
                            mm = pe.transpose(ps[5][:, k * D:(k + 1) * D], outb[:, u.par, u.g * GT + k, 0:D], ident[:, :])
                        mm.then_inc(t2_done.h, 1)

                    def product_out(u):
                        pe.wait_ge(ot_ready.h, ot_ready.at(u.q + 1))
                        if u.past >= 1:
                            pe.wait_ge(m2_read.h, m2_read.at(u.q))
                        for k in range(GT):
                            a = ot[:, u.m % 2, k, :]
                            if second == "keys":
                                mm = pe.matmul(ps[6 + k // 2][:, (k % 2) * 256:(k % 2) * 256 + D + 1], a, key_w[:, :],
                                               start=True, stop=True)
                            else:
                                mm = pe.matmul(ps[6][:, 2 * k:2 * k + 2], a, gat_s[:, score_l, :], start=True, stop=True)
                        mm.then_inc(m2_done.h, 1)

                    def slot(it, n):
                        if u := group(it, n, B):
                            turn(u)
                        if u := group(it, n, 1 + B):
                            product(u)
                        if second and (u := group(it, n, R)):
                            turn_out(u)
                        if second and (u := group(it, n, R + 1)):
                            product_out(u)
                    if products:
                        walk(pe, slot, DEPTH)

                @block.scalar
                def _(act):
                    def lift(u):
                        act.wait_ge(th_done.h, th_done.at(u.q + 1))
                        if u.past >= 2:
                            act.wait_ge(mm_done.h, mm_done.at(u.q - 1))
                        f = ht[:, u.m % 2, :, :].rearrange("p k d -> p (k d)")
                        if bn:
                            act.activation(f, ps[u.m % 2][:, :], ACT.Relu, bias=bn_col[:, 1:2],
                                           scale=bn_col[:, 0:1]).then_inc(ht_ready.h, 1)
                        else:
                            act.copy(f, ps[u.m % 2][:, :]).then_inc(ht_ready.h, 1)
                        if two and mode != "sage":
                            act.wait_ge(tr_done.h, tr_done.at(u.q + 1))
                            act.copy(rt[:, u.m % 2, :, :].rearrange("p k d -> p (k d)"),
                                     ps[turn_banks[u.m % NTB]][:, :]).then_inc(rt_ready.h, 1)

                    def raw_out(u):
                        act.wait_ge(mm_done.h, mm_done.at(u.q + 1))
                        if u.g == 0 and u.past >= 2 * NG:
                            act.wait_ge(stq[u.par].h, stq[u.par].at(16 * stores * u.it))
                            act.wait_ge(sum_ready.h, sum_ready.at(u.q - 2 * NG + NG))
                        act.copy(tiles(outb, u), ps[3 + u.m % 2][:, :].rearrange("p (k d) -> p k d", k=GT))\
                           .then_inc(out_ready.h, 1)
                        if u.past >= 2:
                            act.wait_ge(norm_ready.h, norm_ready.at(u.q - 1))
                        act.activation(ps[5 + u.m % 2][:, :], ps[3 + u.m % 2][:, :], ACT.Square).then_inc(sq_ready.h, 1)

                    def root(u):
                        act.wait_ge(var_ready.h, var_ready.at(u.q + 1))
                        act.activation(std[:, u.m % 4, :], mv[:, u.m % 4, :, 1], ACT.Sqrt).then_inc(std_ready.h, 1)

                    def scale(u):
                        act.wait_ge(norm_ready.h, norm_ready.at(u.q + 1))
                        if u.g == 0 and u.past >= 2 * NG:
                            act.wait_ge(stq[u.par].h, stq[u.par].at(16 * stores * u.it))
                        for k in range(GT):
                            ins = act.activation(outb[:, u.par, u.g * GT + k, 0:D], ub[:, u.m % 4, k, :], ACT.Identity,
                                                 bias=mv[:, u.m % 4, k, 0:1], scale=mv[:, u.m % 4, k, 1:2])
                        ins.then_inc(out_ready.h, 1)

                    def lift_out(u):
                        act.wait_ge(t2_done.h, t2_done.at(u.q + 1))
                        if u.past >= 2:
                            act.wait_ge(m2_done.h, m2_done.at(u.q - 1))
                        act.copy(ot[:, u.m % 2, :, :].rearrange("p k d -> p (k d)"), ps[5][:, :])\
                           .then_inc(ot_ready.h, 1)

                    def slot(it, n):
                        if products and (u := group(it, n, B)):
                            lift(u)
                        if mode == "sage" and (u := group(it, n, 2)):
                            raw_out(u)
                        if normed and (u := group(it, n, 3 + B)):
                            root(u)
                        if normed and (u := group(it, n, 5 + B)):
                            scale(u)
                        if second and (u := group(it, n, R)):
                            lift_out(u)
                    walk(act, slot, DEPTH)

                @block.vector
                def _(dve):
                    go = Chain(dve, dve_s)

                    def join(u):
                        if u.g == 0:
                            dve.wait_ge(ld[u.par].h, ld[u.par].at(16 * loads * (u.it + 1)))
                            go(dve.tensor_scalar(col1[:, u.par, :], in_r[:, u.par, :, D], 1.0, None, ALU.add))
                        if u.past >= 2:
                            dve.wait_ge(th_done.h, th_done.at(u.q - 1))
                        for k in range(GT):
                            c = u.g * GT + k
                            ins = dve.scalar_tensor_tensor(yb[:, u.m % 2, k, :], in_h[:, u.par, c, 0:D],
                                                           col1[:, u.par, c:c + 1], in_r[:, u.par, c, 0:D],
                                                           ALU.mult, ALU.add)
                        ins.then_inc(y_ready.h, 1)

                    def lift_agg(u):
                        dve.wait_ge(tr_done.h, tr_done.at(u.q + 1))
                        if u.past >= 2:
                            dve.wait_ge(mm_done.h, mm_done.at(u.q - 1))
                        dve.tensor_copy(rt[:, u.m % 2, :, :].rearrange("p k d -> p (k d)"),
                                        ps[turn_banks[u.m % NTB]][:, :]).then_inc(rt_ready.h, 1)

                    def squares(u):
                        dve.wait_ge(sq_ready.h, sq_ready.at(u.q + 1))
                        go(dve.tensor_tensor(acc[0:u.parts, 1],
                                             ps[5 + u.m % 2][0:u.parts, :].rearrange("p (k d) -> p k d", k=GT),
                                             acc[0:u.parts, 1], ALU.add))
                        dve.sem_inc(norm_ready.h, 1)

                    def post(u):
                        o3 = ps[3 + u.m % 2][:, :].rearrange("p (k d) -> p k d", k=GT)
                        w = ub[:, u.m % 4, :, :]
                        xb = xbuf[:, u.m % 4]
                        if products:
                            dve.wait_ge(mm_done.h, mm_done.at(u.q + 1))
                        if mode == "gat":
                            if u.g == 0 and u.past >= 2 * NG:
                                dve.wait_ge(stq[u.par].h, stq[u.par].at(16 * stores * u.it))
                            if mid:
                                go(dve.tensor_tensor(w, o3, bias, ALU.add))
                                dve.sem_inc(post_read.h, 1)
                                dve.scalar_tensor_tensor(tiles(outb, u), w, SLOPE, w, ALU.mult, ALU.max)\
                                   .then_inc(out_ready.h, 1)
                            else:
                                go(dve.tensor_tensor(tiles(outb, u), o3, bias, ALU.add))
                                dve.sem_inc(post_read.h, 1)
                                dve.sem_inc(out_ready.h, 1)
                            return
                        if u.past >= 4:
                            dve.wait_ge(out_ready.h, out_ready.at(u.q - 3))
                        if mode == "mean":
                            go(dve.tensor_tensor(w, o3, mean_nb[:, :, :], ALU.max))
                            dve.sem_inc(post_read.h, 1)
                        dve.wait_ge(pre_ready.h, pre_ready.at(u.q + 1))
                        if mode == "skip":
                            go(dve.scalar_tensor_tensor(w, xb, 0.0, tiles(in_e, u), ALU.max, ALU.add))
                        elif mode == "mean":
                            go(dve.tensor_tensor(w, w, xb, ALU.add))
                        else:
                            go(dve.tensor_tensor(w, o3, xb, ALU.add))
                            dve.sem_inc(post_read.h, 1)
                        for k in range(GT):
                            ins = dve.bn_stats(st6[:, k, :], ub[:, u.m % 4, k, :])
                        go(ins)
                        dve.sem_inc(tick.h, 1)
                        for k in range(GT):
                            ins = dve.bn_aggr(mv[:, u.m % 4, k, :], st6[:, k, :])
                        go(ins)
                        dve.tensor_scalar(mv[:, u.m % 4, :, 1], mv[:, u.m % 4, :, 1], EPS, None, ALU.add)\
                           .then_inc(var_ready.h, 1)

                    def norm(u):
                        dve.wait_ge(std_ready.h, std_ready.at(u.q + 1))
                        go(dve.reciprocal(mv[:, u.m % 4, :, 1], std[:, u.m % 4, :]))
                        dve.scalar_tensor_tensor(mv[:, u.m % 4, :, 0], mv[:, u.m % 4, :, 0], -1.0, mv[:, u.m % 4, :, 1],
                                                 ALU.mult, ALU.mult).then_inc(norm_ready.h, 1)

                    def scalars(u):
                        dve.wait_ge(m2_done.h, m2_done.at(u.q + 1))
                        if u.g == 0 and u.past >= 2 * NG:
                            dve.wait_ge(stq[u.par].h, stq[u.par].at(16 * stores * u.it))
                        if second == "keys":
                            for k in range(GT):
                                ins = dve.tensor_tensor(outu[:, u.par, u.g * GT + k, 0:D + 1],
                                                        ps[6 + k // 2][:, (k % 2) * 256:(k % 2) * 256 + D + 1],
                                                        key_b[:, :], ALU.add)
                            ins.then_inc(m2_read.h, 1)
                        else:
                            sv = ps[6][:, 0:2 * GT].rearrange("p (k s) -> p k s", s=2)
                            dve.tensor_copy(outb[:, u.par, u.g * GT:(u.g + 1) * GT, D:D + 2], sv)
                            dve.tensor_copy(outp[:, u.par, u.g * GT:(u.g + 1) * GT, :], sv).then_inc(m2_read.h, 1)

                    def slot(it, n):
                        if normed and (u := group(it, n, 4 + B)):
                            norm(u)
                        if loops and (u := group(it, n, 0)):
                            join(u)
                        if second and (u := group(it, n, R + 2)):
                            scalars(u)
                        if mode == "sage" and (u := group(it, n, 0)):
                            lift_agg(u)
                        if mode == "sage" and (u := group(it, n, 3)):
                            squares(u)
                        if mode != "sage" and (u := group(it, n, 2 + B)):
                            post(u)
                    per = {"sage": 1, "skip": 4, "mean": 5, "att": 4, "last": 4, "gat": 1}[mode] * 2 * NG
                    per += 2 if loops else 0
                    if mode == "sage":
                        go(dve.memset(acc[:, 1], 0.0))
                    walk(dve, slot, DEPTH, go, per)
                    dve_s.total = go.total

            dve_s.base += dve_s.total
            pool_s.base += pool_s.total
            for par, n in ((0, FULL + 1), (1, FULL)):
                ld[par].base += 16 * loads * n
                stq[par].base += 16 * stores * n
            used = [out_ready]
            if products:
                used += [th_done, ht_ready, mm_done]
                if mode != "sage":
                    used += [post_read]
            if loops:
                used += [y_ready]
            if two:
                used += [tr_done, rt_ready]
            if second:
                used += [t2_done, ot_ready, m2_done, m2_read]
            if mode == "sage":
                used += [sq_ready, sum_ready, norm_ready]
            if normed:
                used += [norm_ready, var_ready, std_ready, pre_ready]
            for s in used:
                s.base += NGR

        def batch_norm(layer):
            b, gamma, beta = (bn_par[:, k, layer:layer + 1] for k in range(3))
            with nc.Block() as block:
                @block.scalar
                def _(act):
                    act.wait_ge(d2a.h, d2a.at(1))
                    act.activation(sums[:, 4:5], sums[:, 2:3], ACT.Sqrt).then_inc(a2d.h, 1)

                @block.tensor
                def _(pe):
                    for s in range(2):
                        for k in range(GT):
                            mm = pe.matmul(ps[s][:, 0:1], acc[:, s, k, :], ones[:, 0:1], start=(k == 0),
                                           stop=(k == GT - 1))
                    mm.then_inc(p2d.h, 1)
                    pe.wait_ge(d2p.h, d2p.at(1))
                    pe.transpose(ps[2][:, 0:D], wq[:, :], ident[:, :])
                    pe.transpose(ps[2][:, D:2 * D], wqt[:, :], ident[:, :]).then_inc(p2d.h, 1)

                @block.vector
                def _(dve):
                    go = Chain(dve, dve_s)
                    mean, sq, var, full = (sums[:, k:k + 1] for k in range(4))
                    dve.wait_ge(p2d.h, p2d.at(1))
                    go(dve.tensor_scalar(mean, ps[0][:, 0:1], 1.0 / N, None, ALU.mult))
                    go(dve.tensor_scalar(sq, ps[1][:, 0:1], 1.0 / N, None, ALU.mult))
                    go(dve.tensor_tensor(var, mean, mean, ALU.mult))
                    go(dve.tensor_tensor(var, sq, var, ALU.subtract))
                    go(dve.tensor_scalar(var, var, 0.0, None, ALU.max))
                    go(dve.tensor_scalar(var, var, EPS, None, ALU.add))
                    dve.sem_inc(d2a.h, 1)
                    dve.wait_ge(a2d.h, a2d.at(1))
                    go(dve.reciprocal(var, sums[:, 4:5]))
                    go(dve.tensor_tensor(bn_col[:, 0:1], gamma, var, ALU.mult))
                    go(dve.tensor_tensor(full, mean, b, ALU.add))
                    go(dve.tensor_tensor(full, b, full, ALU.subtract))
                    go(dve.tensor_tensor(full, full, bn_col[:, 0:1], ALU.mult))
                    go(dve.tensor_tensor(bn_col[:, 1:2], full, beta, ALU.add))
                    go(dve.tensor_scalar(wq[:, :], ones[:, :], bn_col[:, 0:1], None, ALU.mult))
                    go(dve.tensor_scalar(wqt[:, :], ones[:, :], bn_col[:, 1:2], None, ALU.mult))
                    dve.sem_inc(d2p.h, 1)
                    dve.wait_ge(p2d.h, p2d.at(2))
                    go(dve.tensor_copy(bn_row[:, 0, :], ps[2][:, 0:D]))
                    go(dve.tensor_copy(bn_row[:, 1, :], ps[2][:, D:2 * D]))
                    dve_s.total = go.total
            dve_s.base += dve_s.total
            p2d.base += 2
            d2p.base += 1
            d2a.base += 1
            a2d.base += 1

        x = t["x"]
        edge_pass("mean", x)
        node_pass("sage", x, tab_a, layer=0)
        batch_norm(0)
        edge_pass("mean", tab_a, bn=True)
        node_pass("sage", tab_a, tab_b, bn=True, layer=1)
        batch_norm(1)
        edge_pass("mean", tab_b, bn=True)
        node_pass("sage", tab_b, tab_a, bn=True, layer=2)
        batch_norm(2)
        node_pass("skip", tab_a, tab_b, extra=x)
        edge_pass("mean", tab_b)
        node_pass("mean", tab_b, tab_a)
        edge_pass("att", tab_a)
        node_pass("att", tab_a, tab_b)
        edge_pass("gat", tab_b, layer=0)
        node_pass("gat", tab_b, tab_x0, layer=0)
        edge_pass("gat", tab_x0, layer=1)
        node_pass("gat", tab_x0, tab_a, layer=1)
        edge_pass("gat", tab_a, layer=2)
        node_pass("gat", tab_a, tab_u, extra=tab_x0, layer=2)
        edge_pass("gat", tab_u, layer=3)
        node_pass("gat", tab_u, tab_a, extra=tab_x0, layer=3)
        edge_pass("gat", tab_a, layer=4)
        node_pass("last", tab_a, out, extra=tab_b, layer=4)


_INS = ['x', 'src', 'dst', 'edge_attr_16', 'L0_gnn_Wl', 'L0_gnn_Wr', 'L0_gnn_b', 'L0_gnn_gamma', 'L0_gnn_beta',
        'L1_gnn_W_self', 'L1_gnn_b_self', 'L1_gnn_W_neigh', 'L1_gnn_b_neigh', 'L2_gnn_W_w', 'L2_gnn_W_b',
        'L2_gnn_WS_w', 'L2_gnn_WS_b', 'L2_gnn_q_w', 'L2_gnn_q_b', 'L2_gnn_k_w', 'L2_gnn_k_b', 'L3_gnn_Ws',
        'L3_gnn_Wes', 'L3_gnn_a_srcs', 'L3_gnn_a_dsts', 'L3_gnn_a_edges', 'L3_gnn_biases', 'L3_gnn_mid_ws']


def kernel(**inputs):
    import numpy as _np
    import concourse.bacc as _bacc
    from concourse import mybir as _mybir
    from concourse.bass_utils import run_bass_kernel_spmd as _run

    nc = _bacc.Bacc("TRN2", target_bir_lowering=False, num_devices=1)
    arrays, aps = {}, {}
    for name in _INS:
        a = _np.ascontiguousarray(inputs[name])
        arrays[f"in_{name}_dram"] = a
        aps[name] = nc.dram_tensor(f"in_{name}_dram", a.shape, _mybir.dt.from_np(a.dtype), kind="ExternalInput").ap()
    shape = tuple(inputs["x"].shape)
    out = nc.dram_tensor("out_0_dram", shape, _mybir.dt.float32, kind="ExternalOutput").ap()
    gnn(nc, aps, out)
    r = _run(nc, [arrays], core_ids=[0])
    return r.results[0]["out_0_dram"]
```

```python
import math
from contextlib import ExitStack
from typing import NamedTuple

import concourse.bass as bass
from concourse import mybir

F32 = mybir.dt.float32
I32 = mybir.dt.int32
ALU = mybir.AluOpType
ACT = mybir.ActivationFunctionType
AX = mybir.AxisListType.X

P = 128
D = 128
W = D + 2
ED = 16
CH = 8
G = 16
GT = 4
NG = G // GT
GH = G // 2
SUP = P * G
BIG = 1.0e30
EPS = 1e-5
LAYERS = 5
ALPHA, THETA = 0.2, 0.2
ATT_SLOPE, SLOPE = 0.2, 0.01


class Sem:

    def __init__(self, handle):
        self.h = handle
        self.base = 0

    def at(self, n):
        return self.base + n


class Group(NamedTuple):
    q: object
    it: object
    par: int
    g: int
    m: int
    parts: int
    past: int

    @property
    def half(self):
        return self.g // (NG // 2)

    @property
    def first(self):
        return self.g % (NG // 2) == 0


class Chain:

    def __init__(self, eng, sem):
        self.eng, self.sem = eng, sem
        self.start, self.i, self.per, self.n, self.total = 0, None, 0, 0, 0

    def enter(self, i, per, turns):
        self.start, self.i, self.per, self.n = self.total, i, per, 0
        self.turns = turns

    def leave(self):
        if self.n != self.per:
            raise AssertionError(f"chain of {self.sem.h}: {self.n} steps in a turn, not {self.per}")
        self.total = self.start + self.turns * self.per
        self.i = None

    def __call__(self, ins):
        ins.then_inc(self.sem.h, 1)
        self.n += 1
        if self.i is None:
            self.total += 1
            self.eng.wait_ge(self.sem.h, self.sem.at(self.total))
        else:
            self.eng.wait_ge(self.sem.h, self.sem.at(self.start + self.i * self.per + self.n))


def gnn(nc, t, out):
    N = t["x"].shape[0]
    E = t["src"].shape[0]
    COLS = (E + P * CH - 1) // (P * CH) * CH
    NCH = COLS // CH
    assert NCH % 2 == 1 and NCH >= 3
    ROWS, REST = E // COLS, E % COLS
    LIVE = ROWS + (REST > 0)
    ST = N // SUP
    assert ST % 2 == 0 and ST >= 6
    LASTP = (N - ST * SUP) // G
    assert ST * SUP + LASTP * G == N and 0 < LASTP < P
    NGR = NG * (ST + 1)

    ctx = ExitStack()
    with ctx, nc.allow_non_contiguous_dma(reason="single columns of weights and of edge lists"):
        def sb(name, shape, dt=F32):
            return ctx.enter_context(nc.sbuf_tensor(name, shape, dt))

        def sem(name):
            return Sem(ctx.enter_context(nc.semaphore(name)))

        def table(name, w=W):
            return nc.dram_tensor(name, (N, w), F32, kind="Internal").ap()
        tab_a, tab_b, tab_x0, tab_u = table("tab_a"), table("tab_b"), table("tab_x0"), table("tab_u")
        pair_tab, agg = table("pair_tab", 2), table("agg_tab")

        src_i = sb("src_i", [P, COLS + 2 * CH], I32)
        dst_i = sb("dst_i", [P, COLS + 2 * CH], I32)
        scat_i = sb("scat_i", [P, COLS], I32)
        fix_i = sb("fix_i", [P, 1], I32)
        dstf = sb("dstf", [P, COLS])
        same = sb("same", [P, COLS])
        pen = sb("pen", [P, COLS])
        fixm = sb("fixm", [P, COLS])
        inv_cnt = sb("inv_cnt", [P, COLS])
        inv_cnt_fix = sb("inv_cnt_fix", [P, 1])
        edge_c = sb("edge_c", [P, LAYERS, COLS])
        loop_c = sb("loop_c", [P, LAYERS, COLS])
        loop_fix = sb("loop_fix", [P, LAYERS])
        chain_m = sb("chain_m", [P, P])
        chain_pen = sb("chain_pen", [P, P])
        ident = sb("ident", [P, P])
        ones = sb("ones", [P, P])
        zrow = sb("zrow", [P, COLS])

        sage_l = sb("sage_l", [P, 3, D])
        sage_r = sb("sage_r", [P, 3, D])
        mean_w = sb("mean_w", [P, 2, D])
        mean_b = sb("mean_b", [P, GT, D])
        mean_nb = sb("mean_nb", [P, GT, D])
        att_w = sb("att_w", [P, 2, D])
        att_b = sb("att_b", [P, GT, D])
        att_mb = sb("att_mb", [P, D])
        key_w = sb("key_w", [P, D + 1])
        key_b = sb("key_b", [P, D + 1])
        gat_w = sb("gat_w", [P, LAYERS, D])
        gat_b = sb("gat_b", [P, LAYERS, GT, D])
        gat_s = sb("gat_s", [P, LAYERS, 2])
        gat_s_row = sb("gat_s_row", [P, 3, 2, D])
        mid_w = sb("mid_w", [P, 3, D])
        bn_col = sb("bn_col", [P, 2])
        bn_row = sb("bn_row", [P, 2, D])
        bn_par = sb("bn_par", [P, 3, 3])

        gi = sb("gi", [P, 2, CH], I32)
        di = sb("di", [P, 2, CH], I32)
        wi = sb("wi", [P, 2, CH], I32)
        dpair = sb("dpair", [P, 2, CH, 2])
        wide = sb("wide", [P, CH, D])
        wide2 = sb("wide2", [P, CH, D])
        obuf = sb("obuf", [P, 2, CH, W])
        fixv = sb("fixv", [P, D])
        fixt = sb("fixt", [P, D])
        m_all = sb("m_all", [P, COLS + 1])
        den_all = sb("den_all", [P, COLS + 1])
        sl_all = sb("sl_all", [P, COLS])
        s8 = sb("s8", [P, CH])
        z8 = sb("z8", [P, CH])
        l8 = sb("l8", [P, CH])
        e4 = sb("e4", [P, 4 * CH])
        x4 = sb("x4", [P, 4 * CH])
        sc8 = sb("sc8", [P, 2, CH])
        fx = sb("fx", [P, 16])
        lrow = sb("lrow", [P, D + 1])
        wq = sb("wq", [P, P])
        wqt = sb("wqt", [P, P])
        fixo = sb("fixo", [P, W])

        node_in = sb("node_in", [P, 3, 2, G, W])
        in_h, in_r, in_e = (node_in[:, k] for k in range(3))
        node_out = sb("node_out", [P, 2, 2, G, W])
        outb, outu = node_out[:, 0], node_out[:, 1]
        outp = sb("outp", [P, 2, G, 2])
        yb = sb("yb", [P, 2, GT, D])
        ht = sb("ht", [P, 2, GT, D])
        rt = sb("rt", [P, 2, GT, D])
        ub = sb("ub", [P, 4, GT, D])
        xbuf = sb("xbuf", [P, 4, GT, D])
        ot = sb("ot", [P, 2, GT, D])
        st6 = sb("st6", [P, GT, 6])
        mv = sb("mv", [P, 4, GT, 2])
        std = sb("std", [P, 4, GT])
        col1 = sb("col1", [P, 2, G])
        acc = sb("acc", [P, 2, GT, D])
        sums = sb("sums", [P, 8])

        room = node_in[:, :, :, :, :].rearrange("p k a g w -> p (k a g w)")
        ea = room[:, 0:COLS * ED]
        at, lots = 0, []
        for w in (D, D, W, W):
            lots.append(room[:, at:at + 2 * CH * w].rearrange("p (a j w) -> p a j w", a=2, j=CH))
            at += 2 * CH * w
        state, rows_x, rows, drows = lots
        eat = node_out[:, :, :, :, :].rearrange("p k a g w -> p (k a g w)")
        assert COLS * ED <= 2 * 2 * G * W

        ps = [ctx.enter_context(nc.psum_tensor(f"ps{i}", [P, 512], F32)) for i in range(8)]

        dve_s, act_s, pool_s, pe_s = sem("dve_s"), sem("act_s"), sem("pool_s"), sem("pe_s")
        tick = sem("tick")
        d2p, p2d, d2a, a2d, p2a, a2p = (sem(n) for n in ("d2p", "p2d", "d2a", "a2d", "p2a", "a2p"))
        load = sem("load")
        gath = [sem("gath0"), sem("gath1")]
        gath_d = [sem("gath_d0"), sem("gath_d1")]
        scat = [sem("scat0"), sem("scat1")]
        scat_fix, zeroed = sem("scat_fix"), sem("zeroed")
        idx_ready, rows_used, ob_ready, exp_in, exp_out = (
            sem(n) for n in ("idx_ready", "rows_used", "ob_ready", "exp_in", "exp_out"))
        fix_ready = sem("fix_ready")
        ld = [[sem(f"ld{par}{half}") for half in range(2)] for par in range(2)]
        stq = [[sem(f"stq{par}{half}") for half in range(2)] for par in range(2)]
        y_ready, th_done, tr_done, ht_ready, rt_ready, mm_done, post_read, out_ready = (
            sem(n) for n in ("y_ready", "th_done", "tr_done", "ht_ready", "rt_ready", "mm_done", "post_read",
                             "out_ready"))
        t2_done, ot_ready, m2_done, m2_read, sq_ready, norm_ready = (
            sem(n) for n in ("t2_done", "ot_ready", "m2_done", "m2_read", "sq_ready", "norm_ready"))
        var_ready, std_ready = sem("var_ready"), sem("std_ready")
        rows_ready, stats_ready, aggr_ready, recip_ready = (
            sem(n) for n in ("rows_ready", "stats_ready", "aggr_ready", "recip_ready"))
        weighed, src_ready, dst_ready = sem("weighed"), sem("src_ready"), sem("dst_ready")
        pre_ready, sum_ready = sem("pre_ready"), sem("sum_ready")

        def bc(ap, n):
            return ap.unsqueeze(1).to_broadcast([P, n, ap.shape[-1]])

        def bl(ap, n=D):
            return ap.unsqueeze(2).to_broadcast([P, ap.shape[-1], n])

        assert 2 * CH == G
        ZERO_STEP = ST // 16
        NLOAD = [0]
        with nc.Block() as block:
            def edge_load(sp, dst_ap, dram, s, w=1):
                n = 0
                src_v = dram[0:ROWS * COLS] if w == 1 else dram[0:ROWS * COLS, :]
                pat = "(p j) -> p j" if w == 1 else "(p j) k -> p (j k)"
                sp.dma_start(dst_ap[0:ROWS, 0:COLS * w], src_v.rearrange(pat, p=ROWS)).then_inc(s.h, 16)
                n += 16
                if REST:
                    src_v = dram[ROWS * COLS:E] if w == 1 else dram[ROWS * COLS:E, :]
                    sp.dma_start(dst_ap[ROWS:ROWS + 1, 0:REST * w], src_v.rearrange(pat, p=1)).then_inc(s.h, 16)
                    n += 16
                return n

            def zero_agg(sp, s0, s1):
                zeros = obuf[:, :, :, :].rearrange("p a j w -> p (a j w)")
                for s in range(s0, s1):
                    m = P if s < ST else LASTP
                    sp.dma_start(agg[s * SUP:s * SUP + m * G, :].rearrange("(p g) w -> p (g w)", p=m),
                                 zeros[0:m, :]).then_inc(zeroed.h, 16)

            dpad = wide[:, :, :].rearrange("p a b -> p (a b)").bitcast(I32)
            bnd = fx[:, 0:2].bitcast(I32)

            @block.sync
            def _(sp):
                sp.wait_ge(d2a.h, d2a.at(1))
                sp.wait_ge(pool_s.h, pool_s.at(1))
                n = edge_load(sp, src_i, t["src"], load)
                n += edge_load(sp, dst_i, t["dst"], load)
                n += edge_load(sp, dpad, t["dst"], load)
                n += edge_load(sp, ea, t["edge_attr_16"], load, ED)
                dd = t["dst"].rearrange("(e o) -> e o", o=1)
                sp.dma_start(bnd[1:LIVE, 0:1], dd[COLS - 1:COLS - 1 + (LIVE - 2) * COLS + 1:COLS, :]).then_inc(load.h, 16)
                sp.dma_start(bnd[0:LIVE - 1, 1:2], dd[COLS:COLS + (LIVE - 2) * COLS + 1:COLS, :]).then_inc(load.h, 16)
                n += 32
                for l in range(LAYERS):
                    sp.dma_start(eat[0:ED, l * D:(l + 1) * D], t["L3_gnn_Wes"][l]).then_inc(load.h, 16)
                    for k in range(ED):
                        sp.dma_start(eat[k:k + 1, (LAYERS + l) * D:(LAYERS + l + 1) * D],
                                     t["L3_gnn_a_edges"][l:l + 1, :]).then_inc(load.h, 16)
                    n += 16 + 16 * ED
                    zero_agg(sp, l * ZERO_STEP, (l + 1) * ZERO_STEP)
                NLOAD[0] = n
                sp.wait_ge(load.h, load.at(n))
                sp.sem_inc(a2d.h, 1)
                zero_agg(sp, LAYERS * ZERO_STEP, ST // 2)

            @block.gpsimd
            def _(pool):
                pool.memset(ea[:, :], 0.0)
                pool.memset(ident[:, :], 0.0).then_inc(pool_s.h, 1)
                pool.wait_ge(pool_s.h, pool_s.at(1))
                pool.affine_select(out=ident[:, :], in_=ident[:, :], compare_op=ALU.not_equal, fill=1.0, base=0,
                                   pattern=[[-1, P]], channel_multiplier=1).then_inc(pool_s.h, 1)
                pool.wait_ge(d2p.h, d2p.at(2))
                pool.affine_select(out=chain_m[:, :], in_=chain_m[:, :], compare_op=ALU.is_gt, fill=0.0, base=0,
                                   pattern=[[1, P]], channel_multiplier=-1).then_inc(pool_s.h, 1)
                pool.affine_select(out=chain_pen[:, :], in_=chain_pen[:, :], compare_op=ALU.is_gt, fill=0.0, base=0,
                                   pattern=[[-1, P]], channel_multiplier=1).then_inc(pool_s.h, 1)

            @block.vector
            def _(dve):
                go = Chain(dve, dve_s)
                dve.memset(src_i[:, :], 0)
                dve.memset(dst_i[:, :], 0)
                dve.memset(dpad, N)
                dve.memset(bnd[:, 0:1], -1)
                dve.memset(bnd[:, 1:2], N + 1)
                dve.memset(ones[:, :], 1.0)
                dve.memset(zrow[:, :], 1.0)
                dve.memset(same[:, 0:1], 0.0)
                dve.memset(eat[:, :], 0.0)
                go(dve.memset(obuf[:, :, :, :], 0.0))
                dve.sem_inc(d2a.h, 1)
                dve.wait_ge(a2d.h, a2d.at(1))
                dve.tensor_copy(fx[:, 2:4], bnd[:, 0:2])
                go(dve.tensor_copy(dstf[:, :], dpad[:, 0:COLS]))
                dve.tensor_tensor(same[:, 1:COLS], dstf[:, 1:COLS], dstf[:, 0:COLS - 1], ALU.is_equal)
                dve.tensor_tensor(pen[:, 0:COLS - 1], dstf[:, 0:COLS - 1], dstf[:, 1:COLS], ALU.not_equal)
                dve.tensor_tensor(pen[:, COLS - 1:COLS], dstf[:, COLS - 1:COLS], fx[:, 3:4], ALU.not_equal)
                dve.tensor_tensor(fx[:, 4:5], dstf[:, 0:1], fx[:, 2:3], ALU.is_equal)
                go(dve.tensor_scalar(fixm[:, :], dstf[:, :], dstf[:, 0:1], None, ALU.is_equal))
                go(dve.scalar_tensor_tensor(fixm[:, :], fixm[:, :], fx[:, 4:5], pen[:, :], ALU.mult, ALU.mult))
                go(dve.tensor_tensor(m_all[:, 0:COLS], pen[:, :], fixm[:, :], ALU.subtract))
                go(dve.scalar_tensor_tensor(den_all[:, 0:COLS], dstf[:, :], float(-N), m_all[:, 0:COLS], ALU.add, ALU.mult))
                dve.tensor_scalar(scat_i[:, :], den_all[:, 0:COLS], float(N), None, ALU.add)
                dve.tensor_reduce(fx[:, 5:6], fixm[:, :], AX, ALU.max)
                go(dve.tensor_scalar(pen[:, :], same[:, :], -1.0, BIG, ALU.add, ALU.mult))
                go(dve.scalar_tensor_tensor(fx[:, 6:7], dstf[:, 0:1], float(-N), fx[:, 5:6], ALU.add, ALU.mult))
                dve.tensor_scalar(fix_i[:, :], fx[:, 6:7], float(N), None, ALU.add)
                go(dve.tensor_tensor_scan(sl_all[:, :], same[:, :], zrow[:, :], 0.0, ALU.mult, ALU.add))
                go(dve.tensor_scalar(inv_cnt[:, :], sl_all[:, :], 1.0, None, ALU.max))
                go(dve.reciprocal(inv_cnt[:, :], inv_cnt[:, :]))
                dve.tensor_tensor_reduce(m_all[:, 0:COLS], fixm[:, :], sl_all[:, :], 1.0, 0.0, ALU.mult, ALU.add,
                                         fx[:, 7:8])
                dve.tensor_scalar(wq[:, :], ones[:, :], dstf[:, 0:1], None, ALU.mult)
                go(dve.tensor_scalar(wqt[:, :], ones[:, :], dstf[:, COLS - 1:COLS], None, ALU.mult))
                for l in range(LAYERS):
                    go(dve.tensor_tensor_reduce(wide2[0:ED, 0, :], eat[0:ED, l * D:(l + 1) * D],
                                                eat[0:ED, (LAYERS + l) * D:(LAYERS + l + 1) * D], 1.0, 0.0,
                                                ALU.mult, ALU.add, e4[0:ED, l:l + 1]))
                dve.wait_ge(pool_s.h, pool_s.at(2))
                for l in range(LAYERS):
                    go(dve.tensor_scalar(lrow[0:ED, l * ED:(l + 1) * ED], ident[0:ED, 0:ED], e4[0:ED, l:l + 1], None,
                                         ALU.mult))
                dve.sem_inc(d2p.h, 1)
                dve.wait_ge(p2d.h, p2d.at(1))
                dve.tensor_scalar(chain_m[:, :], ps[0][:, 0:P], dstf[:, COLS - 1:COLS], None, ALU.is_equal)
                dve.tensor_scalar(chain_pen[:, :], ps[1][:, 0:P], dstf[:, 0:1], None, ALU.is_equal)
                go(dve.tensor_copy(wide2[:, 0, 0:LAYERS * ED], ps[2][:, 0:LAYERS * ED]))
                dve.sem_inc(d2p.h, 1)
                ea3 = ea[:, :].rearrange("p (j k) -> p j k", k=ED)
                eat3 = eat[:, 0:COLS * ED].rearrange("p (j k) -> p j k", k=ED)
                dve.tensor_copy(lrow[:, 0:1], sl_all[:, COLS - 1:COLS])
                for l in range(LAYERS):
                    v = wide2[:, 0, l * ED:(l + 1) * ED].unsqueeze(1).to_broadcast([P, COLS, ED])
                    go(dve.tensor_tensor(eat3, ea3, v, ALU.mult))
                    go(dve.tensor_reduce(edge_c[:, l, :], eat3, AX, ALU.add))
                    go(dve.tensor_tensor_scan(loop_c[:, l, :], same[:, :], edge_c[:, l, :], 0.0, ALU.mult, ALU.add))
                    dve.tensor_copy(lrow[:, 1 + l:2 + l], loop_c[:, l, COLS - 1:COLS])
                    go(dve.tensor_tensor_reduce(m_all[:, 0:COLS], fixm[:, :], loop_c[:, l, :], 1.0, 0.0, ALU.mult,
                                                ALU.add, loop_fix[:, l:l + 1]))
                    go(dve.tensor_tensor(loop_c[:, l, :], loop_c[:, l, :], inv_cnt[:, :], ALU.mult))
                dve.wait_ge(pool_s.h, pool_s.at(4))
                go(dve.tensor_scalar(chain_pen[:, :], chain_pen[:, :], -1.0, BIG, ALU.add, ALU.mult))
                dve.sem_inc(d2p.h, 1)
                dve.wait_ge(p2d.h, p2d.at(2))
                go(dve.tensor_tensor(inv_cnt_fix[:, :], ps[3][:, 0:1], fx[:, 7:8], ALU.add))
                go(dve.tensor_scalar(inv_cnt_fix[:, :], inv_cnt_fix[:, :], 1.0, None, ALU.max))
                go(dve.reciprocal(inv_cnt_fix[:, :], inv_cnt_fix[:, :]))
                go(dve.tensor_tensor(loop_fix[:, :], ps[3][:, 1:1 + LAYERS], loop_fix[:, :], ALU.add))
                go(dve.tensor_scalar(loop_fix[:, :], loop_fix[:, :], inv_cnt_fix[:, 0:1], None, ALU.mult))
                dve_s.total = go.total

            @block.tensor
            def _(pe):
                pe.wait_ge(d2p.h, d2p.at(1))
                pe.transpose(ps[0][:, 0:P], wq[:, :], ident[:, :])
                pe.transpose(ps[1][:, 0:P], wqt[:, :], ident[:, :])
                pe.matmul(ps[2][:, 0:LAYERS * ED], ones[0:ED, :], lrow[0:ED, 0:LAYERS * ED], start=True,
                          stop=True).then_inc(p2d.h, 1)
                pe.wait_ge(d2p.h, d2p.at(3))
                pe.matmul(ps[3][:, 0:1 + LAYERS], chain_m[:, :], lrow[:, 0:1 + LAYERS], start=True,
                          stop=True).then_inc(p2d.h, 1)
        dve_s.base += dve_s.total
        d2a.base += 1
        a2d.base += 1
        pool_s.base += 4
        d2p.base += 3
        p2d.base += 2
        load.base += NLOAD[0]

        raw = [in_h[:, 0, i, 0:D] for i in range(G)] + [in_h[:, 1, i, 0:D] for i in range(G)]
        mean_ws, mean_wn, att_ww, att_ws, kw, mids = raw[0], raw[1], raw[2], raw[3], raw[4], raw[5:8]
        qw = in_h[:, 0, 8, 0:D + 1]
        gat_raw_t = raw[16:16 + LAYERS]
        mbeta = raw[21:24]
        bcols = raw[24:28]
        vec = in_r[:, 0, 0, :]
        V_MS, V_MN, V_AW, V_AS, V_QB, V_KB, V_B, V_SRC, V_DST = 0, 1, 2, 3, 4, 5, 6, 11, 16
        blend = [math.log(THETA / (i + 1) + 1.0) for i in range(3)]
        with nc.Block() as block:
            @block.sync
            def _(sp):
                n = 0

                def get(dst_ap, src_ap):
                    sp.dma_start(dst_ap, src_ap).then_inc(load.h, 16)
                    return 16
                for l in range(3):
                    n += get(sage_l[:, l, :], t["L0_gnn_Wl"][l])
                    n += get(sage_r[:, l, :], t["L0_gnn_Wr"][l])
                    n += get(mids[l], t["L3_gnn_mid_ws"][l])
                for l in range(LAYERS):
                    n += get(gat_w[:, l, :], t["L3_gnn_Ws"][l])
                for a, b in ((mean_ws, "L1_gnn_W_self"), (mean_wn, "L1_gnn_W_neigh"), (att_ww, "L2_gnn_W_w"),
                             (att_ws, "L2_gnn_WS_w"), (kw, "L2_gnn_k_w")):
                    n += get(a, t[b])
                n += get(qw[:, 0:D], t["L2_gnn_q_w"])

                def col(dst_ap, v):
                    return get(dst_ap, v.rearrange("(p o) -> p o", o=1))
                n += col(vec[:, V_MS:V_MS + 1], t["L1_gnn_b_self"])
                n += col(vec[:, V_MN:V_MN + 1], t["L1_gnn_b_neigh"])
                n += col(vec[:, V_AW:V_AW + 1], t["L2_gnn_W_b"])
                n += col(vec[:, V_AS:V_AS + 1], t["L2_gnn_WS_b"])
                n += col(vec[:, V_KB:V_KB + 1], t["L2_gnn_k_b"])
                n += col(qw[:, D:D + 1], t["L2_gnn_q_b"])
                for l in range(LAYERS):
                    n += col(vec[:, V_B + l:V_B + l + 1], t["L3_gnn_biases"][l])
                    n += col(vec[:, V_SRC + 2 * l:V_SRC + 2 * l + 1], t["L3_gnn_a_srcs"][l])
                    n += col(vec[:, V_SRC + 2 * l + 1:V_SRC + 2 * l + 2], t["L3_gnn_a_dsts"][l])
                for l in range(3):
                    n += col(bn_par[:, 0, l:l + 1], t["L0_gnn_b"][l])
                    n += col(bn_par[:, 1, l:l + 1], t["L0_gnn_gamma"][l])
                    n += col(bn_par[:, 2, l:l + 1], t["L0_gnn_beta"][l])
                NLOAD[0] = n
                sp.wait_ge(load.h, load.at(n))
                sp.sem_inc(a2d.h, 1)
                zero_agg(sp, ST // 2, ST + 1)

            @block.vector
            def _(dve):
                go = Chain(dve, dve_s)
                dve.memset(outu[:, :, :, :], 0.0)
                go(dve.memset(outb[:, :, :, :], 0.0))
                dve.wait_ge(a2d.h, a2d.at(1))
                for l in range(3):
                    go(dve.tensor_scalar(mbeta[l], ident[:, :], 1.0 - blend[l], None, ALU.mult))
                    go(dve.scalar_tensor_tensor(mbeta[l], mids[l], blend[l], mbeta[l], ALU.mult, ALU.add))
                    go(dve.tensor_scalar(mid_w[:, l, :], mbeta[l], ALPHA, None, ALU.mult))
                go(dve.tensor_tensor(vec[:, V_MS:V_MS + 1], vec[:, V_MS:V_MS + 1], vec[:, V_MN:V_MN + 1], ALU.add))
                go(dve.tensor_scalar(bcols[0], ones[:, :], vec[:, V_MS:V_MS + 1], None, ALU.mult))
                go(dve.tensor_scalar(bcols[1], ones[:, :], vec[:, V_AS:V_AS + 1], None, ALU.mult))
                go(dve.tensor_scalar(bcols[2], ones[:, :], vec[:, V_AW:V_AW + 1], None, ALU.mult))
                go(dve.tensor_scalar(bcols[3], ones[:, :], vec[:, V_KB:V_KB + 1], None, ALU.mult))
                dve.sem_inc(d2p.h, 1)
                dve.wait_ge(p2d.h, p2d.at(1))
                dve.tensor_copy(mean_w[:, 0, :], ps[0][:, 0:D])
                dve.tensor_copy(mean_w[:, 1, :], ps[0][:, D:2 * D])
                dve.tensor_copy(att_w[:, 0, :], ps[0][:, 2 * D:3 * D])
                dve.tensor_copy(att_w[:, 1, :], ps[0][:, 3 * D:4 * D])
                for g in range(GT):
                    dve.tensor_copy(mean_b[:, g, :], ps[1][:, 0:D])
                    dve.tensor_scalar(mean_nb[:, g, :], ps[1][:, 0:D], -1.0, None, ALU.mult)
                    dve.tensor_copy(att_b[:, g, :], ps[1][:, D:2 * D])
                dve.tensor_copy(att_mb[:, :], ps[1][:, 2 * D:3 * D])
                dve.tensor_scalar(key_w[:, :], ps[2][:, 0:D + 1], float(D) ** -0.5, None, ALU.mult)
                dve.tensor_scalar(key_b[:, :], ps[2][:, 256:256 + D + 1], float(D) ** -0.5, None, ALU.mult)
                for l in range(LAYERS):
                    go(dve.tensor_copy(gat_raw_t[l], ps[3 + l // 4][:, (l % 4) * D:(l % 4 + 1) * D]))
                for l in range(LAYERS):
                    go(dve.tensor_scalar(yb[:, l // 4, l % 4, :], ones[:, :], vec[:, V_B + l:V_B + l + 1], None, ALU.mult))
                for l in range(3):
                    for s in range(2):
                        v = V_SRC + 2 * (l + 2) + s
                        go(dve.tensor_scalar(xbuf[:, l, s, :], ones[:, :], vec[:, v:v + 1], None, ALU.mult))
                dve.sem_inc(d2p.h, 1)
                dve.wait_ge(p2d.h, p2d.at(2))
                for l in range(3):
                    dve.tensor_copy(gat_s_row[:, l, :, :].rearrange("p s d -> p (s d)"),
                                    ps[1 + l // 2][:, l % 2 * 2 * D:(l % 2 + 1) * 2 * D])
                for l in range(LAYERS):
                    dve.tensor_copy(gat_s[:, l, :], ps[5][:, 2 * l:2 * l + 2])
                    scale = 1.0 - ALPHA if 1 <= l <= 3 else 1.0
                    for g in range(GT):
                        dve.tensor_scalar(gat_b[:, l, g, :], ps[6 + l // 4][:, (l % 4) * D:(l % 4 + 1) * D], scale,
                                          None, ALU.mult)
                for l in range(3):
                    go(dve.tensor_scalar(gat_w[:, l + 1, :], ps[0][:, l * D:(l + 1) * D], 1.0 - ALPHA, None, ALU.mult))
                dve_s.total = go.total

            @block.tensor
            def _(pe):
                pe.wait_ge(d2p.h, d2p.at(1))
                for k, w in enumerate((mean_ws, mean_wn, att_ws, att_ww)):
                    pe.transpose(ps[0][:, k * D:(k + 1) * D], w, ident[:, :])
                for k in range(3):
                    pe.matmul(ps[1][:, k * D:(k + 1) * D], bcols[k], ident[:, :], start=True, stop=True)
                pe.matmul(ps[2][:, 0:D + 1], kw, qw, start=True, stop=True)
                pe.matmul(ps[2][:, 256:256 + D + 1], bcols[3], qw, start=True, stop=True)
                for l in range(LAYERS):
                    mm = pe.transpose(ps[3 + l // 4][:, (l % 4) * D:(l % 4 + 1) * D], gat_w[:, l, :], ident[:, :])
                mm.then_inc(p2d.h, 1)
                pe.wait_ge(d2p.h, d2p.at(2))
                for l in range(3):
                    for s in range(2):
                        pe.matmul(ps[1 + l // 2][:, (l % 2 * 2 + s) * D:(l % 2 * 2 + s + 1) * D], xbuf[:, l, s, :],
                                  gat_raw_t[l + 2], start=True, stop=True)
                for l in range(3):
                    pe.matmul(ps[0][:, l * D:(l + 1) * D], gat_raw_t[l + 1], mbeta[l], start=True, stop=True)
                for l in range(LAYERS):
                    pe.matmul(ps[5][:, 2 * l:2 * l + 2], gat_raw_t[l], vec[:, V_SRC + 2 * l:V_SRC + 2 * l + 2],
                              start=True, stop=True)
                    mm = pe.matmul(ps[6 + l // 4][:, (l % 4) * D:(l % 4 + 1) * D], yb[:, l // 4, l % 4, :],
                                   mbeta[l - 1] if 1 <= l <= 3 else ident[:, :], start=True, stop=True)
                mm.then_inc(p2d.h, 1)
        dve_s.base += dve_s.total
        a2d.base += 1
        d2p.base += 2
        p2d.base += 2
        load.base += NLOAD[0]

        def edge_pass(mode, tab, bn=False, layer=0):
            wide_tab = tab.shape[1] == W
            buf = rows if wide_tab else rows_x
            flash = mode != "mean"
            PER = {"mean": 18 + 6 * bn, "att": 26, "gat": 36}[mode]

            with nc.Block() as block:
                @block.gpsimd
                def _(pool):
                    def ticked(s, n):
                        pool.wait_ge(s.h, s.at(n))
                        pool.sem_inc(tick.h, 1)

                    def gathers(par):
                        for j in range(CH):
                            pool.indirect_dma_start(
                                out=buf[:, par, j, :], out_offset=None, in_=tab[:, :],
                                in_offset=bass.IndirectOffsetOnAxis(ap=gi[:, par, j:j + 1], axis=0)
                            ).then_inc(gath[par].h, 16)
                            if flash:
                                dtab = tab_u if mode == "att" else pair_tab
                                dbuf = drows if mode == "att" else dpair
                                pool.indirect_dma_start(
                                    out=dbuf[:, par, j, :], out_offset=None, in_=dtab[:, :],
                                    in_offset=bass.IndirectOffsetOnAxis(ap=di[:, par, j:j + 1], axis=0)
                                ).then_inc(gath_d[par].h, 16)

                    def scatters(k, par):
                        ticked(ob_ready, k + 1)
                        for j in range(CH):
                            pool.indirect_dma_start(
                                out=agg[:, :], out_offset=bass.IndirectOffsetOnAxis(ap=wi[:, par, j:j + 1], axis=0),
                                in_=obuf[:, par, j, :], in_offset=None, bounds_check=N - 1, oob_is_err=False
                            ).then_inc(scat[par].h, 16)

                    def step(k, par, first=False):
                        ticked(idx_ready, k + 2)
                        if not first:
                            ticked(rows_used, k)
                        gathers(1 - par)
                        scatters(k, par)

                    ticked(idx_ready, 1)
                    gathers(0)
                    pool.wait_ge(zeroed.h, 16 * (ST + 1))
                    step(0, 0, True)
                    step(1, 1)
                    with pool.Fori(1, (NCH - 1) // 2) as i:
                        step(2 * i, 0)
                        step(2 * i + 1, 1)
                    scatters(NCH - 1, 0)
                    ticked(fix_ready, 1)
                    pool.indirect_dma_start(
                        out=agg[:, :], out_offset=bass.IndirectOffsetOnAxis(ap=fix_i[:, 0:1], axis=0),
                        in_=fixo[:, :], in_offset=None, bounds_check=N - 1, oob_is_err=False).then_inc(scat_fix.h, 16)
                    pool.wait_ge(scat_fix.h, scat_fix.at(16))
                    pool.wait_ge(scat[0].h, scat[0].at(16 * CH * ((NCH + 1) // 2)))
                    pool.wait_ge(scat[1].h, scat[1].at(16 * CH * ((NCH - 1) // 2)))

                @block.vector
                def _(dve):
                    go = Chain(dve, dve_s)

                    def copy_at(dst_ap, src_ap):
                        dve.sem_inc(tick.h, 1)
                        return dve.tensor_copy(dst_ap, src_ap)

                    def stage(k, par):
                        if flash:
                            copy_at(di[:, par, :], dst_i[:, bass.ds(k * CH, CH)])
                        copy_at(gi[:, par, :], src_i[:, bass.ds(k * CH, CH)]).then_inc(idx_ready.h, 1)

                    def chunk(k, par, it, first=False):
                        c = bass.ds(k * CH, CH)
                        c1 = bass.ds(k * CH + 1, CH)
                        now = bass.ds(k * CH, 1)
                        g = buf[:, par, :, 0:D]
                        dve.wait_ge(gath[par].h, gath[par].at(16 * CH * (it + 1)))
                        if flash:
                            dve.wait_ge(gath_d[par].h, gath_d[par].at(16 * CH * (it + 1)))
                        stage(k + 2, par)
                        if mode == "mean":
                            if bn:
                                go(dve.tensor_tensor(wide[:, :, :], g, bc(bn_row[:, 0, :], CH), ALU.mult))
                                go(dve.tensor_tensor(wide[:, :, :], wide[:, :, :], bc(bn_row[:, 1, :], CH), ALU.add))
                                go(dve.tensor_scalar(wide[:, :, :], wide[:, :, :], 0.0, None, ALU.max))
                                terms = wide
                            else:
                                terms = buf[:, par]
                            copy_at(sc8[:, 0, :], inv_cnt[:, c])
                            go(copy_at(x4[:, 0:CH], same[:, c]))
                        else:
                            if mode == "gat":
                                go(dve.tensor_tensor(z8[:, :], buf[:, par, :, D], dpair[:, par, :, 1], ALU.add))
                                dve.tensor_tensor(sl_all[:, c], dpair[:, par, :, 0], dpair[:, par, :, 1], ALU.add)
                                go(dve.tensor_tensor(z8[:, :], z8[:, :], edge_c[:, layer, c], ALU.add))
                                go(dve.tensor_tensor(l8[:, :], sl_all[:, c], loop_c[:, layer, c], ALU.add))
                                go(dve.scalar_tensor_tensor(s8[:, :], z8[:, :], ATT_SLOPE, z8[:, :], ALU.mult, ALU.max))
                                go(dve.scalar_tensor_tensor(l8[:, :], l8[:, :], ATT_SLOPE, l8[:, :], ALU.mult, ALU.max))
                            else:
                                go(dve.tensor_tensor(wide[:, :, :], g, drows[:, par, :, 0:D], ALU.mult))
                                go(dve.tensor_reduce(z8[:, :], wide[:, :, :], AX, ALU.add))
                                go(dve.tensor_tensor(s8[:, :], z8[:, :], drows[:, par, :, D], ALU.add))
                            go(dve.tensor_tensor_scan(m_all[:, c1], pen[:, c], s8[:, :], m_all[:, now], ALU.add, ALU.max))
                            go(dve.tensor_tensor(z8[:, :], m_all[:, c], pen[:, c], ALU.add))
                            dve.tensor_tensor(e4[:, 0:CH], z8[:, :], m_all[:, c1], ALU.subtract)
                            go(dve.tensor_tensor(e4[:, CH:2 * CH], s8[:, :], m_all[:, c1], ALU.subtract))
                            ne = 2
                            if mode == "gat":
                                ne = 4
                                go(dve.tensor_tensor(z8[:, :], m_all[:, c1], l8[:, :], ALU.max))
                                dve.tensor_tensor(e4[:, 2 * CH:3 * CH], m_all[:, c1], z8[:, :], ALU.subtract)
                                go(dve.tensor_tensor(e4[:, 3 * CH:4 * CH], l8[:, :], z8[:, :], ALU.subtract))
                            dve.sem_inc(exp_in.h, 1)
                            dve.wait_ge(exp_out.h, exp_out.at(k + 1))
                            go(dve.tensor_tensor_scan(den_all[:, c1], x4[:, 0:CH], x4[:, CH:2 * CH], den_all[:, now],
                                                      ALU.mult, ALU.add))
                            if mode == "gat":
                                go(dve.tensor_tensor(z8[:, :], den_all[:, c1], x4[:, 2 * CH:3 * CH], ALU.mult))
                                go(dve.tensor_tensor(z8[:, :], z8[:, :], x4[:, 3 * CH:4 * CH], ALU.add))
                                go(dve.reciprocal(z8[:, :], z8[:, :]))
                                dve.tensor_tensor(sc8[:, 0, :], z8[:, :], x4[:, 2 * CH:3 * CH], ALU.mult)
                                go(dve.tensor_tensor(l8[:, :], z8[:, :], x4[:, 3 * CH:4 * CH], ALU.mult))
                                go(dve.tensor_scalar(sc8[:, 1, :], l8[:, :], -1.0, None, ALU.add))
                            else:
                                go(copy_at(z8[:, :], den_all[:, c1]))
                                go(dve.reciprocal(sc8[:, 0, :], z8[:, :]))
                            go(dve.tensor_tensor(wide[:, :, :], g, bl(x4[:, CH:2 * CH]), ALU.mult))
                            terms = wide
                        for j in range(CH):
                            before = state[:, par, j - 1, :] if j else state[:, 1 - par, CH - 1, :]
                            go(dve.scalar_tensor_tensor(state[:, par, j, :], before, x4[:, j:j + 1],
                                                        terms[:, j, 0:D], ALU.mult, ALU.add))
                        dve.sem_inc(rows_used.h, 1)
                        if not first:
                            dve.wait_ge(scat[par].h, scat[par].at(16 * CH * it))
                        copy_at(wi[:, par, :], scat_i[:, c])
                        if flash:
                            dve.tensor_copy(obuf[:, par, :, D], sc8[:, 1, :] if mode == "gat" else ones[:, 0:CH])
                        go(dve.tensor_tensor(obuf[:, par, :, 0:D], state[:, par, :, :], bl(sc8[:, 0, :]), ALU.mult))
                        dve.sem_inc(ob_ready.h, 1)
                        go(copy_at(z8[:, :], fixm[:, c]))
                        go(dve.tensor_tensor(wide2[:, :, :], state[:, par, :, :], bl(z8[:, :]), ALU.mult))
                        go(dve.tensor_reduce(fixt[:, :], wide2[:, :, :].rearrange("p j d -> p d j"), AX, ALU.add))
                        go(dve.tensor_tensor(fixv[:, :], fixv[:, :], fixt[:, :], ALU.add))

                    go(dve.memset(state[:, :, :, :], 0.0))
                    go(dve.memset(fixv[:, :], 0.0))
                    dve.memset(m_all[:, 0:1], -BIG)
                    go(dve.memset(den_all[:, 0:1], 0.0))
                    stage(0, 0)
                    stage(1, 1)
                    dve.wait_ge(zeroed.h, 16 * (ST + 1))
                    chunk(0, 0, 0, True)
                    chunk(1, 1, 0, True)
                    turns = (NCH - 1) // 2 - 1
                    with dve.Fori(1, (NCH - 1) // 2) as i:
                        go.enter(i - 1, PER_TURN[mode, bn], turns)
                        chunk(2 * i, 0, i)
                        chunk(2 * i + 1, 1, i)
                        go.leave()
                    chunk(NCH - 1, 0, (NCH - 1) // 2)

                    last = state[:, 0, CH - 1, :]
                    go(dve.tensor_copy(lrow[:, 0:D], last))
                    go(dve.memset(fixo[:, :], 0.0))
                    if not flash:
                        dve.sem_inc(d2p.h, 1)
                        dve.wait_ge(p2d.h, p2d.at(1))
                        go(dve.tensor_tensor(fixt[:, :], ps[0][:, 0:D], fixv[:, :], ALU.add))
                        go(dve.tensor_scalar(fixo[:, 0:D], fixt[:, :], inv_cnt_fix[:, 0:1], None, ALU.mult))
                    else:
                        go(dve.tensor_copy(lrow[:, D:D + 1], den_all[:, COLS:COLS + 1]))
                        go(dve.tensor_scalar(wq[:, :], ones[:, :], m_all[:, COLS:COLS + 1], None, ALU.mult))
                        dve.sem_inc(d2p.h, 1)
                        for k, a in ((0, m_all[:, 1:COLS + 1]), (1, den_all[:, 1:COLS + 1]), (2, sl_all[:, :])):
                            if k < 2 or mode == "gat":
                                go(dve.tensor_tensor_reduce(zrow[:, :], fixm[:, :], a, 1.0, 0.0, ALU.mult, ALU.add,
                                                            fx[:, k:k + 1]))
                        dve.wait_ge(p2d.h, p2d.at(1))
                        go(dve.tensor_tensor(wq[:, :], ps[0][:, 0:P], chain_pen[:, :], ALU.add))
                        go(dve.tensor_reduce(fx[:, 3:4], wq[:, :], AX, ALU.max))
                        go(dve.tensor_tensor(fx[:, 3:4], fx[:, 3:4], fx[:, 0:1], ALU.max))
                        if mode == "gat":
                            go(dve.tensor_tensor(fx[:, 2:3], fx[:, 2:3], loop_fix[:, layer:layer + 1], ALU.add))
                            go(dve.scalar_tensor_tensor(fx[:, 2:3], fx[:, 2:3], ATT_SLOPE, fx[:, 2:3], ALU.mult,
                                                        ALU.max))
                            go(dve.tensor_tensor(fx[:, 3:4], fx[:, 3:4], fx[:, 2:3], ALU.max))
                            go(dve.tensor_tensor(fx[:, 5:6], fx[:, 2:3], fx[:, 3:4], ALU.subtract))
                        else:
                            go(dve.memset(fx[:, 5:6], -BIG))
                        go(dve.tensor_scalar(wq[:, :], wq[:, :], fx[:, 3:4], None, ALU.subtract))
                        go(dve.tensor_tensor(fx[:, 4:5], fx[:, 0:1], fx[:, 3:4], ALU.subtract))
                        dve.sem_inc(exp_in.h, 1)
                        dve.wait_ge(p2d.h, p2d.at(2))
                        go(dve.tensor_copy(wqt[:, :], ps[1][:, 0:P]))
                        dve.sem_inc(d2p.h, 1)
                        dve.wait_ge(p2d.h, p2d.at(3))
                        go(dve.tensor_scalar(fx[:, 8:9], fx[:, 1:2], fx[:, 6:7], None, ALU.mult))
                        go(dve.tensor_tensor(fx[:, 8:9], ps[0][:, D:D + 1], fx[:, 8:9], ALU.add))
                        go(dve.tensor_tensor(fx[:, 8:9], fx[:, 8:9], fx[:, 7:8], ALU.add))
                        go(dve.tensor_scalar(fx[:, 8:9], fx[:, 8:9], 1.0e-30, None, ALU.max))
                        go(dve.reciprocal(fx[:, 9:10], fx[:, 8:9]))
                        go(dve.scalar_tensor_tensor(fixt[:, :], fixv[:, :], fx[:, 6:7], ps[0][:, 0:D], ALU.mult, ALU.add))
                        go(dve.tensor_scalar(fixo[:, 0:D], fixt[:, :], fx[:, 9:10], None, ALU.mult))
                        if mode == "gat":
                            go(dve.tensor_tensor(fx[:, 10:11], fx[:, 7:8], fx[:, 9:10], ALU.mult))
                            go(dve.tensor_scalar(fixo[:, D:D + 1], fx[:, 10:11], -1.0, None, ALU.add))
                        else:
                            go(dve.memset(fixo[:, D:D + 1], 1.0))
                    dve.sem_inc(fix_ready.h, 1)
                    dve_s.total = go.total

                if flash:
                    @block.scalar
                    def _(act):
                        n = (4 if mode == "gat" else 2) * CH

                        def exps(k):
                            act.wait_ge(exp_in.h, exp_in.at(k + 1))
                            act.activation(x4[:, 0:n], e4[:, 0:n], ACT.Exp).then_inc(exp_out.h, 1)
                        with act.Fori(0, NCH) as k:
                            exps(k)
                        act.wait_ge(exp_in.h, exp_in.at(NCH + 1))
                        act.activation(wqt[:, :], wq[:, :], ACT.Exp)
                        act.activation(fx[:, 6:8], fx[:, 4:6], ACT.Exp).then_inc(exp_out.h, 1)
                        act.wait_ge(exp_out.h, exp_out.at(NCH + 1))
                        act.sem_inc(a2p.h, 1)

                @block.tensor
                def _(pe):
                    if not flash:
                        pe.wait_ge(d2p.h, d2p.at(1))
                        pe.matmul(ps[0][:, 0:D], chain_m[:, :], lrow[:, 0:D], start=True, stop=True).then_inc(p2d.h, 1)
                    else:
                        pe.wait_ge(d2p.h, d2p.at(1))
                        pe.transpose(ps[0][:, 0:P], wq[:, :], ident[:, :]).then_inc(p2d.h, 1)
                        pe.wait_ge(a2p.h, a2p.at(1))
                        pe.transpose(ps[1][:, 0:P], wqt[:, :], ident[:, :]).then_inc(p2d.h, 1)
                        pe.wait_ge(d2p.h, d2p.at(2))
                        pe.matmul(ps[0][:, 0:D + 1], wqt[:, :], lrow[:, :], start=True, stop=True).then_inc(p2d.h, 1)

            dve_s.base += dve_s.total
            idx_ready.base += NCH + 2
            rows_used.base += NCH
            ob_ready.base += NCH
            fix_ready.base += 1
            scat_fix.base += 16
            for par, n in ((0, (NCH + 1) // 2), (1, (NCH - 1) // 2)):
                gath[par].base += 16 * CH * n
                scat[par].base += 16 * CH * n
                if flash:
                    gath_d[par].base += 16 * CH * n
            if flash:
                exp_in.base += NCH + 1
                exp_out.base += NCH + 1
                a2p.base += 1
                d2p.base += 2
                p2d.base += 3
            else:
                d2p.base += 1
                p2d.base += 1

        PER_TURN = {("mean", False): 2 * (1 + CH + 1 + 4), ("mean", True): 2 * (4 + CH + 1 + 4),
                    ("att", False): 2 * (3 + 3 + 4 + CH + 1 + 4), ("gat", False): 2 * (5 + 3 + 2 + 7 + CH + 1 + 4)}

        def node_pass(mode, h_tab, out_tab, extra=None, bn=False, layer=0):
            has_agg = products = mode != "skip"
            mid = mode == "gat" and 1 <= layer <= 3
            loops = mode in ("gat", "last")
            two = mode in ("sage", "mean", "att") or mid
            normed = mode in ("skip", "mean", "att", "last")
            second = "dots" if mid else {"mean": "keys", "att": "scal", "gat": "scal"}.get(mode)
            turned = second in ("keys", "scal")
            loads = 1 + has_agg + (extra is not None)
            stores = 1 + (second is not None)
            o_w = out_tab.shape[1]
            same_x0 = mid and layer == 1
            score_l = 0 if mode == "att" else layer + 1
            if mode == "sage":
                w1, w2 = sage_r[:, layer, :], sage_l[:, layer, :]
            elif mode == "mean":
                w1, w2 = mean_w[:, 0, :], mean_w[:, 1, :]
            elif mode == "att":
                w1, w2 = att_w[:, 0, :], att_w[:, 1, :]
            elif loops:
                w1 = gat_w[:, layer, :]
                w2 = mid_w[:, layer - 1, :] if mid else None
            bias = gat_b[:, layer] if loops else None
            B = 1 if loops else 0
            R = 6 if normed else 3 + B
            DEPTH = {"sage": 3, "skip": 5, "mean": R + 2, "att": R + 2, "gat": R + 2, "last": 5 + B}[mode]
            assert DEPTH <= 2 * NG
            turn_banks = [2] if second == "keys" else [2, 7]
            NTB = len(turn_banks)
            readers = {"sage": (th_done, tr_done), "skip": (pre_ready, rows_ready), "mean": (th_done, tr_done, pre_ready),
                       "att": (th_done, tr_done, pre_ready), "last": (y_ready, pre_ready),
                       "gat": (y_ready, tr_done) if mid else (y_ready,)}[mode]
            finished = m2_read if second else out_ready
            done = {"sage": 2, "skip": 5, "last": 5 + B}.get(mode, R + 2)
            HLAG = (done - B + 8) // 2
            assert HLAG <= 8
            FULL = ST // 2

            def tiles(buf, u):
                return buf[:, u.par, u.g * GT:(u.g + 1) * GT, 0:D]

            def rows_of(tab, s, half, parts):
                rows = tab[bass.ds(s * SUP, parts * G), :].rearrange("(p g) w -> p g w", p=parts)
                return rows[:, half * GH:(half + 1) * GH, :]

            def group(it, n, lag):
                m = n - lag
                if isinstance(it, int):
                    q = 2 * NG * it + m
                    if not 0 <= q < NGR:
                        return None
                    it, m = q // (2 * NG), q % (2 * NG)
                    return Group(q, it, m // NG, m % NG, m, LASTP if q >= NG * ST else P, q)
                back = m < 0
                return Group(it * (2 * NG) + m, it - 1 if back else it, m % (2 * NG) // NG, m % NG, m % (2 * NG), P,
                             4 * NG)

            def walk(eng, slot, depth, chain=None, per=0):
                for n in range(4 * NG):
                    slot(0, n)
                with eng.Fori(2, FULL) as i:
                    if chain is not None:
                        chain.enter(i - 2, per, FULL - 2)
                    for n in range(2 * NG):
                        slot(i, n)
                    if chain is not None:
                        chain.leave()
                for n in range(NG + depth):
                    slot(FULL, n)

            with nc.Block() as block:
                @block.sync
                def _(sp):
                    def fetch(s, par, half, parts, waits):
                        if waits:
                            for r in readers:
                                sp.wait_ge(r.h, r.at(NG * (s - 1) - (NG // 2 if half == 0 else 0)))
                                sp.sem_inc(tick.h, 1)
                        g = slice(half * GH, (half + 1) * GH)
                        for tab, b in ((h_tab, in_h), (agg if has_agg else None, in_r), (extra, in_e)):
                            if tab is not None:
                                sp.dma_start(b[0:parts, par, g, 0:tab.shape[1]], rows_of(tab, s, half, parts))\
                                  .then_inc(ld[par][half].h, 16)

                    def put(s, par, half, parts):
                        sp.wait_ge(finished.h, finished.at(NG * s + NG // 2 * (half + 1)))
                        sp.sem_inc(tick.h, 1)
                        g = slice(half * GH, (half + 1) * GH)
                        done_sem = stq[par][half].h
                        sp.dma_start(rows_of(out_tab, s, half, parts), outb[0:parts, par, g, 0:o_w]).then_inc(done_sem, 16)
                        if second == "keys":
                            sp.dma_start(rows_of(tab_u, s, half, parts), outu[0:parts, par, g, :]).then_inc(done_sem, 16)
                        if second in ("scal", "dots"):
                            sp.dma_start(rows_of(pair_tab, s, half, parts), outp[0:parts, par, g, :])\
                              .then_inc(done_sem, 16)

                    for h in range(8):
                        fetch(h // 2, h // 2 % 2, h % 2, P, h >= 4)
                        if h >= HLAG:
                            b = h - HLAG
                            put(b // 2, b // 2 % 2, b % 2, P)
                    with sp.Fori(2, FULL) as i:
                        for h in range(4):
                            fetch(2 * i + h // 2, h // 2, h % 2, P, True)
                            b = h - HLAG
                            put(2 * i + b // 2, b // 2 % 2, b % 2, P)
                    for h in range(2 * ST, 2 * ST + 2 + HLAG):
                        if h < 2 * ST + 2:
                            fetch(ST, 0, h % 2, LASTP, True)
                        b = h - HLAG
                        put(b // 2, b // 2 % 2, b % 2, LASTP if b >= 2 * ST else P)
                    for half in range(2):
                        sp.wait_ge(stq[0][half].h, stq[0][half].at(16 * stores * (FULL + 1)))
                        sp.wait_ge(stq[1][half].h, stq[1][half].at(16 * stores * FULL))

                @block.gpsimd
                def _(pool):
                    go = Chain(pool, pool_s)

                    def pre(u):
                        xb = xbuf[:, u.m % 4]
                        pool.wait_ge(ld[u.par][u.half].h, ld[u.par][u.half].at(16 * loads * (u.it + 1)))
                        if u.past >= 4:
                            pool.wait_ge(var_ready.h, var_ready.at(u.q - 3))
                        if mode == "skip":
                            go(pool.tensor_tensor(xb, tiles(in_h, u), bc(bn_row[:, 0, :], GT), ALU.mult))
                            pool.tensor_tensor(xb, xb, bc(bn_row[:, 1, :], GT), ALU.add).then_inc(pre_ready.h, 1)
                        if mode == "mean":
                            pool.tensor_tensor(xb, tiles(in_h, u), mean_b[:, :, :], ALU.add).then_inc(pre_ready.h, 1)
                        if mode == "att":
                            col = in_r[:, u.par, u.g * GT:(u.g + 1) * GT, D]
                            go(pool.tensor_tensor(xb, bc(att_mb[:, :], GT), bl(col), ALU.mult))
                            go(pool.tensor_tensor(xb, xb, tiles(in_h, u), ALU.add))
                            pool.tensor_tensor(xb, xb, att_b[:, :, :], ALU.add).then_inc(pre_ready.h, 1)
                        if mode == "last":
                            pool.tensor_tensor(xb, tiles(in_e, u), bias, ALU.add).then_inc(pre_ready.h, 1)

                    def total(u):
                        pool.wait_ge(out_ready.h, out_ready.at(u.q + 1))
                        go(pool.tensor_tensor(acc[0:u.parts, 0], tiles(outb, u)[0:u.parts], acc[0:u.parts, 0], ALU.add))
                        pool.sem_inc(sum_ready.h, 1)

                    def weigh(u):
                        pool.wait_ge(out_ready.h, out_ready.at(u.q + 1))
                        if u.past >= 2:
                            pool.wait_ge(src_ready.h, src_ready.at(u.q - 1))
                            pool.wait_ge(dst_ready.h, dst_ready.at(u.q - 1))
                        for s in range(2):
                            ins = pool.tensor_tensor(xbuf[:, u.m % 2 * 2 + s], tiles(outb, u),
                                                     bc(gat_s_row[:, score_l - 2, s, :], GT), ALU.mult)
                        ins.then_inc(weighed.h, 1)

                    def slot(it, n):
                        if normed and (u := group(it, n, 0)):
                            pre(u)
                        if second == "dots" and (u := group(it, n, R)):
                            weigh(u)
                        if mode == "sage" and (u := group(it, n, 3)):
                            total(u)
                    per = 2 * NG * {"skip": 1, "att": 2, "sage": 1}.get(mode, 0)
                    if mode == "sage":
                        go(pool.memset(acc[:, 0], 0.0))
                    if mode != "gat" or mid:
                        walk(pool, slot, DEPTH, go, per)
                    pool_s.total = go.total

                @block.tensor
                def _(pe):
                    def turn(u):
                        if u.first:
                            pe.wait_ge(ld[u.par][u.half].h, ld[u.par][u.half].at(16 * loads * (u.it + 1)))
                        if loops:
                            pe.wait_ge(y_ready.h, y_ready.at(u.q + 1))
                        if u.past >= 2:
                            pe.wait_ge(ht_ready.h, ht_ready.at(u.q - 1))
                        for k in range(GT):
                            a = yb[:, u.m % 2, k, :] if loops else in_h[:, u.par, u.g * GT + k, 0:D]
                            mm = pe.transpose(ps[u.m % 2][:, k * D:(k + 1) * D], a, ident[:, :])
                        mm.then_inc(th_done.h, 1)
                        if two:
                            if u.past >= NTB:
                                pe.wait_ge(rt_ready.h, rt_ready.at(u.q + 1 - NTB))
                            b = in_r if not mid else (in_h if same_x0 else in_e)
                            o = ps[turn_banks[u.m % NTB]]
                            for k in range(GT):
                                mm = pe.transpose(o[:, k * D:(k + 1) * D], b[:, u.par, u.g * GT + k, 0:D], ident[:, :])
                            mm.then_inc(tr_done.h, 1)

                    def product(u):
                        pe.wait_ge(ht_ready.h, ht_ready.at(u.q + 1))
                        if two:
                            pe.wait_ge(rt_ready.h, rt_ready.at(u.q + 1))
                        if u.past >= 2:
                            used = sq_ready if mode == "sage" else post_read
                            pe.wait_ge(used.h, used.at(u.q - 1))
                        for k in range(GT):
                            o = ps[3 + u.m % 2][:, k * D:(k + 1) * D]
                            mm = pe.matmul(o, ht[:, u.m % 2, k, :], w1, start=True, stop=not two)
                            if two:
                                mm = pe.matmul(o, rt[:, u.m % 2, k, :], w2, start=False, stop=True)
                        mm.then_inc(mm_done.h, 1)

                    def turn_out(u):
                        pe.wait_ge(out_ready.h, out_ready.at(u.q + 1))
                        if u.past >= 1:
                            pe.wait_ge(ot_ready.h, ot_ready.at(u.q))
                        for k in range(GT):
                            mm = pe.transpose(ps[5][:, k * D:(k + 1) * D], outb[:, u.par, u.g * GT + k, 0:D], ident[:, :])
                        mm.then_inc(t2_done.h, 1)

                    def product_out(u):
                        pe.wait_ge(ot_ready.h, ot_ready.at(u.q + 1))
                        if u.past >= 1:
                            pe.wait_ge(m2_read.h, m2_read.at(u.q))
                        for k in range(GT):
                            a = ot[:, u.m % 2, k, :]
                            if second == "keys":
                                mm = pe.matmul(ps[6 + k // 2][:, (k % 2) * 256:(k % 2) * 256 + D + 1], a, key_w[:, :],
                                               start=True, stop=True)
                            else:
                                mm = pe.matmul(ps[6][:, 2 * k:2 * k + 2], a, gat_s[:, score_l, :], start=True, stop=True)
                        mm.then_inc(m2_done.h, 1)

                    def slot(it, n):
                        if u := group(it, n, B):
                            turn(u)
                        if u := group(it, n, 1 + B):
                            product(u)
                        if turned and (u := group(it, n, R)):
                            turn_out(u)
                        if turned and (u := group(it, n, R + 1)):
                            product_out(u)
                    if products:
                        walk(pe, slot, DEPTH)

                @block.scalar
                def _(act):
                    def lift(u):
                        act.wait_ge(th_done.h, th_done.at(u.q + 1))
                        if u.past >= 2:
                            act.wait_ge(mm_done.h, mm_done.at(u.q - 1))
                        f = ht[:, u.m % 2, :, :].rearrange("p k d -> p (k d)")
                        if bn:
                            act.activation(f, ps[u.m % 2][:, :], ACT.Relu, bias=bn_col[:, 1:2],
                                           scale=bn_col[:, 0:1]).then_inc(ht_ready.h, 1)
                        else:
                            act.copy(f, ps[u.m % 2][:, :]).then_inc(ht_ready.h, 1)
                        if two and mode != "sage":
                            act.wait_ge(tr_done.h, tr_done.at(u.q + 1))
                            act.copy(rt[:, u.m % 2, :, :].rearrange("p k d -> p (k d)"),
                                     ps[turn_banks[u.m % NTB]][:, :]).then_inc(rt_ready.h, 1)

                    def raw_out(u):
                        act.wait_ge(mm_done.h, mm_done.at(u.q + 1))
                        if u.first and u.past >= 2 * NG:
                            act.wait_ge(stq[u.par][u.half].h, stq[u.par][u.half].at(16 * stores * u.it))
                            act.wait_ge(sum_ready.h, sum_ready.at(u.q - 2 * NG + NG // 2))
                        act.copy(tiles(outb, u), ps[3 + u.m % 2][:, :].rearrange("p (k d) -> p k d", k=GT))\
                           .then_inc(out_ready.h, 1)
                        if u.past >= 2:
                            act.wait_ge(norm_ready.h, norm_ready.at(u.q - 1))
                        act.activation(ps[5 + u.m % 2][:, :], ps[3 + u.m % 2][:, :], ACT.Square).then_inc(sq_ready.h, 1)

                    def root(u):
                        act.wait_ge(var_ready.h, var_ready.at(u.q + 1))
                        act.activation(std[:, u.m % 4, :], mv[:, u.m % 4, :, 1], ACT.Sqrt).then_inc(std_ready.h, 1)

                    def scale(u):
                        act.wait_ge(norm_ready.h, norm_ready.at(u.q + 1))
                        if u.first and u.past >= 2 * NG:
                            act.wait_ge(stq[u.par][u.half].h, stq[u.par][u.half].at(16 * stores * u.it))
                        for k in range(GT):
                            ins = act.activation(outb[:, u.par, u.g * GT + k, 0:D], ub[:, u.m % 4, k, :], ACT.Identity,
                                                 bias=mv[:, u.m % 4, k, 0:1], scale=mv[:, u.m % 4, k, 1:2])
                        ins.then_inc(out_ready.h, 1)

                    def sum_dst(u):
                        act.wait_ge(weighed.h, weighed.at(u.q + 1))
                        if u.first and u.past >= 2 * NG:
                            act.wait_ge(stq[u.par][u.half].h, stq[u.par][u.half].at(16 * stores * u.it))
                        for k in range(GT):
                            c = u.g * GT + k
                            row = xbuf[:, u.m % 2 * 2 + 1, k, :]
                            ins = act.activation(row, row, ACT.Identity, accum_out=outp[:, u.par, c, 1:2])
                        ins.then_inc(dst_ready.h, 1)

                    def lift_out(u):
                        act.wait_ge(t2_done.h, t2_done.at(u.q + 1))
                        if u.past >= 2:
                            act.wait_ge(m2_done.h, m2_done.at(u.q - 1))
                        act.copy(ot[:, u.m % 2, :, :].rearrange("p k d -> p (k d)"), ps[5][:, :])\
                           .then_inc(ot_ready.h, 1)

                    def slot(it, n):
                        if products and (u := group(it, n, B)):
                            lift(u)
                        if mode == "sage" and (u := group(it, n, 2)):
                            raw_out(u)
                        if normed and (u := group(it, n, 3 + B)):
                            root(u)
                        if normed and (u := group(it, n, 5 + B)):
                            scale(u)
                        if mid and (u := group(it, n, R + 1)):
                            sum_dst(u)
                        if turned and (u := group(it, n, R)):
                            lift_out(u)
                    walk(act, slot, DEPTH)

                @block.vector
                def _(dve):
                    go = Chain(dve, dve_s)

                    def join(u):
                        if u.first:
                            dve.wait_ge(ld[u.par][u.half].h, ld[u.par][u.half].at(16 * loads * (u.it + 1)))
                            g = slice(u.half * GH, (u.half + 1) * GH)
                            go(dve.tensor_scalar(col1[:, u.par, g], in_r[:, u.par, g, D], 1.0, None, ALU.add))
                        if u.past >= 2:
                            dve.wait_ge(th_done.h, th_done.at(u.q - 1))
                        for k in range(GT):
                            c = u.g * GT + k
                            ins = dve.scalar_tensor_tensor(yb[:, u.m % 2, k, :], in_h[:, u.par, c, 0:D],
                                                           col1[:, u.par, c:c + 1], in_r[:, u.par, c, 0:D],
                                                           ALU.mult, ALU.add)
                        ins.then_inc(y_ready.h, 1)

                    def lift_agg(u):
                        dve.wait_ge(tr_done.h, tr_done.at(u.q + 1))
                        if u.past >= 2:
                            dve.wait_ge(mm_done.h, mm_done.at(u.q - 1))
                        dve.tensor_copy(rt[:, u.m % 2, :, :].rearrange("p k d -> p (k d)"),
                                        ps[turn_banks[u.m % NTB]][:, :]).then_inc(rt_ready.h, 1)

                    def squares(u):
                        dve.wait_ge(sq_ready.h, sq_ready.at(u.q + 1))
                        go(dve.tensor_tensor(acc[0:u.parts, 1],
                                             ps[5 + u.m % 2][0:u.parts, :].rearrange("p (k d) -> p k d", k=GT),
                                             acc[0:u.parts, 1], ALU.add))
                        dve.sem_inc(norm_ready.h, 1)

                    def post(u):
                        o3 = ps[3 + u.m % 2][:, :].rearrange("p (k d) -> p k d", k=GT)
                        w = ub[:, u.m % 4, :, :]
                        xb = xbuf[:, u.m % 4]
                        if products:
                            dve.wait_ge(mm_done.h, mm_done.at(u.q + 1))
                        if mid:
                            dve.tensor_tensor(w, o3, bias, ALU.add).then_inc(post_read.h, 1)
                            return
                        if mode == "gat":
                            if u.first and u.past >= 2 * NG:
                                dve.wait_ge(stq[u.par][u.half].h, stq[u.par][u.half].at(16 * stores * u.it))
                            go(dve.tensor_tensor(tiles(outb, u), o3, bias, ALU.add))
                            dve.sem_inc(post_read.h, 1)
                            dve.sem_inc(out_ready.h, 1)
                            return
                        if u.past >= 4:
                            dve.wait_ge(out_ready.h, out_ready.at(u.q - 3))
                        if mode == "mean":
                            dve.tensor_tensor(w, o3, mean_nb[:, :, :], ALU.max).then_inc(post_read.h, 1)
                            return
                        dve.wait_ge(pre_ready.h, pre_ready.at(u.q + 1))
                        if mode == "skip":
                            dve.scalar_tensor_tensor(w, xb, 0.0, tiles(in_e, u), ALU.max, ALU.add)\
                               .then_inc(rows_ready.h, 1)
                        else:
                            dve.tensor_tensor(w, o3, xb, ALU.add).then_inc(post_read.h, 1)

                    def leak(u):
                        w = ub[:, u.m % 4, :, :]
                        dve.wait_ge(post_read.h, post_read.at(u.q + 1))
                        if u.first and u.past >= 2 * NG:
                            dve.wait_ge(stq[u.par][u.half].h, stq[u.par][u.half].at(16 * stores * u.it))
                        dve.scalar_tensor_tensor(tiles(outb, u), w, SLOPE, w, ALU.mult, ALU.max)\
                           .then_inc(out_ready.h, 1)

                    def stats(u):
                        if mode == "mean":
                            dve.wait_ge(post_read.h, post_read.at(u.q + 1))
                            dve.wait_ge(pre_ready.h, pre_ready.at(u.q + 1))
                            dve.tensor_tensor(ub[:, u.m % 4, :, :], ub[:, u.m % 4, :, :], xbuf[:, u.m % 4], ALU.add)\
                               .then_inc(rows_ready.h, 1)
                        made = rows_ready if mode in ("skip", "mean") else post_read
                        dve.wait_ge(made.h, made.at(u.q + 1))
                        for k in range(GT):
                            ins = dve.bn_stats(st6[:, k, :], ub[:, u.m % 4, k, :])
                        ins.then_inc(stats_ready.h, 1)

                    def aggregate(u):
                        dve.wait_ge(stats_ready.h, stats_ready.at(u.q + 1))
                        dve.sem_inc(tick.h, 1)
                        for k in range(GT):
                            ins = dve.bn_aggr(mv[:, u.m % 4, k, :], st6[:, k, :])
                        ins.then_inc(aggr_ready.h, 1)

                    def add_eps(u):
                        dve.wait_ge(aggr_ready.h, aggr_ready.at(u.q + 1))
                        dve.tensor_scalar(mv[:, u.m % 4, :, 1], mv[:, u.m % 4, :, 1], EPS, None, ALU.add)\
                           .then_inc(var_ready.h, 1)

                    def invert(u):
                        dve.wait_ge(std_ready.h, std_ready.at(u.q + 1))
                        dve.reciprocal(mv[:, u.m % 4, :, 1], std[:, u.m % 4, :]).then_inc(recip_ready.h, 1)

                    def norm(u):
                        dve.wait_ge(recip_ready.h, recip_ready.at(u.q + 1))
                        dve.scalar_tensor_tensor(mv[:, u.m % 4, :, 0], mv[:, u.m % 4, :, 0], -1.0, mv[:, u.m % 4, :, 1],
                                                 ALU.mult, ALU.mult).then_inc(norm_ready.h, 1)

                    def scalars(u):
                        dve.wait_ge(m2_done.h, m2_done.at(u.q + 1))
                        if u.first and u.past >= 2 * NG:
                            dve.wait_ge(stq[u.par][u.half].h, stq[u.par][u.half].at(16 * stores * u.it))
                        if second == "keys":
                            for k in range(GT):
                                ins = dve.tensor_tensor(outu[:, u.par, u.g * GT + k, 0:D + 1],
                                                        ps[6 + k // 2][:, (k % 2) * 256:(k % 2) * 256 + D + 1],
                                                        key_b[:, :], ALU.add)
                            ins.then_inc(m2_read.h, 1)
                        else:
                            sv = ps[6][:, 0:2 * GT].rearrange("p (k s) -> p k s", s=2)
                            dve.tensor_copy(outb[:, u.par, u.g * GT:(u.g + 1) * GT, D:D + 2], sv)
                            dve.tensor_copy(outp[:, u.par, u.g * GT:(u.g + 1) * GT, :], sv).then_inc(m2_read.h, 1)

                    def sum_src(u):
                        dve.wait_ge(weighed.h, weighed.at(u.q + 1))
                        if u.first and u.past >= 2 * NG:
                            dve.wait_ge(stq[u.par][u.half].h, stq[u.par][u.half].at(16 * stores * u.it))
                        dve.tensor_reduce(outp[:, u.par, u.g * GT:(u.g + 1) * GT, 0], xbuf[:, u.m % 2 * 2], AX,
                                          ALU.add).then_inc(src_ready.h, 1)

                    def join_scalars(u):
                        dve.wait_ge(src_ready.h, src_ready.at(u.q + 1))
                        dve.wait_ge(dst_ready.h, dst_ready.at(u.q + 1))
                        dve.tensor_copy(outb[:, u.par, u.g * GT:(u.g + 1) * GT, D:D + 2],
                                        outp[:, u.par, u.g * GT:(u.g + 1) * GT, :]).then_inc(m2_read.h, 1)

                    def slot(it, n):
                        if normed and (u := group(it, n, 4 + B)):
                            invert(u)
                        if normed and (u := group(it, n, 3 + B)):
                            aggregate(u)
                        if mode != "sage" and (mode != "gat" or mid) and (u := group(it, n, 2 + B)):
                            post(u)
                        if normed and (u := group(it, n, 4 + B)):
                            norm(u)
                        if normed and (u := group(it, n, 3 + B)):
                            add_eps(u)
                        if turned and (u := group(it, n, R + 2)):
                            scalars(u)
                        if mid and (u := group(it, n, R + 2)):
                            join_scalars(u)
                        if mid and (u := group(it, n, R + 1)):
                            sum_src(u)
                        if loops and (u := group(it, n, 0)):
                            join(u)
                        if mode == "sage" and (u := group(it, n, 0)):
                            lift_agg(u)
                        if mode == "sage" and (u := group(it, n, 3)):
                            squares(u)
                        if mode == "gat" and not mid and (u := group(it, n, 2 + B)):
                            post(u)
                        if mid and (u := group(it, n, 2 + B)):
                            leak(u)
                        if normed and (u := group(it, n, 2 + B)):
                            stats(u)
                    per = 2 * NG if mode == "sage" or (mode == "gat" and not mid) else 0
                    per += 4 if loops else 0
                    if mode == "sage":
                        go(dve.memset(acc[:, 1], 0.0))
                    walk(dve, slot, DEPTH, go, per)
                    dve_s.total = go.total

            dve_s.base += dve_s.total
            pool_s.base += pool_s.total
            for par, n in ((0, FULL + 1), (1, FULL)):
                for half in range(2):
                    ld[par][half].base += 16 * loads * n
                    stq[par][half].base += 16 * stores * n
            used = [out_ready]
            if products:
                used += [th_done, ht_ready, mm_done]
                if mode != "sage":
                    used += [post_read]
            if loops:
                used += [y_ready]
            if two:
                used += [tr_done, rt_ready]
            if turned:
                used += [t2_done, ot_ready, m2_done, m2_read]
            if mid:
                used += [weighed, src_ready, dst_ready, m2_read]
            if mode == "sage":
                used += [sq_ready, sum_ready, norm_ready]
            if normed:
                used += [norm_ready, var_ready, std_ready, pre_ready, stats_ready, aggr_ready, recip_ready]
            if mode in ("skip", "mean"):
                used += [rows_ready]
            for s in used:
                s.base += NGR

        def batch_norm(layer):
            b, gamma, beta = (bn_par[:, k, layer:layer + 1] for k in range(3))
            with nc.Block() as block:
                @block.scalar
                def _(act):
                    act.wait_ge(d2a.h, d2a.at(1))
                    act.activation(sums[:, 4:5], sums[:, 2:3], ACT.Sqrt).then_inc(a2d.h, 1)

                @block.tensor
                def _(pe):
                    for s in range(2):
                        for k in range(GT):
                            mm = pe.matmul(ps[s][:, 0:1], acc[:, s, k, :], ones[:, 0:1], start=(k == 0),
                                           stop=(k == GT - 1))
                    mm.then_inc(p2d.h, 1)
                    pe.wait_ge(d2p.h, d2p.at(1))
                    pe.transpose(ps[2][:, 0:D], wq[:, :], ident[:, :])
                    pe.transpose(ps[2][:, D:2 * D], wqt[:, :], ident[:, :]).then_inc(p2d.h, 1)

                @block.vector
                def _(dve):
                    go = Chain(dve, dve_s)
                    mean, sq, var, full = (sums[:, k:k + 1] for k in range(4))
                    dve.wait_ge(p2d.h, p2d.at(1))
                    go(dve.tensor_scalar(mean, ps[0][:, 0:1], 1.0 / N, None, ALU.mult))
                    go(dve.tensor_scalar(sq, ps[1][:, 0:1], 1.0 / N, None, ALU.mult))
                    go(dve.tensor_tensor(var, mean, mean, ALU.mult))
                    go(dve.tensor_tensor(var, sq, var, ALU.subtract))
                    go(dve.tensor_scalar(var, var, 0.0, None, ALU.max))
                    go(dve.tensor_scalar(var, var, EPS, None, ALU.add))
                    dve.sem_inc(d2a.h, 1)
                    dve.wait_ge(a2d.h, a2d.at(1))
                    go(dve.reciprocal(var, sums[:, 4:5]))
                    go(dve.tensor_tensor(bn_col[:, 0:1], gamma, var, ALU.mult))
                    go(dve.tensor_tensor(full, mean, b, ALU.add))
                    go(dve.tensor_tensor(full, b, full, ALU.subtract))
                    go(dve.tensor_tensor(full, full, bn_col[:, 0:1], ALU.mult))
                    go(dve.tensor_tensor(bn_col[:, 1:2], full, beta, ALU.add))
                    go(dve.tensor_scalar(wq[:, :], ones[:, :], bn_col[:, 0:1], None, ALU.mult))
                    go(dve.tensor_scalar(wqt[:, :], ones[:, :], bn_col[:, 1:2], None, ALU.mult))
                    dve.sem_inc(d2p.h, 1)
                    dve.wait_ge(p2d.h, p2d.at(2))
                    go(dve.tensor_copy(bn_row[:, 0, :], ps[2][:, 0:D]))
                    go(dve.tensor_copy(bn_row[:, 1, :], ps[2][:, D:2 * D]))
                    dve_s.total = go.total
            dve_s.base += dve_s.total
            p2d.base += 2
            d2p.base += 1
            d2a.base += 1
            a2d.base += 1

        x = t["x"]
        edge_pass("mean", x)
        node_pass("sage", x, tab_a, layer=0)
        batch_norm(0)
        edge_pass("mean", tab_a, bn=True)
        node_pass("sage", tab_a, tab_b, bn=True, layer=1)
        batch_norm(1)
        edge_pass("mean", tab_b, bn=True)
        node_pass("sage", tab_b, tab_a, bn=True, layer=2)
        batch_norm(2)
        node_pass("skip", tab_a, tab_b, extra=x)
        edge_pass("mean", tab_b)
        node_pass("mean", tab_b, tab_a)
        edge_pass("att", tab_a)
        node_pass("att", tab_a, tab_b)
        edge_pass("gat", tab_b, layer=0)
        node_pass("gat", tab_b, tab_x0, layer=0)
        edge_pass("gat", tab_x0, layer=1)
        node_pass("gat", tab_x0, tab_a, layer=1)
        edge_pass("gat", tab_a, layer=2)
        node_pass("gat", tab_a, tab_u, extra=tab_x0, layer=2)
        edge_pass("gat", tab_u, layer=3)
        node_pass("gat", tab_u, tab_a, extra=tab_x0, layer=3)
        edge_pass("gat", tab_a, layer=4)
        node_pass("last", tab_a, out, extra=tab_b, layer=4)


_INS = ['x', 'src', 'dst', 'edge_attr_16', 'L0_gnn_Wl', 'L0_gnn_Wr', 'L0_gnn_b', 'L0_gnn_gamma', 'L0_gnn_beta',
        'L1_gnn_W_self', 'L1_gnn_b_self', 'L1_gnn_W_neigh', 'L1_gnn_b_neigh', 'L2_gnn_W_w', 'L2_gnn_W_b',
        'L2_gnn_WS_w', 'L2_gnn_WS_b', 'L2_gnn_q_w', 'L2_gnn_q_b', 'L2_gnn_k_w', 'L2_gnn_k_b', 'L3_gnn_Ws',
        'L3_gnn_Wes', 'L3_gnn_a_srcs', 'L3_gnn_a_dsts', 'L3_gnn_a_edges', 'L3_gnn_biases', 'L3_gnn_mid_ws']


def kernel(**inputs):
    import numpy as _np
    import concourse.bacc as _bacc
    from concourse import mybir as _mybir
    from concourse.bass_utils import run_bass_kernel_spmd as _run

    nc = _bacc.Bacc("TRN2", target_bir_lowering=False, num_devices=1)
    arrays, aps = {}, {}
    for name in _INS:
        a = _np.ascontiguousarray(inputs[name])
        arrays[f"in_{name}_dram"] = a
        aps[name] = nc.dram_tensor(f"in_{name}_dram", a.shape, _mybir.dt.from_np(a.dtype), kind="ExternalInput").ap()
    shape = tuple(inputs["x"].shape)
    out = nc.dram_tensor("out_0_dram", shape, _mybir.dt.float32, kind="ExternalOutput").ap()
    gnn(nc, aps, out)
    r = _run(nc, [arrays], core_ids=[0])
    return r.results[0]["out_0_dram"]
```
